# Optimizing a Trainium2 kernel written in Bass

```python
import numpy as np
import jax
import jax.numpy as jnp

def _softmax(x, axis=-1):
    return jax.nn.softmax(x, axis=axis)

def _gelu(x):
    return jax.nn.gelu(x, approximate=True)

def _silu(x):
    return jax.nn.silu(x)

def _sigmoid(x):
    return jax.nn.sigmoid(x)

def _layernorm(x, axis=-1, eps=1e-05):
    m = jnp.mean(x, axis=axis, keepdims=True)
    v = jnp.var(x, axis=axis, keepdims=True)
    return (x - m) / jnp.sqrt(v + eps)

def _scatter_add(tgt, idx, src, axis=0):
    return tgt.at[idx].add(src)

def _segment_sum(src, seg, n):
    return jax.ops.segment_sum(src, seg, n)
kernel_name = 'mk_conv_preact_d2_conv_nchw512_r2_b1e758'

def setup_inputs(seed: int=0):
    np.random.seed(seed)
    _w = jnp.asarray

    def _rec_inputs():
        import jax
        import jax.numpy as jnp
        _gk = jax.random.key(seed)
        x = -0.000125 + 0.9999 * jax.random.normal(jax.random.fold_in(_gk, 1), (16, 256, 32, 32), jnp.float32)
        return x
    x = _rec_inputs()

    def _L0_conv_setup():
        import jax, jax.numpy as jnp
        import numpy as np
        B, C, H, W, K = (16, 256, 32, 32, 7)
        LN_EPS = 1e-05
        key = jax.random.key(seed)
        ks = jax.random.split(key, 6)
        x = jax.random.normal(ks[0], (B, C, H, W), dtype=jnp.float32)
        K_w = jax.random.normal(ks[1], (K * K, C), dtype=jnp.float32) * 0.02
        K_b = jnp.zeros((K * K,), dtype=jnp.float32)
        conv0_w = jax.random.normal(ks[2], (C, C), dtype=jnp.float32) * 0.02
        conv0_b = jnp.zeros((C,), dtype=jnp.float32)
        ln_w = jnp.ones((C, K, K), dtype=jnp.float32)
        ln_b = jnp.zeros((C, K, K), dtype=jnp.float32)
        conv1_w = jax.random.normal(ks[3], (C, C), dtype=jnp.float32) * 0.02
        conv1_b = jnp.zeros((C,), dtype=jnp.float32)
        return {'x': x, 'K_w': K_w, 'K_b': K_b, 'conv0_w': conv0_w, 'conv0_b': conv0_b, 'ln_w': ln_w, 'ln_b': ln_b, 'conv1_w': conv1_w, 'conv1_b': conv1_b}
    _L0_conv_all = _L0_conv_setup()
    _L0_conv_in = {k: v for k, v in _L0_conv_all.items() if k in ('K_w', 'K_b', 'conv0_w', 'conv0_b', 'ln_w', 'ln_b', 'conv1_w', 'conv1_b')}
    del _L0_conv_all

    def _L1_conv_setup():
        import jax, jax.numpy as jnp
        from jax import lax
        import numpy as np
        D_IN = 256
        HID = 64
        D_INNER = 2 * HID
        D_PROJ = 2 * D_INNER
        N_STATE = 16
        R_DT = 8
        B, H, W = (8, 32, 32)

        def _layernorm(y, g, b):
            mu = y.mean(-1, keepdims=True)
            var = ((y - mu) ** 2).mean(-1, keepdims=True)
            return (y - mu) / jnp.sqrt(var + 1e-05) * g + b

        def _ssm(x, xw, dtw, dtb, Al, Dv, g, be):
            Bb, D, L = x.shape
            n = Al.shape[1]
            xd = jnp.einsum('bdl,kd->blk', x, xw)
            dts = xd[..., :R_DT]
            Bs = xd[..., R_DT:R_DT + n]
            Cs = xd[..., R_DT + n:]
            delta = jax.nn.softplus(jnp.einsum('blr,dr->bld', dts, dtw) + dtb)
            A = -jnp.exp(Al)
            xt = x.transpose(0, 2, 1)
            dA = jnp.exp(delta[..., None] * A)
            dBx = delta[..., None] * Bs[:, :, None, :] * xt[..., None]

            def step(h, inp):
                da, dbx, c = inp
                h = h * da + dbx
                return (h, jnp.einsum('bdn,bn->bd', h, c))
            h0 = jnp.zeros((Bb, D, n), x.dtype)
            _, ys = lax.scan(step, h0, (dA.transpose(1, 0, 2, 3), dBx.transpose(1, 0, 2, 3), Cs.transpose(1, 0, 2)))
            y = ys.transpose(1, 0, 2) + xt * Dv
            return _layernorm(y, g, be)

        def _up2(y, h, w):
            Bb, L, C = y.shape
            img = y.transpose(0, 2, 1).reshape(Bb, C, h, w)
            img = jnp.repeat(jnp.repeat(img, 2, axis=2), 2, axis=3)
            return img.reshape(Bb, C, 4 * L).transpose(0, 2, 1)

        def _conv1x1(x, w, b):
            return jnp.einsum('bchw,oc->bohw', x, w) + b[None, :, None, None]

        def _conv2s2(x, w, b):
            out = lax.conv_general_dilated(x, w, (2, 2), 'VALID', dimension_numbers=('NCHW', 'OIHW', 'NCHW'))
            return out + b[None, :, None, None]

        def _forward(input_f, in_w, in_b, c1_w, c1_b, c2_w, c2_b, c3_w, c3_b, out_w, out_b, xw1, dtw1, dtb1, Al1, Dv1, g1, be1, xw2, dtw2, dtb2, Al2, Dv2, g2, be2, xw3, dtw3, dtb3, Al3, Dv3, g3, be3):
            xz = _conv1x1(input_f, in_w, in_b)
            x, z = jnp.split(xz, 2, axis=1)
            f1 = _conv1x1(x, c1_w, c1_b)
            f2 = _conv2s2(f1, c2_w, c2_b)
            f3 = _conv2s2(f2, c3_w, c3_b)
            Bb, C, h3, w3 = f3.shape
            fx3 = f3.reshape(Bb, C, h3 * w3)
            y3 = _ssm(fx3, xw3, dtw3, dtb3, Al3, Dv3, g3, be3) + jnp.flip(_ssm(jnp.flip(fx3, -1), xw3, dtw3, dtb3, Al3, Dv3, g3, be3), 1)
            y2_ = _up2(y3, h3, w3)
            _, _, h2, w2 = f2.shape
            fx2 = f2.reshape(Bb, C, h2 * w2)
            y2 = _ssm(fx2, xw2, dtw2, dtb2, Al2, Dv2, g2, be2) + jnp.flip(_ssm(jnp.flip(fx2, -1), xw2, dtw2, dtb2, Al2, Dv2, g2, be2), 1) + y2_
            y1_ = _up2(y2, h2, w2)
            _, _, h1, w1 = f1.shape
            fx1 = f1.reshape(Bb, C, h1 * w1)
            y1 = _ssm(fx1, xw1, dtw1, dtb1, Al1, Dv1, g1, be1) + jnp.flip(_ssm(jnp.flip(fx1, -1), xw2, dtw2, dtb2, Al2, Dv2, g2, be2), 1) + y1_
            out1 = y1.transpose(0, 2, 1).reshape(Bb, C, h1, w1)
            out = out1 * jax.nn.silu(z)
            return _conv1x1(out, out_w, out_b)
        key = jax.random.key(seed)
        ks = iter(jax.random.split(key, 32))

        def nrm(shape, s=0.05):
            return jax.random.normal(next(ks), shape, dtype=jnp.float32) * s
        inp = {'input_f': jax.random.normal(next(ks), (B, D_IN, H, W), dtype=jnp.float32), 'in_w': nrm((D_PROJ, D_IN)), 'in_b': nrm((D_PROJ,)), 'c1_w': nrm((D_INNER, D_INNER)), 'c1_b': nrm((D_INNER,)), 'c2_w': nrm((D_INNER, D_INNER, 2, 2)), 'c2_b': nrm((D_INNER,)), 'c3_w': nrm((D_INNER, D_INNER, 2, 2)), 'c3_b': nrm((D_INNER,)), 'out_w': nrm((D_IN, D_INNER)), 'out_b': nrm((D_IN,))}
        Al = jnp.log(jnp.tile(jnp.arange(1, N_STATE + 1, dtype=jnp.float32), (D_INNER, 1)))
        for i in (1, 2, 3):
            inp[f'xw{i}'] = nrm((R_DT + 2 * N_STATE, D_INNER))
            inp[f'dtw{i}'] = nrm((D_INNER, R_DT), s=R_DT ** (-0.5))
            inp[f'dtb{i}'] = nrm((D_INNER,)) - 4.0
            inp[f'Al{i}'] = Al
            inp[f'Dv{i}'] = jnp.ones((D_INNER,), jnp.float32)
            inp[f'g{i}'] = jnp.ones((D_INNER,), jnp.float32)
            inp[f'be{i}'] = jnp.zeros((D_INNER,), jnp.float32)
        return inp
    _L1_conv_all = _L1_conv_setup()
    _L1_conv_in = {k: v for k, v in _L1_conv_all.items() if k in ('in_w', 'in_b', 'c1_w', 'c1_b', 'c2_w', 'c2_b', 'c3_w', 'c3_b', 'out_w', 'out_b', 'xw1', 'dtw1', 'dtb1', 'Al1', 'Dv1', 'g1', 'be1', 'xw2', 'dtw2', 'dtb2', 'Al2', 'Dv2', 'g2', 'be2', 'xw3', 'dtw3', 'dtb3', 'Al3', 'Dv3', 'g3', 'be3')}
    del _L1_conv_all
    return {'x': x, 'L0_conv_K_w': _L0_conv_in['K_w'], 'L0_conv_K_b': _L0_conv_in['K_b'], 'L0_conv_conv0_w': _L0_conv_in['conv0_w'], 'L0_conv_conv0_b': _L0_conv_in['conv0_b'], 'L0_conv_ln_w': _L0_conv_in['ln_w'], 'L0_conv_ln_b': _L0_conv_in['ln_b'], 'L0_conv_conv1_w': _L0_conv_in['conv1_w'], 'L0_conv_conv1_b': _L0_conv_in['conv1_b'], 'L1_conv_in_w': _L1_conv_in['in_w'], 'L1_conv_in_b': _L1_conv_in['in_b'], 'L1_conv_c1_w': _L1_conv_in['c1_w'], 'L1_conv_c1_b': _L1_conv_in['c1_b'], 'L1_conv_c2_w': _L1_conv_in['c2_w'], 'L1_conv_c2_b': _L1_conv_in['c2_b'], 'L1_conv_c3_w': _L1_conv_in['c3_w'], 'L1_conv_c3_b': _L1_conv_in['c3_b'], 'L1_conv_out_w': _L1_conv_in['out_w'], 'L1_conv_out_b': _L1_conv_in['out_b'], 'L1_conv_xw1': _L1_conv_in['xw1'], 'L1_conv_dtw1': _L1_conv_in['dtw1'], 'L1_conv_dtb1': _L1_conv_in['dtb1'], 'L1_conv_Al1': _L1_conv_in['Al1'], 'L1_conv_Dv1': _L1_conv_in['Dv1'], 'L1_conv_g1': _L1_conv_in['g1'], 'L1_conv_be1': _L1_conv_in['be1'], 'L1_conv_xw2': _L1_conv_in['xw2'], 'L1_conv_dtw2': _L1_conv_in['dtw2'], 'L1_conv_dtb2': _L1_conv_in['dtb2'], 'L1_conv_Al2': _L1_conv_in['Al2'], 'L1_conv_Dv2': _L1_conv_in['Dv2'], 'L1_conv_g2': _L1_conv_in['g2'], 'L1_conv_be2': _L1_conv_in['be2'], 'L1_conv_xw3': _L1_conv_in['xw3'], 'L1_conv_dtw3': _L1_conv_in['dtw3'], 'L1_conv_dtb3': _L1_conv_in['dtb3'], 'L1_conv_Al3': _L1_conv_in['Al3'], 'L1_conv_Dv3': _L1_conv_in['Dv3'], 'L1_conv_g3': _L1_conv_in['g3'], 'L1_conv_be3': _L1_conv_in['be3']}

def reference(x, L0_conv_K_w, L0_conv_K_b, L0_conv_conv0_w, L0_conv_conv0_b, L0_conv_ln_w, L0_conv_ln_b, L0_conv_conv1_w, L0_conv_conv1_b, L1_conv_in_w, L1_conv_in_b, L1_conv_c1_w, L1_conv_c1_b, L1_conv_c2_w, L1_conv_c2_b, L1_conv_c3_w, L1_conv_c3_b, L1_conv_out_w, L1_conv_out_b, L1_conv_xw1, L1_conv_dtw1, L1_conv_dtb1, L1_conv_Al1, L1_conv_Dv1, L1_conv_g1, L1_conv_be1, L1_conv_xw2, L1_conv_dtw2, L1_conv_dtb2, L1_conv_Al2, L1_conv_Dv2, L1_conv_g2, L1_conv_be2, L1_conv_xw3, L1_conv_dtw3, L1_conv_dtb3, L1_conv_Al3, L1_conv_Dv3, L1_conv_g3, L1_conv_be3):
    import jax
    import jax.numpy as jnp

    def _L0_conv_ref(x, K_w, K_b, conv0_w, conv0_b, ln_w, ln_b, conv1_w, conv1_b):
        import jax, jax.numpy as jnp
        import numpy as np
        B, C, H, W, K = (16, 256, 32, 32, 7)
        LN_EPS = 1e-05
        b, c, h, w = x.shape
        kk = K_w.shape[0]
        k = int(round(kk ** 0.5))
        hw = h * w
        query = x.reshape(b, c, hw)
        key = jnp.einsum('bchw,oc->bohw', x, K_w) + K_b[None, :, None, None]
        key = key.reshape(b, kk, hw).transpose(0, 2, 1)
        key = jax.nn.softmax(key, axis=1)
        filters = jnp.einsum('bcn,bnk->bck', query, key).reshape(b, c, k, k)
        filters = jnp.einsum('bcij,oc->boij', filters, conv0_w) + conv0_b[None, :, None, None]
        mean = jnp.mean(filters, axis=(1, 2, 3), keepdims=True)
        var = jnp.var(filters, axis=(1, 2, 3), keepdims=True)
        filters = (filters - mean) * jax.lax.rsqrt(var + LN_EPS)
        filters = filters * ln_w[None] + ln_b[None]
        filters = jax.nn.relu(filters)
        filters = jnp.einsum('bcij,oc->boij', filters, conv1_w) + conv1_b[None, :, None, None]
        wgt = filters.reshape(b * c, 1, k, k)
        x_r = x.reshape(1, b * c, h, w)
        pad = k // 2
        out = jax.lax.conv_general_dilated(x_r, wgt, window_strides=(1, 1), padding=[(pad, pad), (pad, pad)], feature_group_count=b * c, dimension_numbers=('NCHW', 'OIHW', 'NCHW'))
        return out.reshape(b, c, h, w)

    def _L1_conv_ref(input_f, in_w, in_b, c1_w, c1_b, c2_w, c2_b, c3_w, c3_b, out_w, out_b, xw1, dtw1, dtb1, Al1, Dv1, g1, be1, xw2, dtw2, dtb2, Al2, Dv2, g2, be2, xw3, dtw3, dtb3, Al3, Dv3, g3, be3):
        import jax, jax.numpy as jnp
        from jax import lax
        import numpy as np
        D_IN = 256
        HID = 64
        D_INNER = 2 * HID
        D_PROJ = 2 * D_INNER
        N_STATE = 16
        R_DT = 8
        B, H, W = (8, 32, 32)

        def _layernorm(y, g, b):
            mu = y.mean(-1, keepdims=True)
            var = ((y - mu) ** 2).mean(-1, keepdims=True)
            return (y - mu) / jnp.sqrt(var + 1e-05) * g + b

        def _ssm(x, xw, dtw, dtb, Al, Dv, g, be):
            Bb, D, L = x.shape
            n = Al.shape[1]
            xd = jnp.einsum('bdl,kd->blk', x, xw)
            dts = xd[..., :R_DT]
            Bs = xd[..., R_DT:R_DT + n]
            Cs = xd[..., R_DT + n:]
            delta = jax.nn.softplus(jnp.einsum('blr,dr->bld', dts, dtw) + dtb)
            A = -jnp.exp(Al)
            xt = x.transpose(0, 2, 1)
            dA = jnp.exp(delta[..., None] * A)
            dBx = delta[..., None] * Bs[:, :, None, :] * xt[..., None]

            def step(h, inp):
                da, dbx, c = inp
                h = h * da + dbx
                return (h, jnp.einsum('bdn,bn->bd', h, c))
            h0 = jnp.zeros((Bb, D, n), x.dtype)
            _, ys = lax.scan(step, h0, (dA.transpose(1, 0, 2, 3), dBx.transpose(1, 0, 2, 3), Cs.transpose(1, 0, 2)))
            y = ys.transpose(1, 0, 2) + xt * Dv
            return _layernorm(y, g, be)

        def _up2(y, h, w):
            Bb, L, C = y.shape
            img = y.transpose(0, 2, 1).reshape(Bb, C, h, w)
            img = jnp.repeat(jnp.repeat(img, 2, axis=2), 2, axis=3)
            return img.reshape(Bb, C, 4 * L).transpose(0, 2, 1)

        def _conv1x1(x, w, b):
            return jnp.einsum('bchw,oc->bohw', x, w) + b[None, :, None, None]

        def _conv2s2(x, w, b):
            out = lax.conv_general_dilated(x, w, (2, 2), 'VALID', dimension_numbers=('NCHW', 'OIHW', 'NCHW'))
            return out + b[None, :, None, None]

        def _forward(input_f, in_w, in_b, c1_w, c1_b, c2_w, c2_b, c3_w, c3_b, out_w, out_b, xw1, dtw1, dtb1, Al1, Dv1, g1, be1, xw2, dtw2, dtb2, Al2, Dv2, g2, be2, xw3, dtw3, dtb3, Al3, Dv3, g3, be3):
            xz = _conv1x1(input_f, in_w, in_b)
            x, z = jnp.split(xz, 2, axis=1)
            f1 = _conv1x1(x, c1_w, c1_b)
            f2 = _conv2s2(f1, c2_w, c2_b)
            f3 = _conv2s2(f2, c3_w, c3_b)
            Bb, C, h3, w3 = f3.shape
            fx3 = f3.reshape(Bb, C, h3 * w3)
            y3 = _ssm(fx3, xw3, dtw3, dtb3, Al3, Dv3, g3, be3) + jnp.flip(_ssm(jnp.flip(fx3, -1), xw3, dtw3, dtb3, Al3, Dv3, g3, be3), 1)
            y2_ = _up2(y3, h3, w3)
            _, _, h2, w2 = f2.shape
            fx2 = f2.reshape(Bb, C, h2 * w2)
            y2 = _ssm(fx2, xw2, dtw2, dtb2, Al2, Dv2, g2, be2) + jnp.flip(_ssm(jnp.flip(fx2, -1), xw2, dtw2, dtb2, Al2, Dv2, g2, be2), 1) + y2_
            y1_ = _up2(y2, h2, w2)
            _, _, h1, w1 = f1.shape
            fx1 = f1.reshape(Bb, C, h1 * w1)
            y1 = _ssm(fx1, xw1, dtw1, dtb1, Al1, Dv1, g1, be1) + jnp.flip(_ssm(jnp.flip(fx1, -1), xw2, dtw2, dtb2, Al2, Dv2, g2, be2), 1) + y1_
            out1 = y1.transpose(0, 2, 1).reshape(Bb, C, h1, w1)
            out = out1 * jax.nn.silu(z)
            return _conv1x1(out, out_w, out_b)
        return _forward(input_f, in_w, in_b, c1_w, c1_b, c2_w, c2_b, c3_w, c3_b, out_w, out_b, xw1, dtw1, dtb1, Al1, Dv1, g1, be1, xw2, dtw2, dtb2, Al2, Dv2, g2, be2, xw3, dtw3, dtb3, Al3, Dv3, g3, be3)

    def _gn(v, G=32, eps=1e-05):
        B_, C_, H_, W_ = v.shape
        g = v.reshape(B_, G, C_ // G, H_, W_)
        m = jnp.mean(g, axis=(2, 3, 4), keepdims=True)
        s = jnp.var(g, axis=(2, 3, 4), keepdims=True)
        return ((g - m) / jnp.sqrt(s + eps)).reshape(v.shape)

    def _ln_c(v, eps=1e-06):
        m = jnp.mean(v, axis=1, keepdims=True)
        s = jnp.var(v, axis=1, keepdims=True)
        return (v - m) / jnp.sqrt(s + eps)

    def _ln_t(v, eps=1e-05):
        m = jnp.mean(v, axis=-1, keepdims=True)
        s = jnp.var(v, axis=-1, keepdims=True)
        return (v - m) / jnp.sqrt(s + eps)

    def _to_tokens(v):
        B_, C_, H_, W_ = v.shape
        return v.reshape(B_, C_, H_ * W_).transpose(0, 2, 1)

    def _from_tokens(t, like):
        B_, C_, H_, W_ = like.shape
        return t.transpose(0, 2, 1).reshape(B_, C_, H_, W_)
    x = x + _L0_conv_ref(_gn(x), L0_conv_K_w, L0_conv_K_b, L0_conv_conv0_w, L0_conv_conv0_b, L0_conv_ln_w, L0_conv_ln_b, L0_conv_conv1_w, L0_conv_conv1_b)
    x = x + _L1_conv_ref(_gn(x), L1_conv_in_w, L1_conv_in_b, L1_conv_c1_w, L1_conv_c1_b, L1_conv_c2_w, L1_conv_c2_b, L1_conv_c3_w, L1_conv_c3_b, L1_conv_out_w, L1_conv_out_b, L1_conv_xw1, L1_conv_dtw1, L1_conv_dtb1, L1_conv_Al1, L1_conv_Dv1, L1_conv_g1, L1_conv_be1, L1_conv_xw2, L1_conv_dtw2, L1_conv_dtb2, L1_conv_Al2, L1_conv_Dv2, L1_conv_g2, L1_conv_be2, L1_conv_xw3, L1_conv_dtw3, L1_conv_dtb3, L1_conv_Al3, L1_conv_Dv3, L1_conv_g3, L1_conv_be3)
    return x

_drawn_inputs = setup_inputs


def setup_inputs(seed=0):
    import zlib

    import numpy as np

    out = dict(_drawn_inputs(seed))
    spreads = {'L0_conv_K_b': (0.0, 2.0),
     'L0_conv_conv0_b': (0.0, 0.1),
     'L0_conv_ln_w': (1.0, 0.2),
     'L0_conv_ln_b': (0.0, 0.1),
     'L0_conv_conv1_b': (0.0, 0.1),
     'L1_conv_Dv1': (1.0, 0.6),
     'L1_conv_g1': (1.0, 0.6),
     'L1_conv_be1': (0.0, 0.671),
     'L1_conv_Dv2': (1.0, 0.6),
     'L1_conv_g2': (1.0, 0.2),
     'L1_conv_be2': (0.0, 0.1),
     'L1_conv_Dv3': (1.0, 0.6),
     'L1_conv_g3': (1.0, 0.2),
     'L1_conv_be3': (0.0, 0.356)}
    factors = {'L1_conv_c3_b': 2.732,
     'L1_conv_xw1': 8.0,
     'L1_conv_dtw1': 8.0,
     'L1_conv_dtb1': 73.881,
     'L1_conv_Al1': 8.0,
     'L1_conv_xw2': 8.0,
     'L1_conv_dtw2': 8.0,
     'L1_conv_dtb2': 111.344,
     'L1_conv_Al2': 8.0,
     'L1_conv_xw3': 8.0,
     'L1_conv_dtw3': 8.0,
     'L1_conv_dtb3': 38.098,
     'L1_conv_Al3': 8.0}
    for name, (base, spread) in spreads.items():
        noise = np.random.default_rng([zlib.crc32(name.encode()), seed]).standard_normal(out[name].shape)
        drawn = base * np.exp(spread * noise) if base else spread * noise
        out[name] = jnp.asarray(drawn.astype(out[name].dtype))
    for name, factor in factors.items():
        out[name] = (out[name] * factor).astype(out[name].dtype)
    return out
```

```python
from contextlib import ExitStack

import concourse.bass as bass
from concourse import mybir

ALU = mybir.AluOpType
ACT = mybir.ActivationFunctionType
AX = mybir.AxisListType
F32 = mybir.dt.float32
F16 = mybir.dt.float16
BF16 = mybir.dt.bfloat16

P = 128
B, C, H, W = 16, 256, 32, 32
HW = H * W
CT = C // P
KK = 7
K2 = KK * KK
PADW = W + KK - 1
D = 128
NS = 16
R_DT = 8
L1, L2, L3 = HW, HW // 4, HW // 16
LF = L1 + L2 + L3
HALF = 512
GROUP = C // 32
SA, SB, SC, SD = 0, L1, 2 * L1, 2 * L1 + L2
LS = 2 * L1 + L2 + L3
CHUNKS = [(SD, L3, L1 + L2, 2), (SC, L2, L1, 1),
          (SA, HALF, 0, 0), (SA + HALF, HALF, HALF, 0), (SB, HALF, 0, 1), (SB + HALF, HALF, HALF, 1)]
NCH = len(CHUNKS)
UNITS = [(3, 2, 2, 0, NS)] + [(2, 1, 2, n, 4) for n in range(0, NS, 4)] + \
        [(1, 0, 0, n, 1) for n in range(NS)] + [(1, 1, 1, n, 1) for n in range(NS)]
NU = len(UNITS)
PRODUCTS = [(u, d) for u, (_, _, dd, _, _) in enumerate(UNITS) for d in ((0, 1) if dd == 2 else (dd,))]
NP = len(PRODUCTS)
LEVEL = {1: (L1, 0, SA, 1), 2: (L2, L1, SC, 4), 3: (L3, L1 + L2, SD, NS)}
BUF = NS * (L3 + 1)
ROWS = [(t, r) for t in range(CT) for r in range(KK)]
NR = len(ROWS)
RING = 4
EPS = 1e-5
NORMS = [(2, L1 + L2, L3), (2, L1, L2), (0, 0, HALF), (0, HALF, HALF), (1, 0, HALF), (1, HALF, HALF)]
NN = len(NORMS)

CONSTS = ["ident", "cen", "ones", "grp"]


def products_of(u):
    return [q for q, (v, _) in enumerate(PRODUCTS) if v == u]


def build(nc, a, out):
    with ExitStack() as ctx:
        def sb(name, shape, dt=F32):
            return ctx.enter_context(nc.sbuf_tensor(name, shape, dt))

        def ps(name, shape, dt=F32):
            return ctx.enter_context(nc.psum_tensor(name, shape, dt))

        def sem(name):
            return ctx.enter_context(nc.semaphore(name))

        class Count:

            def __init__(self, name, per):
                self.sem, self.per = sem(name), per

            def at(self, b, c):
                return b * self.per + c

        class Chain:

            def __init__(self, name, per):
                self.count, self.per = Count(name, per), per

            def start(self, eng, b):
                self.eng, self.b, self.n = eng, b, 0

            def __call__(self, ins):
                self.n += 1
                ins.then_inc(self.count.sem, 1)
                self.eng.wait_ge(self.count.sem, self.count.at(self.b, self.n))

            def end(self):
                assert self.n == self.per, (self.n, self.per)

        mats = {n: sb(n, [P, P]) for n in CONSTS}
        ident, cen, ones, grp = (mats[n] for n in CONSTS)
        id16 = sb("id16", [P, P], F16)
        sel = sb("sel", [96, 32], BF16)
        sel32 = sb("sel32", [96, 32])
        wk = sb("wk", [P, CT, K2])
        w0 = sb("w0", [P, CT, C])
        w1 = sb("w1", [P, CT, C])
        win = sb("win", [P, C])
        wz = sb("wz", [P, CT, P])
        wc1 = sb("wc1", [P, P])
        wf = sb("wf", [P, CT, P])
        wc2 = sb("wc2", [P, 4, P])
        wc3 = sb("wc3", [P, 4, P])
        wo = sb("wo", [P, C])
        wx8 = sb("wx8", [R_DT, 3, P])
        wdt = sb("wdt", [R_DT, 3, P])
        wdelta = sb("wdelta", [P, 3, P])
        wbc = sb("wbc", [P, 3, 96])
        vec = sb("vec", [P, 32])
        kb = sb("kb", [K2, 1])
        lnw = sb("lnw", [P, CT, K2])
        lnb = sb("lnb", [P, CT, K2])
        al = sb("al", [P, 3, NS])
        nega = sb("nega", [P, 3, NS])
        bf1 = sb("bf1", [P, 1])
        eps = sb("eps", [P, 1])
        bes = sb("bes", [P, 3])
        v_inx, v_inz, v_c1, v_c2, v_c3 = (vec[:, i:i + 1] for i in range(5))
        v_out, v_b0, v_b1 = (vec[:, i:i + 2] for i in (5, 7, 9))
        v_dtb, v_dv, v_g, v_be = (vec[:, i:i + 3] for i in (11, 14, 17, 20))

        xr = sb("xr", [P, CT, HW])
        xh = sb("xh", [P, CT, HW])
        pad = sb("pad", [P, CT, 2, PADW, PADW], F16)
        ex = sb("ex", [K2, HW])
        kt = sb("kt", [P, HW // P, K2])
        dg49 = sb("dg49", [K2, K2])
        fi = sb("fi", [P, CT, K2])
        f2 = sb("f2", [P, CT, K2])
        wg = sb("wg", [P, CT, K2])
        whi = sb("whi", [P, CT, K2], F16)
        wlo = sb("wlo", [P, CT, K2], F16)
        wsc = sb("wsc", [P, CT])
        diag = sb("diag", [P, RING, 2, KK, P], F16)
        sa = sb("sa", [P, 128])
        sk = sb("sk", [K2, 4])

        xn = sb("xn", [P, CT, HW])
        xc = sb("xc", [P, CT, HW])
        xg = sb("xg", [P, CT, HW])
        xt = xg[:, :, :].rearrange("p t (n c) -> p (t n) c", c=C)
        f = sb("f", [P, LF])
        sz = sb("sz", [P, HW])
        bcs = sb("bcs", [96, LS], BF16)
        rest = sb("rest", [64, 2, HALF])
        delta = sb("delta", [P, LS])
        u = sb("u", [P, LS])
        y = sb("y", [P, 2, LF])
        work = sb("work", [P, 6, BUF])
        ea, bx, h = work[:, 0:2, :], work[:, 2:4, :], work[:, 4:6, :]
        flat = work[:, :, :].rearrange("p a n -> p (a n)")
        es, qs = flat[:, 0:LS], flat[:, LS:2 * LS]
        pr = sb("pr", [P, 2, HW])
        a3, b3 = sb("a3", [P, NS, L3 + 1]), sb("b3", [P, NS, L3 + 1])
        a2, b2 = (v[:, :, 0:4 * (L2 + 1)].rearrange("p a (m l) -> p a m l", m=4) for v in (ea, bx))
        sq = sb("sq", [P, 1, HALF])
        rs = sb("rs", [P, 2, HALF])
        o3 = sb("o3", [P, L3])
        o2 = sb("o2", [P, L2])
        o1 = sb("o1", [P, HW])
        ob = sb("ob", [P, CT, HW])
        token = sb("token", [P, 1])
        sg = sb("sg", [P, 128])
        slot_b = ps("slot_b", [P, HW])
        slot_c = ps("slot_c", [P, HW])
        pconv = ps("pconv", [P, HW])
        pm = ps("pm", [P, HW])

        consts_in = sem("consts_in")
        setup_pe = sem("setup_pe")
        setup = sem("setup")
        x_in = Count("x_in", 16)
        xr_free = Count("xr_free", 1)
        ob_free = Count("ob_free", 16)
        ob_ready = Count("ob_ready", 1)
        ea_a, ea_b = Chain("dve_a", 18), Chain("dve_b", 5)
        act_a, act_b = Chain("act_a", 2), Chain("act_b", 1)
        a_stats = Count("a_stats", 1)
        a_sums = Count("a_sums", 4)
        a_spread = Count("a_spread", 2)
        a_var = Count("a_var", 2)
        a_rstd = Count("a_rstd", 2)
        a_shift = Count("a_shift", 1)
        a_xh = Count("a_xh", CT)
        a_hi = Count("a_hi", CT)
        a_pad = Count("a_pad", CT)
        a_key = Count("a_key", 1)
        a_keyb = Count("a_keyb", 1)
        a_max = Count("a_max", 1)
        a_exp = Count("a_exp", 1)
        a_dg = Count("a_dg", 1)
        a_xt = Count("a_xt", 4)
        a_xtc = Count("a_xtc", 4)
        a_kt = Count("a_kt", 1)
        a_ktc = Count("a_ktc", 1)
        a_fi = Count("a_fi", 1)
        a_fic = Count("a_fic", 1)
        a_f2 = Count("a_f2", 1)
        a_f2c = Count("a_f2c", 1)
        a_f3 = Count("a_f3", 1)
        a_wg = Count("a_wg", 1)
        a_wgc = Count("a_wgc", 1)
        a_w16 = Count("a_w16", 1)
        a_copy = Count("a_copy", 1)
        diag_made = Count("diag_made", NR)
        row_done = Count("row_done", NR)
        conv_out = Count("conv_out", CT)
        b_stats = Count("b_stats", 1)
        b_sums = Count("b_sums", 2)
        b_spread = Count("b_spread", 1)
        b_var = Count("b_var", 1)
        b_rstd = Count("b_rstd", 1)
        b_shift = Count("b_shift", 1)
        b_xg = Count("b_xg", CT)
        b_xc = Count("b_xc", 1)
        b_proj = Count("b_proj", 4)
        b_f = Count("b_f", 3)
        b_z = Count("b_z", 2)
        b_sz = Count("b_sz", 1)
        ch_bc = Count("ch_bc", NCH)
        ch_dt = Count("ch_dt", NCH)
        ch_hi = Count("ch_hi", NCH)
        ch_abs = Count("ch_abs", NCH)
        ch_exp = Count("ch_exp", NCH)
        ch_q = Count("ch_q", NCH)
        ch_rest = Count("ch_rest", NCH)
        ch_pos = Count("ch_pos", NCH)
        ch_err = Count("ch_err", NCH)
        ch_m2 = Count("ch_m2", NCH)
        ch_ln = Count("ch_ln", NCH)
        ch_mid = Count("ch_mid", NCH)
        ch_lo = Count("ch_lo", NCH)
        ch_delta = Count("ch_delta", NCH)
        ch_u = Count("ch_u", NCH)
        y_init = Count("y_init", 5)
        u_b = Count("u_b", NU)
        u_c = Count("u_c", NU)
        u_ea = Count("u_ea", NU)
        u_bx = Count("u_bx", NU)
        u_zero = Count("u_zero", 2)
        q_h = Count("q_h", NP)
        q_pr = Count("q_pr", NP)
        q_y = Count("q_y", NP)
        n_y = Count("n_y", 24)
        n_yc = Count("n_yc", NN)
        n_sq = Count("n_sq", NN)
        n_var = Count("n_var", NN)
        n_ln = Count("n_ln", NN)
        n_rs = Count("n_rs", NN)
        n_t = Count("n_t", NN)
        n_o = Count("n_o", STEPS[-1])
        b_g = Count("b_g", 2)
        b_out = Count("b_out", 4)

        xv = a["x"].rearrange("b (t p) h w -> b p t (h w)", p=P)
        ov = out.rearrange("b (t p) h w -> b p t (h w)", p=P)
        block = ctx.enter_context(nc.Block())

        loads = [(mats[n][:, :], a["c_" + n]) for n in CONSTS] + [
            (sel32[:, :], a["c_sel"]),
            (wk[:, :, :], a["wk"]), (w0[:, :, :], a["w0"]), (w1[:, :, :], a["w1"]), (win[:, :], a["win"]),
            (wz[:, :, :], a["wz"]), (wc1[:, :], a["wc1"]), (wc2[:, :, :], a["wc2"]), (wc3[:, :, :], a["wc3"]),
            (wo[:, :], a["wo"]), (wx8[:, :, :], a["wx8"]), (wdt[:, :, :], a["wdt"]), (wbc[:, :, :], a["wbc"]),
            (vec[:, 0:23], a["vec"]), (kb[:, :], a["kb"]), (lnw[:, :, :], a["lnw"]), (lnb[:, :, :], a["lnb"]),
            (al[:, :, :], a["al"])]
        LOADED = 16 * len(loads)
        DVE_SET, ACT_SET = 7, 5

        def bank(t, k):
            return t[:, k * HALF:(k + 1) * HALF]

        def img(ap, side):
            return ap.rearrange("p (r c) -> p r c", c=side)

        @block.sync
        def _(sp):
            for dst, src in loads:
                sp.dma_start(dst, src).then_inc(consts_in, 16)
            sp.dma_start(token[0:K2, :], a["kb"]).then_inc(ob_free.sem, 16)
            sp.dma_start(xr[:, :, :], xv[0]).then_inc(x_in.sem, 16)
            sp.wait_ge(xr_free.sem, xr_free.at(1, 0))
            sp.dma_start(xr[:, :, :], xv[1]).then_inc(x_in.sem, 16)
            with sp.Fori(0, B - 2) as i:
                sp.wait_ge(xr_free.sem, xr_free.at(i + 2, 0))
                sp.dma_start(xr[:, :, :], xv[i + 2]).then_inc(x_in.sem, 16)
                sp.wait_ge(ob_ready.sem, ob_ready.at(i + 1, 0))
                sp.dma_start(ov[i], ob[:, :, :]).then_inc(ob_free.sem, 16)
            for i in range(B - 2, B):
                sp.wait_ge(ob_ready.sem, ob_ready.at(i + 1, 0))
                sp.dma_start(ov[i], ob[:, :, :]).then_inc(ob_free.sem, 16)
            sp.wait_ge(ob_free.sem, ob_free.at(B + 1, 0))

        @block.vector
        def _(dve):
            for ins in (nc.vector.memset(eps[:, :], EPS), nc.vector.memset(pad[:, :, :, :, :], 0.0),
                        nc.vector.memset(a3[:, :, :], 0.0), nc.vector.memset(b3[:, :, :], 0.0)):
                ins.then_inc(setup, 1)
            dve.wait_ge(consts_in, LOADED)
            nc.vector.tensor_copy(id16[:, :], ident[:, :]).then_inc(setup, 1)
            nc.vector.tensor_copy(sel[:, :], sel32[:, :]).then_inc(setup, 1)
            nc.vector.scalar_tensor_tensor(bes[:, 0:1], v_be[:, 0:1], 0.0, v_be[:, 1:2], ALU.add, ALU.add)
            nc.vector.tensor_scalar(bes[:, 1:3], v_be[:, 1:3], 2.0, None, ALU.mult).then_inc(setup, 1)
            dve.wait_ge(setup, DVE_SET + ACT_SET)

            def a1(j):
                ch = ea_a
                ch.start(dve, j)
                dve.wait_ge(x_in.sem, x_in.at(j + 1, 0))
                for t in range(CT):
                    for k in range(2):
                        ins = nc.vector.bn_stats(sa[:, 12 * t + 6 * k:12 * t + 6 * k + 6], bank(xr[:, t, :], k))
                ins.then_inc(a_stats.sem, 1)
                gn(ch, j, sa, pconv, a_sums, a_stats, a_spread, a_var, a_rstd, a_shift)
                for t in range(CT):
                    dve.wait_ge(a_hi.sem, a_hi.at(j, t + 1))
                    dve.wait_ge(a_xh.sem, a_xh.at(j, t + 1))
                    inner = pad[:, t, :, 3:3 + H, 3:3 + W]
                    nc.vector.tensor_tensor(inner[:, 1], img(xh[:, t, :], W), inner[:, 0], ALU.subtract).then_inc(a_pad.sem, 1)

            def gn(ch, b, s, pp, sums, stats, spread, var, rstd, shift):
                st = s[:, 0:24].rearrange("p (t k c) -> p t k c", t=CT, c=3)
                gm = pp[:, 0:24].rearrange("p (t k c) -> p t k c", t=CT, c=3)
                d = s[:, 32:40].rearrange("p (t k) -> p t k", t=CT)
                w = s[:, 40:48].rearrange("p (t k) -> p t k", t=CT)
                dve.wait_ge(sums.sem, sums.at(b, 1))
                ch(nc.vector.tensor_reduce(s[:, 24:26], gm[:, :, :, 1], AX.X, ALU.add))
                ch(nc.vector.tensor_tensor(d, st[:, :, :, 1], s[:, 24:26, None].to_broadcast([P, CT, 4]), ALU.subtract))
                ch(nc.vector.tensor_tensor(w, d, d, ALU.mult))
                nc.vector.scalar_tensor_tensor(w, st[:, :, :, 2], 1.0 / 256, w, ALU.mult, ALU.add).then_inc(spread.sem, 1)
                dve.wait_ge(sums.sem, sums.at(b, 2))
                nc.vector.tensor_reduce(s[:, 50:52], pp[:, 32:40].rearrange("p (t k) -> p t k", t=CT), AX.X,
                                        ALU.add).then_inc(var.sem, 1)
                dve.wait_ge(rstd.sem, rstd.at(b, 1))
                nc.vector.scalar_tensor_tensor(s[:, 56:58], s[:, 24:26], -1.0, s[:, 54:56], ALU.mult, ALU.mult).then_inc(shift.sem, 1)

            def a3_(j):
                ch = ea_a
                dve.wait_ge(a_keyb.sem, a_keyb.at(j, 1))
                nc.vector.tensor_reduce(sk[:, 0:1], ex[:, :], AX.X, ALU.max, negate=True).then_inc(a_max.sem, 1)
                dve.wait_ge(a_exp.sem, a_exp.at(j, 1))
                ch(nc.vector.reciprocal(sk[:, 2:3], sk[:, 1:2]))
                nc.vector.tensor_scalar(dg49[:, :], ident[0:K2, 0:K2], sk[:, 2:3], None, ALU.mult).then_inc(a_dg.sem, 1)

            def a4(j):
                dve.wait_ge(a_kt.sem, a_kt.at(j, 1))
                nc.vector.tensor_copy(kt[:, :, :], pm[:, 0:8 * K2].rearrange("p (n k) -> p n k", n=8)).then_inc(a_ktc.sem, 1)
                dve.wait_ge(a_fi.sem, a_fi.at(j, 1))
                nc.vector.tensor_copy(fi[:, :, :], pm[:, HALF:HALF + 2 * K2].rearrange("p (t k) -> p t k", t=CT)).then_inc(a_fic.sem, 1)

            def a5(j):
                ch = ea_a
                dve.wait_ge(a_f2.sem, a_f2.at(j, 1))
                for t in range(CT):
                    ins = nc.vector.tensor_scalar(f2[:, t, :], pm[:, t * 64:t * 64 + K2], v_b0[:, t:t + 1], None, ALU.add)
                ch(ins)
                s = sa
                nc.vector.bn_stats(s[:, 60:66], f2[:, :, :].rearrange("p t k -> p (t k)")).then_inc(a_f2c.sem, 1)
                st = s[:, 60:66].rearrange("p (k c) -> p k c", c=3)
                dve.wait_ge(a_sums.sem, a_sums.at(j, 3))
                ch(nc.vector.tensor_reduce(s[:, 66:67], pm[:, 128:134].rearrange("p (k c) -> p k c", c=3)[:, :, 1], AX.X, ALU.add))
                ch(nc.vector.tensor_scalar(s[:, 67:68], s[:, 66:67], 0.5, None, ALU.mult))
                ch(nc.vector.tensor_tensor(s[:, 68:70], st[:, :, 1], s[:, 67:68].to_broadcast([P, 2]), ALU.subtract))
                ch(nc.vector.scalar_tensor_tensor(s[:, 70:72], s[:, 68:70], 0.5, s[:, 68:70], ALU.mult, ALU.mult))
                nc.vector.scalar_tensor_tensor(s[:, 72:74], st[:, :, 2], 0.5 / K2, s[:, 70:72], ALU.mult, ALU.add).then_inc(a_spread.sem, 1)
                dve.wait_ge(a_sums.sem, a_sums.at(j, 4))
                nc.vector.tensor_reduce(s[:, 74:75], pm[:, 136:138], AX.X, ALU.add).then_inc(a_var.sem, 1)
                dve.wait_ge(a_rstd.sem, a_rstd.at(j, 2))
                ch(nc.vector.tensor_scalar(f2[:, :, :], f2[:, :, :], s[:, 67:68], s[:, 76:77], ALU.subtract, ALU.mult))
                ch(nc.vector.tensor_tensor(f2[:, :, :], f2[:, :, :], lnw[:, :, :], ALU.mult))
                ch(nc.vector.tensor_tensor(f2[:, :, :], f2[:, :, :], lnb[:, :, :], ALU.add))
                nc.vector.tensor_scalar(f2[:, :, :], f2[:, :, :], 0.0, None, ALU.max).then_inc(a_f3.sem, 1)
                dve.wait_ge(a_wg.sem, a_wg.at(j, 1))
                for t in range(CT):
                    ins = nc.vector.tensor_scalar(wg[:, t, :], pm[:, 256 + t * 64:256 + t * 64 + K2], v_b1[:, t:t + 1], None, ALU.add)
                ch(ins)
                ch(nc.vector.tensor_reduce(s[:, 80:82], wg[:, :, :], AX.X, ALU.max, apply_absolute_value=True))
                ch(nc.vector.tensor_scalar(wsc[:, :], s[:, 80:82], 1e-30, None, ALU.max))
                ch(nc.vector.reciprocal(s[:, 82:84], wsc[:, :]))
                ch(nc.vector.tensor_tensor(wg[:, :, :], wg[:, :, :], s[:, 82:84, None].to_broadcast([P, CT, K2]), ALU.mult))
                ch(nc.vector.tensor_copy(whi[:, :, :], wg[:, :, :]))
                nc.vector.tensor_tensor(wlo[:, :, :], wg[:, :, :], whi[:, :, :], ALU.subtract).then_inc(a_w16.sem, 1)
                ch.end()

            def conv_add(j, t):
                dve.wait_ge(row_done.sem, row_done.at(j, KK * (t + 1)))
                if t == 0:
                    dve.wait_ge(a_copy.sem, a_copy.at(j, 1))
                nc.vector.scalar_tensor_tensor(xn[:, t, :], pconv[:, :], wsc[:, t:t + 1], xn[:, t, :],
                                               ALU.mult, ALU.add).then_inc(conv_out.sem, 1)

            def b1(i):
                ch = ea_b
                ch.start(dve, i)
                dve.wait_ge(conv_out.sem, conv_out.at(i, CT))
                for t in range(CT):
                    for k in range(2):
                        ins = nc.vector.bn_stats(sg[:, 12 * t + 6 * k:12 * t + 6 * k + 6], bank(xn[:, t, :], k))
                ins.then_inc(b_stats.sem, 1)
                gn(ch, i, sg, slot_b, b_sums, b_stats, b_spread, b_var, b_rstd, b_shift)
                nc.vector.tensor_copy(xc[:, :, :], xn[:, :, :]).then_inc(b_xc.sem, 1)

            def b3_(i):
                for c, (s, n, fc, _) in enumerate(CHUNKS):
                    k = c % 2
                    pb, pd = bank(slot_b, k)[:, 0:n], bank(slot_c, k)[:, 0:n]
                    setn = CHUNKS[c][3]
                    dve.wait_ge(ch_abs.sem, ch_abs.at(i, c + 1))
                    nc.vector.tensor_scalar(delta[:, s:s + n], pd, v_dtb[:, setn:setn + 1], 0.0, ALU.add,
                                            ALU.max).then_inc(ch_pos.sem, 1)
                    dve.wait_ge(ch_hi.sem, ch_hi.at(i, c + 1))
                    if c >= 2:
                        dve.wait_ge(ch_lo.sem, ch_lo.at(i, c - 1))
                    nc.vector.tensor_tensor(rest[:, k, 0:n], pb[0:64], bcs[0:64, s:s + n], ALU.subtract).then_inc(ch_rest.sem, 1)
                    dve.wait_ge(ch_q.sem, ch_q.at(i, c + 1))
                    nc.vector.scalar_tensor_tensor(es[:, s:s + n], qs[:, s:s + n], 1.0, es[:, s:s + n], ALU.subtract,
                                                   ALU.subtract).then_inc(ch_err.sem, 1)
                    dve.wait_ge(ch_err.sem, ch_err.at(i, c + 1))
                    nc.vector.tensor_tensor(delta[:, s:s + n], delta[:, s:s + n], es[:, s:s + n], ALU.subtract).then_inc(ch_m2.sem, 1)

            def b4_(i):
                ch = ea_b
                dve.wait_ge(b_z.sem, b_z.at(i, 2))
                ch(nc.vector.tensor_scalar(o1[:, :], o1[:, :], 1.0, None, ALU.add))
                ch(nc.vector.reciprocal(o1[:, :], o1[:, :]))
                nc.vector.tensor_tensor(sz[:, :], sz[:, :], o1[:, :], ALU.mult).then_inc(b_sz.sem, 1)
                ch.end()

            def inputs(i, k):
                lv, st, dd, n0, m = UNITS[k]
                ln, fc, sc, _ = LEVEL[lv]
                so = SB if dd == 1 else sc
                dve.wait_ge(u_b.sem, u_b.at(i, k + 1))
                if k == 0:
                    dve.wait_ge(ch_u.sem, ch_u.at(i, NCH))
                us = u[:, so:so + ln]
                if lv == 1:
                    o, i0, i1 = bx[:, k % 2, 0:ln], slot_b[:, :], us
                else:
                    o = b3[:, :, 0:ln] if lv == 3 else b2[:, k % 2, :, 0:ln]
                    i0 = slot_b[:, :].rearrange("p (m l) -> p m l", m=m)
                    i1 = us[:, None, :].to_broadcast([P, m, ln])
                nc.vector.tensor_tensor(o, i0, i1, ALU.mult).then_inc(u_bx.sem, 1)

            def scan(i, q):
                k, d = PRODUCTS[q]
                lv, m = UNITS[k][0], UNITS[k][4]
                ln = LEVEL[lv][0]
                n = ln if lv == 1 else m * (ln + 1)
                if lv == 1:
                    av, bv = ea[:, k % 2, 0:n], bx[:, k % 2, 0:n]
                elif lv == 2:
                    av, bv = (v[:, k % 2].rearrange("p m l -> p (m l)") for v in (a2, b2))
                else:
                    av, bv = (v[:, :, :].rearrange("p m l -> p (m l)") for v in (a3, b3))
                hv = h[:, q % 2, 0:n]
                if d:
                    av, bv, hv = av[:, ::-1], bv[:, ::-1], hv[:, ::-1]
                dve.wait_ge(u_ea.sem, u_ea.at(i, k + 1))
                dve.wait_ge(u_bx.sem, u_bx.at(i, k + 1))
                if k == 1:
                    dve.wait_ge(u_zero.sem, u_zero.at(i, 2))
                nc.vector.tensor_tensor_scan(hv, av, bv, 0.0, ALU.mult, ALU.add).then_inc(q_h.sem, 1)

            def weigh(i, q):
                k, d = PRODUCTS[q]
                lv, m = UNITS[k][0], UNITS[k][4]
                ln = LEVEL[lv][0]
                dve.wait_ge(u_c.sem, u_c.at(i, k + 1))
                dve.wait_ge(q_h.sem, q_h.at(i, q + 1))
                if q >= 2:
                    dve.wait_ge(q_y.sem, q_y.at(i, q - 1))
                if lv == 1:
                    nc.vector.tensor_tensor(pr[:, q % 2, :], slot_c[:, :], h[:, q % 2, 0:ln], ALU.mult).then_inc(q_pr.sem, 1)
                    return
                hv = h[:, q % 2, 0:m * (ln + 1)].rearrange("p (m l) -> p m l", m=m)[:, :, 0:ln]
                pv = pr[:, q % 2, :].rearrange("p (m l) -> p m l", m=m)
                nc.vector.tensor_tensor(pv, slot_c[:, :].rearrange("p (m l) -> p m l", m=m), hv, ALU.mult).then_inc(q_pr.sem, 1)

            def up_add(dst, src, side):
                dv = dst.rearrange("p (r s c) -> p r s c", s=2, c=2 * side)
                sv = src.rearrange("p (r c) -> p r c", c=side)
                rows = dv.shape[1]
                for s in range(2):
                    d = dv[:, :, s, :].rearrange("p r (c e) -> p r c e", e=2)
                    ins = nc.vector.tensor_tensor(d, d, sv[:, :, :, None].to_broadcast([P, rows, side, 2]), ALU.add)
                return ins

            def norm(i, k):
                d, c0, n = NORMS[k]
                cols = 2 * n if d == 2 else n
                seq = n_o

                def step(ins):
                    step.n += 1
                    ins.then_inc(seq.sem, 1)
                    dve.wait_ge(seq.sem, seq.at(i, step.n))
                step.n = STEPS[k]
                t_ = rs[:, 0, 0:cols]
                dve.wait_ge(n_rs.sem, n_rs.at(i, k + 1))
                ins = nc.vector.tensor_tensor(t_, pm[:, 0:cols], rs[:, 1, 0:cols], ALU.mult)
                ins.then_inc(n_t.sem, 1)
                dve.wait_ge(n_t.sem, n_t.at(i, k + 1))
                if k < 2:
                    o = (o3, o2)[k]
                    step(nc.vector.tensor_tensor(o[:, :], t_[:, 0:n], t_[:, n:2 * n], ALU.add))
                    p = 2 - k
                    step(nc.vector.tensor_scalar(o[:, :], o[:, :], v_g[:, p:p + 1], bes[:, p:p + 1], ALU.mult, ALU.add))
                    if k == 1:
                        step(up_add(o2[:, :], o3[:, :], 8))
                elif d == 0:
                    o = o1[:, c0:c0 + n]
                    step(nc.vector.tensor_scalar(o, t_, v_g[:, 0:1], bes[:, 0:1], ALU.mult, ALU.add))
                    hh = c0 // HALF
                    step(up_add(o, o2[:, hh * 128:hh * 128 + 128], 16))
                else:
                    o = o1[:, c0:c0 + n]
                    step(nc.vector.scalar_tensor_tensor(o, t_, v_g[:, 1:2], o, ALU.mult, ALU.add))
                    nc.vector.tensor_tensor(o, o, sz[:, c0:c0 + n], ALU.mult).then_inc(b_g.sem, 1)
                assert step.n == STEPS[k + 1]

            def b_end(i):
                norm(i, 4)
                norm(i, 5)
                dve.wait_ge(ob_free.sem, ob_free.at(i + 1, 0))
                for hh in range(2):
                    for t in range(CT):
                        k = 2 * hh + t
                        dve.wait_ge(b_out.sem, b_out.at(i, k + 1))
                        src = bank((slot_b, slot_c)[hh], t)
                        ins = nc.vector.scalar_tensor_tensor(ob[:, t, hh * HALF:(hh + 1) * HALF], src, v_out[:, t:t + 1],
                                                             xc[:, t, hh * HALF:(hh + 1) * HALF], ALU.add, ALU.add)
                ins.then_inc(ob_ready.sem, 1)

            def units(i, j):
                if i is None:
                    conv_add(j, 0)
                    conv_add(j, 1)
                    return
                inputs(i, 0)
                for v in (a2, b2):
                    nc.vector.memset(v[:, :, :, L2], 0.0).then_inc(u_zero.sem, 1)
                for k in range(NU):
                    for n, q in enumerate(products_of(k)):
                        scan(i, q)
                        if n == 0 and k + 1 < NU:
                            inputs(i, k + 1)
                        weigh(i, q)
                    for nn, at in NORM_AT.items():
                        if at == k:
                            norm(i, nn)
                    if j is not None and k == NU // 2:
                        conv_add(j, 0)
                if j is not None:
                    conv_add(j, 1)

            stages(a1, None, a3_, a4, a5, b1, None, b3_, b4_, units, b_end, dve)

        @block.tensor
        def _(pe):
            pe.wait_ge(consts_in, LOADED)
            for t in range(CT):
                nc.tensor.matmul(pm[:, t * P:(t + 1) * P], win[:, t * P:(t + 1) * P], wc1[:, :], start=True, stop=True)
            nc.tensor.matmul(pm[:, HALF:HALF + 1], wc1[:, :], v_inx, start=True, stop=True).then_inc(setup_pe, 1)
            for p in range(3):
                ins = nc.tensor.matmul(pconv[:, p * P:(p + 1) * P], wx8[:, p, :], wdt[:, p, :], start=True, stop=True)
            ins.then_inc(setup_pe, 1)
            pe.wait_ge(setup, DVE_SET + ACT_SET)

            def gn(b, s, pp, sums, stats, spread):
                pe.wait_ge(stats.sem, stats.at(b, 1))
                nc.tensor.matmul(pp[:, 0:24], grp[:, :], s[:, 0:24], start=True, stop=True).then_inc(sums.sem, 1)
                pe.wait_ge(spread.sem, spread.at(b, 1))
                nc.tensor.matmul(pp[:, 32:40], grp[:, :], s[:, 40:48], start=True, stop=True).then_inc(sums.sem, 1)

            def a1(j):
                gn(j, sa, pconv, a_sums, a_stats, a_spread)

            def a2_(j):
                for t in range(CT):
                    pe.wait_ge(a_xh.sem, a_xh.at(j, t + 1))
                    for k in range(2):
                        ins = nc.tensor.matmul(bank(pm, k)[0:K2], wk[:, t, :], bank(xh[:, t, :], k),
                                               start=(t == 0), stop=(t == CT - 1))
                ins.then_inc(a_key.sem, 1)
                for g in range(4):
                    if g >= 2:
                        pe.wait_ge(a_xtc.sem, a_xtc.at(j, g - 1))
                    for m in range(2):
                        for t in range(CT):
                            n = 2 * g + m
                            ins = nc.tensor.transpose(bank(pconv, g % 2)[:, (2 * m + t) * P:(2 * m + t + 1) * P],
                                                      xh[:, t, n * P:(n + 1) * P], ident[:, :])
                    ins.then_inc(a_xt.sem, 1)

            def a4(j):
                pe.wait_ge(a_dg.sem, a_dg.at(j, 1))
                for n in range(8):
                    ins = nc.tensor.matmul(pm[:, n * K2:(n + 1) * K2], ex[:, n * P:(n + 1) * P], dg49[:, :], start=True, stop=True)
                ins.then_inc(a_kt.sem, 1)
                pe.wait_ge(a_ktc.sem, a_ktc.at(j, 1))
                pe.wait_ge(a_xtc.sem, a_xtc.at(j, 4))
                for t in range(CT):
                    for n in range(8):
                        ins = nc.tensor.matmul(pm[:, HALF + t * K2:HALF + (t + 1) * K2], xt[:, n, t * P:(t + 1) * P], kt[:, n, :],
                                               start=(n == 0), stop=(n == 7))
                ins.then_inc(a_fi.sem, 1)

            def a5(j):
                def mix(w, src, o):
                    for t in range(CT):
                        for k in range(CT):
                            ins = nc.tensor.matmul(pm[:, o + t * 64:o + t * 64 + K2], w[:, k, t * P:(t + 1) * P], src[:, k, :],
                                                   start=(k == 0), stop=(k == CT - 1))
                    return ins
                pe.wait_ge(a_fic.sem, a_fic.at(j, 1))
                mix(w0, fi, 0).then_inc(a_f2.sem, 1)
                pe.wait_ge(a_f2c.sem, a_f2c.at(j, 1))
                nc.tensor.matmul(pm[:, 128:134], ones[:, :], sa[:, 60:66], start=True, stop=True).then_inc(a_sums.sem, 1)
                pe.wait_ge(a_spread.sem, a_spread.at(j, 2))
                nc.tensor.matmul(pm[:, 136:138], ones[:, :], sa[:, 72:74], start=True, stop=True).then_inc(a_sums.sem, 1)
                pe.wait_ge(a_f3.sem, a_f3.at(j, 1))
                mix(w1, f2, 256).then_inc(a_wg.sem, 1)

            def taps(j, lo, hi):
                for n in range(lo, hi):
                    r, dx = divmod(n, KK)
                    t, dy = ROWS[r]
                    if dx == 0:
                        pe.wait_ge(diag_made.sem, diag_made.at(j, r + 1))
                        if dy == 0 and t > 0:
                            pe.wait_ge(conv_out.sem, conv_out.at(j, t))
                    first, last = dy == 0 and dx == 0, dy == KK - 1 and dx == KK - 1
                    dh, dl = diag[:, r % RING, 0, dx, :], diag[:, r % RING, 1, dx, :]
                    for m, (w, part) in enumerate(((dh, 0), (dh, 1), (dl, 0))):
                        for k in range(2):
                            rows = dy + 16 * k
                            ins = nc.tensor.matmul(bank(pconv, k), w, pad[:, t, part, rows:rows + 16, dx:dx + W],
                                                   start=first and m == 0, stop=last and m == 2)
                    if dx == KK - 1:
                        ins.then_inc(row_done.sem, 1)

            def b1(i):
                gn(i, sg, slot_b, b_sums, b_stats, b_spread)

            def b2_(i):
                for t in range(CT):
                    pe.wait_ge(b_xg.sem, b_xg.at(i, t + 1))
                    for k in range(2):
                        ins = nc.tensor.matmul(bank(slot_b, k), wf[:, t, :], bank(xg[:, t, :], k), start=(t == 0), stop=(t == CT - 1))
                ins.then_inc(b_proj.sem, 1)
                for t in range(CT):
                    for k in range(2):
                        ins = nc.tensor.matmul(bank(slot_c, k), wz[:, t, :], bank(xg[:, t, :], k), start=(t == 0), stop=(t == CT - 1))
                ins.then_inc(b_proj.sem, 1)
                for lv, (w, o) in enumerate(((wc2, 0), (wc3, HALF))):
                    n = (L2, L3)[lv]
                    side = (16, 8)[lv]
                    src = f[:, (0, L1)[lv]:(0, L1)[lv] + 4 * n].rearrange("p (r s c e) -> p r s c e", s=2, e=2, c=side)
                    pe.wait_ge(b_f.sem, b_f.at(i, lv + 1))
                    for m in range(4):
                        ins = nc.tensor.matmul(slot_b[:, o:o + n], w[:, m, :], src[:, :, m // 2, :, m % 2], start=(m == 0), stop=(m == 3))
                    ins.then_inc(b_proj.sem, 1)

            def b3_(i):
                for c, (s, n, fc, st) in enumerate(CHUNKS):
                    k = c % 2
                    if c == 0:
                        pe.wait_ge(b_f.sem, b_f.at(i, 3))
                        pe.wait_ge(b_z.sem, b_z.at(i, 1))
                    if c >= 2:
                        pe.wait_ge(ch_rest.sem, ch_rest.at(i, c - 1))
                        pe.wait_ge(ch_pos.sem, ch_pos.at(i, c - 1))
                    nc.tensor.matmul(bank(slot_b, k)[0:96, 0:n], wbc[:, st, :], f[:, fc:fc + n], start=True, stop=True).then_inc(ch_bc.sem, 1)
                    nc.tensor.matmul(bank(slot_c, k)[:, 0:n], wdelta[:, st, :], f[:, fc:fc + n], start=True, stop=True).then_inc(ch_dt.sem, 1)

            def spread(i, k, slot, row0, done):
                lv, st, dd, n0, m = UNITS[k]
                ln, fc, sc, _ = LEVEL[lv]
                so = SB if dd == 1 else sc
                per = min(ln, HALF)
                for n in range(m):
                    for c in range(0, ln, per):
                        o = n * ln + c
                        ins = nc.tensor.matmul(slot[:, o:o + per], sel[:, row0 + n0 + n:row0 + n0 + n + 1].to_broadcast([96, P]), bcs[:, so + c:so + c + per],
                                               start=True, stop=True)
                ins.then_inc(done.sem, 1)

            def put_b(i, k):
                if k == 0:
                    pe.wait_ge(ch_lo.sem, ch_lo.at(i, NCH))
                    pe.wait_ge(ch_rest.sem, ch_rest.at(i, NCH))
                else:
                    pe.wait_ge(u_bx.sem, u_bx.at(i, k))
                spread(i, k, slot_b, 0, u_b)

            def put_c(i, k):
                if k == 0:
                    pe.wait_ge(ch_pos.sem, ch_pos.at(i, NCH))
                    pe.wait_ge(ch_abs.sem, ch_abs.at(i, NCH))
                else:
                    pe.wait_ge(q_pr.sem, q_pr.at(i, products_of(k - 1)[-1] + 1))
                spread(i, k, slot_c, NS, u_c)

            def norm(i, k):
                d, c0, n = NORMS[k]
                src = y[:, :, c0:c0 + n] if d == 2 else y[:, d, c0:c0 + n]
                cols = 2 * n if d == 2 else n
                qn = {0: 2, 1: 10, 2: 26, 3: 42, 4: 26, 5: 42}[k]
                if k == 0:
                    pe.wait_ge(y_init.sem, y_init.at(i, 5))
                else:
                    pe.wait_ge(n_t.sem, n_t.at(i, k))
                pe.wait_ge(q_y.sem, q_y.at(i, NORM_NEEDS[k]))
                o = pm[:, 0:cols]
                if d == 2:
                    o = o.rearrange("p (d n) -> p d n", d=2)
                nc.tensor.matmul(o, cen[:, :], src, start=True, stop=True).then_inc(n_yc.sem, 1)
                pe.wait_ge(n_sq.sem, n_sq.at(i, k + 1))
                nc.tensor.matmul(pm[:, HALF:HALF + cols], ones[:, :], sq[:, 0, 0:cols], start=True, stop=True).then_inc(n_var.sem, 1)

            def b_end(i):
                norm(i, 4)
                norm(i, 5)
                for hh in range(2):
                    pe.wait_ge(b_g.sem, b_g.at(i, hh + 1))
                    for t in range(CT):
                        nc.tensor.matmul(bank((slot_b, slot_c)[hh], t), wo[:, t * P:(t + 1) * P], o1[:, hh * HALF:(hh + 1) * HALF],
                                         start=True, stop=True).then_inc(b_out.sem, 1)

            def units(i, j):
                total = CT * K2
                if i is None:
                    taps(j, 0, total)
                    return
                put_b(i, 0)
                put_c(i, 0)
                at = 0
                for k in range(NU):
                    if k + 1 < NU:
                        put_b(i, k + 1)
                    mid, end = total * (2 * k + 1) // (2 * NU), total * (k + 1) // NU
                    if j is not None:
                        taps(j, at, mid)
                    if k + 1 < NU:
                        put_c(i, k + 1)
                    if j is not None:
                        taps(j, mid, end)
                    at = end
                    for nn, where in NORM_AT.items():
                        if where == k:
                            norm(i, nn)

            stages(a1, a2_, None, a4, a5, b1, b2_, b3_, None, units, b_end, pe)

        @block.scalar
        def _(act):
            act.preload_act_table_set("natural_log_exp_and_others")
            act.wait_ge(consts_in, LOADED)
            nc.scalar.activation(nega[:, :, :], al[:, :, :], ACT.Exp).then_inc(setup, 1)
            act.wait_ge(setup_pe, 1)
            nc.scalar.activation(wf[:, :, :], pm[:, 0:C].rearrange("p (t m) -> p t m", t=CT), ACT.Copy).then_inc(setup, 1)
            nc.scalar.activation(bf1[:, :], pm[:, HALF:HALF + 1], ACT.Identity, bias=v_c1).then_inc(setup, 1)
            act.wait_ge(setup_pe, 2)
            nc.scalar.activation(wdelta[:, :, :], pconv[:, 0:3 * P].rearrange("p (t m) -> p t m", t=3), ACT.Copy).then_inc(setup, 1)
            act.wait_ge(setup, 5)
            act.wait_ge(setup, DVE_SET + 4)
            nc.scalar.mul(nega[:, :, :], nega[:, :, :], -1.0).then_inc(setup, 1)
            act.wait_ge(setup, DVE_SET + ACT_SET)

            def rsqrt(b, s, var, rstd, c, iv, io, n):
                act.wait_ge(var.sem, var.at(b, c))
                return (nc.scalar.activation(s[:, io - 2:io - 2 + n], s[:, iv:iv + n], ACT.Ln, bias=eps[:, 0:1]),
                        lambda: nc.scalar.activation(s[:, io:io + n], s[:, io - 2:io - 2 + n], ACT.Exp, scale=-0.5).then_inc(rstd.sem, 1))

            def a1(j):
                act_a.start(act, j)
                ins, fin = rsqrt(j, sa, a_var, a_rstd, 1, 50, 54, 2)
                act_a(ins)
                fin()
                act.wait_ge(a_rstd.sem, a_rstd.at(j, 1))
                act.wait_ge(a_shift.sem, a_shift.at(j, 1))
                for t in range(CT):
                    nc.scalar.activation(xh[:, t, :], xr[:, t, :], ACT.Identity, scale=sa[:, 54 + t:55 + t],
                                         bias=sa[:, 56 + t:57 + t]).then_inc(a_xh.sem, 1)
                for t in range(CT):
                    nc.scalar.activation(pad[:, t, 0, 3:3 + H, 3:3 + W], img(xr[:, t, :], W), ACT.Identity,
                                         scale=sa[:, 54 + t:55 + t], bias=sa[:, 56 + t:57 + t]).then_inc(a_hi.sem, 1)

            def a2_(j):
                act.wait_ge(a_key.sem, a_key.at(j, 1))
                nc.scalar.activation(ex[:, :], pm[0:K2, :], ACT.Identity, bias=kb[:, 0:1]).then_inc(a_keyb.sem, 1)
                for g in range(4):
                    act.wait_ge(a_xt.sem, a_xt.at(j, g + 1))
                    nc.scalar.activation(xt[:, 2 * g:2 * g + 2, :], bank(pconv, g % 2).rearrange("p (n c) -> p n c", n=2),
                                         ACT.Copy).then_inc(a_xtc.sem, 1)

            def a3_(j):
                act.wait_ge(a_max.sem, a_max.at(j, 1))
                nc.scalar.activation(ex[:, :], ex[:, :], ACT.Exp, bias=sk[:, 0:1], accum_out=sk[:, 1:2]).then_inc(a_exp.sem, 1)

            def a5(j):
                ins, fin = rsqrt(j, sa, a_var, a_rstd, 2, 74, 78, 1)
                act_a(ins)
                nc.scalar.activation(sa[:, 76:77], sa[:, 76:77], ACT.Exp, scale=-0.5).then_inc(a_rstd.sem, 1)
                act_a.end()

            def b1(i):
                act_b.start(act, i)
                ins, fin = rsqrt(i, sg, b_var, b_rstd, 1, 50, 54, 2)
                act_b(ins)
                fin()
                act.wait_ge(b_rstd.sem, b_rstd.at(i, 1))
                act.wait_ge(b_shift.sem, b_shift.at(i, 1))
                for t in range(CT):
                    nc.scalar.activation(xg[:, t, :], xn[:, t, :], ACT.Identity, scale=sg[:, 54 + t:55 + t],
                                         bias=sg[:, 56 + t:57 + t]).then_inc(b_xg.sem, 1)
                act_b.end()

            def b2_(i):
                act.wait_ge(b_proj.sem, b_proj.at(i, 1))
                nc.scalar.activation(f[:, 0:L1], slot_b[:, :], ACT.Identity, bias=bf1[:, 0:1]).then_inc(b_f.sem, 1)
                act.wait_ge(b_proj.sem, b_proj.at(i, 3))
                nc.scalar.activation(f[:, L1:L1 + L2], slot_b[:, 0:L2], ACT.Identity, bias=v_c2).then_inc(b_f.sem, 1)
                nc.scalar.activation(sz[:, :], slot_c[:, :], ACT.Identity, bias=v_inz).then_inc(b_z.sem, 1)
                act.wait_ge(b_proj.sem, b_proj.at(i, 4))
                nc.scalar.activation(f[:, L1 + L2:LF], slot_b[:, HALF:HALF + L3], ACT.Identity, bias=v_c3).then_inc(b_f.sem, 1)

            def b3_(i):
                def log(c):
                    s, n, _, _ = CHUNKS[c]
                    act.wait_ge(ch_err.sem, ch_err.at(i, c + 1))
                    nc.scalar.activation(qs[:, s:s + n], qs[:, s:s + n], ACT.Ln).then_inc(ch_ln.sem, 1)
                    act.wait_ge(ch_rest.sem, ch_rest.at(i, c + 1))
                    nc.scalar.activation(bcs[0:64, s:s + n], rest[:, c % 2, 0:n], ACT.Copy).then_inc(ch_mid.sem, 1)
                for c, (s, n, fc, st) in enumerate(CHUNKS):
                    k = c % 2
                    act.wait_ge(ch_bc.sem, ch_bc.at(i, c + 1))
                    nc.scalar.activation(bcs[:, s:s + n], bank(slot_b, k)[0:96, 0:n], ACT.Copy).then_inc(ch_hi.sem, 1)
                    act.wait_ge(ch_dt.sem, ch_dt.at(i, c + 1))
                    nc.scalar.activation(es[:, s:s + n], bank(slot_c, k)[:, 0:n], ACT.Abs, bias=v_dtb[:, st:st + 1]).then_inc(ch_abs.sem, 1)
                    act.wait_ge(ch_abs.sem, ch_abs.at(i, c + 1))
                    nc.scalar.activation(es[:, s:s + n], es[:, s:s + n], ACT.Exp, scale=-1.0).then_inc(ch_exp.sem, 1)
                    act.wait_ge(ch_exp.sem, ch_exp.at(i, c + 1))
                    nc.scalar.activation(qs[:, s:s + n], es[:, s:s + n], ACT.Identity, bias=1.0).then_inc(ch_q.sem, 1)
                    if c:
                        log(c - 1)
                log(NCH - 1)

            def b4_(i):
                act.wait_ge(b_z.sem, b_z.at(i, 1))
                nc.scalar.activation(o1[:, :], sz[:, :], ACT.Exp, scale=-1.0).then_inc(b_z.sem, 1)
                for d, o, n, p in ((0, 0, L1, 0), (0, L1, L2, 1), (0, L1 + L2, L3, 2), (1, 0, L1 + L2, 1), (1, L1 + L2, L3, 2)):
                    nc.scalar.activation(y[:, d, o:o + n], f[:, o:o + n], ACT.Copy, scale=v_dv[:, p:p + 1]).then_inc(y_init.sem, 1)

            def decay(i, k):
                lv, st, dd, n0, m = UNITS[k]
                ln, fc, sc, _ = LEVEL[lv]
                so = SB if dd == 1 else sc
                if k == 0:
                    act.wait_ge(ch_delta.sem, ch_delta.at(i, NCH))
                    act.wait_ge(ch_u.sem, ch_u.at(i, NCH))
                if k >= 2:
                    act.wait_ge(q_h.sem, q_h.at(i, products_of(k - 2)[-1] + 1))
                for n in range(m):
                    o = ea[:, k % 2, 0:ln] if lv == 1 else a3[:, n, 0:ln] if lv == 3 else a2[:, k % 2, n, 0:ln]
                    ins = nc.scalar.activation(o, delta[:, so:so + ln], ACT.Exp, scale=nega[:, st, n0 + n:n0 + n + 1])
                ins.then_inc(u_ea.sem, 1)

            def norm(i, k):
                d, c0, n = NORMS[k]
                cols = 2 * n if d == 2 else n
                act.wait_ge(n_yc.sem, n_yc.at(i, k + 1))
                nc.scalar.activation(sq[:, 0, 0:cols], pm[:, 0:cols], ACT.Square).then_inc(n_sq.sem, 1)
                act.wait_ge(n_var.sem, n_var.at(i, k + 1))
                if k:
                    act.wait_ge(n_o.sem, n_o.at(i, STEPS[k]))
                nc.scalar.activation(rs[:, 0, 0:cols], pm[:, HALF:HALF + cols], ACT.Ln, bias=eps[:, 0:1]).then_inc(n_ln.sem, 1)
                act.wait_ge(n_ln.sem, n_ln.at(i, k + 1))
                nc.scalar.activation(rs[:, 1, 0:cols], rs[:, 0, 0:cols], ACT.Exp, scale=-0.5).then_inc(n_rs.sem, 1)

            def units(i, j):
                if i is None:
                    return
                decay(i, 0)
                decay(i, 1)
                for k in range(NU):
                    if k + 2 < NU:
                        decay(i, k + 2)
                    for nn, where in NORM_AT.items():
                        if where == k:
                            norm(i, nn)

            def b_end(i):
                norm(i, 4)
                norm(i, 5)

            stages(a1, a2_, a3_, None, a5, b1, b2_, b3_, b4_, units, b_end, act)

        @block.gpsimd
        def _(pool):
            pool.wait_ge(setup, DVE_SET + ACT_SET)

            def a1(j):
                pool.wait_ge(a_hi.sem, a_hi.at(j, CT))
                copy_x(j)

            def copy_x(j):
                if not (isinstance(j, int) and j == 0):
                    pool.wait_ge(b_xc.sem, b_xc.at(j, 0))
                    pool.wait_ge(b_xg.sem, b_xg.at(j, 0))
                pool.tensor_tensor(token[:, 0:1], eps[:, :], eps[:, :], ALU.add)
                pool.tensor_copy(xn[:, :, :], xr[:, :, :]).then_inc(a_copy.sem, 1)
                pool.wait_ge(a_pad.sem, a_pad.at(j, CT))
                pool.wait_ge(a_copy.sem, a_copy.at(j, 1))
                pool.tensor_tensor(token[:, 0:1], eps[:, :], eps[:, :], ALU.add).then_inc(xr_free.sem, 1)

            def b3_(i):
                def low(c):
                    s, n, fc, _ = CHUNKS[c]
                    pool.wait_ge(ch_mid.sem, ch_mid.at(i, c + 1))
                    pool.tensor_tensor(bcs[0:32, s:s + n], rest[0:32, c % 2, 0:n], bcs[0:32, s:s + n], ALU.subtract).then_inc(ch_lo.sem, 1)
                    pool.wait_ge(ch_m2.sem, ch_m2.at(i, c + 1))
                    pool.wait_ge(ch_ln.sem, ch_ln.at(i, c + 1))
                    pool.tensor_tensor(delta[:, s:s + n], delta[:, s:s + n], qs[:, s:s + n], ALU.add).then_inc(ch_delta.sem, 1)
                    pool.wait_ge(ch_delta.sem, ch_delta.at(i, c + 1))
                    pool.tensor_tensor(u[:, s:s + n], delta[:, s:s + n], f[:, fc:fc + n], ALU.mult).then_inc(ch_u.sem, 1)
                for c in range(NCH):
                    low(c)

            def make_row(j, r):
                t, dy = ROWS[r]
                if r >= RING:
                    pool.wait_ge(row_done.sem, row_done.at(j, r - RING + 1))
                elif not (isinstance(j, int) and j == 0):
                    pool.wait_ge(row_done.sem, row_done.at(j, 0))
                for m, w in enumerate((whi, wlo)):
                    ins = pool.tensor_tensor(diag[:, r % RING, m, :, :], id16[:, None, :].to_broadcast([P, KK, P]),
                                             w[:, t, dy * KK:(dy + 1) * KK, None].to_broadcast([P, KK, P]), ALU.mult)
                ins.then_inc(diag_made.sem, 1)

            def a5(j):
                pool.wait_ge(a_w16.sem, a_w16.at(j, 1))
                make_row(j, 0)
                make_row(j, 1)

            def gather(i, q):
                k, d = PRODUCTS[q]
                lv, m = UNITS[k][0], UNITS[k][4]
                ln, fc, _, _ = LEVEL[lv]
                yv = y[:, d, fc:fc + ln]
                if q == 0:
                    pool.wait_ge(y_init.sem, y_init.at(i, 5))
                pool.wait_ge(q_pr.sem, q_pr.at(i, q + 1))
                src = pr[:, q % 2, :]
                width = HW // 2
                while width >= ln:
                    pool.tensor_tensor(src[:, 0:width], src[:, 0:width], src[:, width:2 * width], ALU.add).then_inc(n_y.sem, 1)
                    gather.n += 1
                    pool.wait_ge(n_y.sem, n_y.at(i, gather.n))
                    width //= 2
                if q:
                    pool.wait_ge(q_y.sem, q_y.at(i, q))
                pool.tensor_tensor(yv, yv, src[:, 0:ln], ALU.add).then_inc(q_y.sem, 1)

            def units(i, j):
                gather.n = 0
                r = 2
                if i is None:
                    for r in range(2, NR):
                        make_row(j, r)
                    return
                for k in range(NU):
                    while j is not None and r < NR and (r - 2) * NU <= k * NR:
                        make_row(j, r)
                        r += 1
                    for q in products_of(k):
                        gather(i, q)
                assert gather.n == n_y.per

            stages(a1, None, None, None, a5, None, None, b3_, None, units, None, pool)


NORM_AT = {0: 3, 1: 8, 2: 24, 3: 26}
NORM_NEEDS = {0: 2, 1: 10, 2: 26, 3: 26, 4: 42, 5: 42}
STEPS = [0, 2, 5, 7, 9, 10, 11]


def stages(a1, a2, a3, a4, a5, b1, b2, b3, b4, units, b_end, eng):
    def body(i, j):
        for stage, b in ((b1, i), (a1, j), (b2, i), (a2, j), (b3, i), (a3, j), (a4, j), (b4, i), (a5, j)):
            if stage is not None and b is not None:
                stage(b)
        units(i, j)
        if b_end is not None and i is not None:
            b_end(i)
    body(None, 0)
    with eng.Fori(0, B - 1) as i:
        body(i, i + 1)
    body(B - 1, None)


_INS = ["x"]


def kernel(**inputs):
    import numpy as np
    import concourse.bacc as bacc
    from concourse.bass_utils import run_bass_kernel_spmd as run

    A = {n: np.asarray(v) for n, v in inputs.items()}
    g0 = lambda n: A["L0_conv_" + n]
    g1 = lambda n: A["L1_conv_" + n]

    def tiles(w):
        return w.reshape(CT, P, -1).transpose(1, 0, 2)

    eye = np.eye(P, dtype=np.float32)
    sel = np.concatenate([np.eye(32, dtype=np.float32)] * 3)
    arrays = {
        "x": A["x"],
        "c_ident": eye,
        "c_cen": eye - np.float32(1.0 / D),
        "c_ones": np.full((P, P), 1.0 / D, np.float32),
        "c_grp": np.kron(np.eye(P // GROUP), np.full((GROUP, GROUP), 1.0 / (4 * GROUP))).astype(np.float32),
        "c_sel": sel,
        "wk": tiles(g0("K_w").T),
        "w0": tiles(g0("conv0_w").T),
        "w1": tiles(g0("conv1_w").T),
        "win": g1("in_w")[:P],
        "wz": tiles(g1("in_w")[P:].T),
        "wc1": g1("c1_w").T,
        "wc2": g1("c2_w").reshape(P, P, 4).transpose(1, 2, 0),
        "wc3": g1("c3_w").reshape(P, P, 4).transpose(1, 2, 0),
        "wo": g1("out_w").T,
        "wx8": np.stack([g1(f"xw{s}")[:R_DT] for s in (1, 2, 3)], 1),
        "wdt": np.stack([g1(f"dtw{s}").T for s in (1, 2, 3)], 1),
        "wbc": np.stack([np.concatenate([g1(f"xw{s}")[R_DT:].T] * 3, 1) for s in (1, 2, 3)], 1),
        "vec": np.stack([g1("in_b")[:P], g1("in_b")[P:], g1("c1_b"), g1("c2_b"), g1("c3_b"),
                         *g1("out_b").reshape(CT, P), *g0("conv0_b").reshape(CT, P), *g0("conv1_b").reshape(CT, P),
                         *[g1(f"{n}{s}") for n in ("dtb", "Dv", "g", "be") for s in (1, 2, 3)]], 1),
        "kb": g0("K_b")[:, None],
        "lnw": tiles(g0("ln_w").reshape(C, K2)),
        "lnb": tiles(g0("ln_b").reshape(C, K2)),
        "al": np.stack([g1(f"Al{s}") for s in (1, 2, 3)], 1),
    }
    arrays = {n: np.ascontiguousarray(v) for n, v in arrays.items()}
    nc = bacc.Bacc("TRN2", target_bir_lowering=False, num_devices=1)
    aps = {n: nc.dram_tensor("in_" + n, v.shape, mybir.dt.from_np(v.dtype), kind="ExternalInput").ap() for n, v in arrays.items()}
    out = nc.dram_tensor("out_0", A["x"].shape, F32, kind="ExternalOutput").ap()
    build(nc, aps, out)
    r = run(nc, [{"in_" + n: v for n, v in arrays.items()}], core_ids=[0])
    return r.results[0]["out_0"]
```

```python
from contextlib import ExitStack

import concourse.bass as bass
from concourse import mybir

ALU = mybir.AluOpType
ACT = mybir.ActivationFunctionType
AX = mybir.AxisListType
F32 = mybir.dt.float32
F16 = mybir.dt.float16
BF16 = mybir.dt.bfloat16

P = 128
B, C, H, W = 16, 256, 32, 32
HW = H * W
CT = C // P
KK = 7
K2 = KK * KK
PADW = W + KK - 1
D = 128
NS = 16
R_DT = 8
L1, L2, L3 = HW, HW // 4, HW // 16
LF = L1 + L2 + L3
HALF = 512
GROUP = C // 32
SA, SB, SC, SD = 0, L1, 2 * L1, 2 * L1 + L2
LS = 2 * L1 + L2 + L3
CHUNKS = [(SD, L3, L1 + L2, 2), (SC, L2, L1, 1),
          (SA, HALF, 0, 0), (SA + HALF, HALF, HALF, 0), (SB, HALF, 0, 1), (SB + HALF, HALF, HALF, 1)]
NCH = len(CHUNKS)
UNITS = [(3, 2, 2, 0, NS)] + [(2, 1, 2, n, 4) for n in range(0, NS, 4)] + \
        [(1, 0, 0, n, 1) for n in range(NS)] + [(1, 1, 1, n, 1) for n in range(NS)]
NU = len(UNITS)
PRODUCTS = [(u, d) for u, (_, _, dd, _, _) in enumerate(UNITS) for d in ((0, 1) if dd == 2 else (dd,))]
NP = len(PRODUCTS)
LEVEL = {1: (L1, 0, SA, 1), 2: (L2, L1, SC, 4), 3: (L3, L1 + L2, SD, NS)}
BUF = NS * (L3 + 1)
ROWS = [(t, r) for t in range(CT) for r in range(KK)]
NR = len(ROWS)
HR = 3
RING = 4
EPS = 1e-5
NORMS = [(2, L1 + L2, L3), (2, L1, L2), (0, 0, HALF), (0, HALF, HALF), (1, 0, HALF), (1, HALF, HALF)]
NN = len(NORMS)

CONSTS = ["ident", "cen", "ones", "grp"]


def products_of(u):
    return [q for q, (v, _) in enumerate(PRODUCTS) if v == u]


def build(nc, a, out):
    with ExitStack() as ctx:
        def sb(name, shape, dt=F32):
            return ctx.enter_context(nc.sbuf_tensor(name, shape, dt))

        def ps(name, shape, dt=F32):
            return ctx.enter_context(nc.psum_tensor(name, shape, dt))

        def sem(name):
            return ctx.enter_context(nc.semaphore(name))

        class Count:

            def __init__(self, name, per):
                self.sem, self.per = sem(name), per

            def at(self, b, c):
                return b * self.per + c

        class Chain:

            def __init__(self, name, per):
                self.count, self.per = Count(name, per), per

            def start(self, eng, b):
                self.eng, self.b, self.n = eng, b, 0

            def __call__(self, ins):
                self.n += 1
                ins.then_inc(self.count.sem, 1)
                self.eng.wait_ge(self.count.sem, self.count.at(self.b, self.n))

            def end(self):
                assert self.n == self.per, (self.n, self.per)

        mats = {n: sb(n, [P, P]) for n in CONSTS}
        ident, cen, ones, grp = (mats[n] for n in CONSTS)
        id16 = sb("id16", [P, P], F16)
        sel = sb("sel", [96, 32], BF16)
        sel32 = sb("sel32", [96, 32])
        wk = sb("wk", [P, CT, K2])
        w0 = sb("w0", [P, CT, C])
        w1 = sb("w1", [P, CT, C])
        win = sb("win", [P, C])
        wz = sb("wz", [P, CT, P])
        wc1 = sb("wc1", [P, P])
        wf = sb("wf", [P, CT, P])
        wc2 = sb("wc2", [P, 4, P])
        wc3 = sb("wc3", [P, 4, P])
        wo = sb("wo", [P, C])
        wx8 = sb("wx8", [R_DT, 3, P])
        wdt = sb("wdt", [R_DT, 3, P])
        wdelta = sb("wdelta", [P, 3, P])
        wbc = sb("wbc", [P, 3, 96])
        vec = sb("vec", [P, 32])
        kb = sb("kb", [K2, 1])
        lnw = sb("lnw", [P, CT, K2])
        lnb = sb("lnb", [P, CT, K2])
        al = sb("al", [P, 3, NS])
        nega = sb("nega", [P, 3, NS])
        bf1 = sb("bf1", [P, 1])
        eps = sb("eps", [P, 1])
        bes = sb("bes", [P, 3])
        v_inx, v_inz, v_c1, v_c2, v_c3 = (vec[:, i:i + 1] for i in range(5))
        v_out, v_b0, v_b1 = (vec[:, i:i + 2] for i in (5, 7, 9))
        v_dtb, v_dv, v_g, v_be = (vec[:, i:i + 3] for i in (11, 14, 17, 20))

        xr = sb("xr", [P, CT, HW])
        xh = sb("xh", [P, CT, HW])
        pad = sb("pad", [P, CT, 2, PADW, PADW], F16)
        ex = sb("ex", [K2, HW])
        kt = sb("kt", [P, HW // P, K2])
        dg49 = sb("dg49", [K2, K2])
        fi = sb("fi", [P, CT, K2])
        f2 = sb("f2", [P, CT, K2])
        wg = sb("wg", [P, CT, K2])
        whi = sb("whi", [P, CT, K2], F16)
        wlo = sb("wlo", [P, CT, K2], F16)
        wsc = sb("wsc", [P, CT])
        chi = sb("chi", [P, CT, K2], F16)
        clo = sb("clo", [P, CT, K2], F16)
        csc = sb("csc", [P, CT])
        diag = sb("diag", [P, RING, 2, KK, P], F16)
        sa = sb("sa", [P, 128])
        sk = sb("sk", [K2, 4])

        xn = sb("xn", [P, CT, HW])
        xc = sb("xc", [P, CT, HW])
        xg = sb("xg", [P, CT, HW])
        xt = xg[:, :, :].rearrange("p t (n c) -> p (t n) c", c=C)
        f = sb("f", [P, LF])
        sz = sb("sz", [P, HW])
        bcs = sb("bcs", [96, LS], BF16)
        rest = sb("rest", [64, 2, HALF])
        delta = sb("delta", [P, LS])
        u = sb("u", [P, LS])
        y = sb("y", [P, 2, LF])
        work = sb("work", [P, 4 + HR, BUF])
        ea, bx, h = work[:, 0:2, :], work[:, 2:4, :], work[:, 4:4 + HR, :]
        es, qs, rs = (sb(n, [P, 2, HALF]) for n in ("es", "qs", "rs"))
        er = rs
        a3, b3 = sb("a3", [P, NS, L3 + 1]), sb("b3", [P, NS, L3 + 1])
        a2, b2 = (v[:, :, 0:4 * (L2 + 1)].rearrange("p a (m l) -> p a m l", m=4) for v in (ea, bx))
        sq = es
        o3 = sb("o3", [P, L3])
        o2 = sb("o2", [P, L2])
        o1 = sb("o1", [P, HW])
        ob = sb("ob", [P, CT, HW])
        token = sb("token", [P, 1])
        sg = sb("sg", [P, 128])
        slot_b = ps("slot_b", [P, HW])
        slot_c = ps("slot_c", [P, HW])
        pconv = ps("pconv", [P, HW])
        pm = ps("pm", [P, HW])

        consts_in = sem("consts_in")
        setup_pe = sem("setup_pe")
        setup = sem("setup")
        x_in = Count("x_in", 16)
        ob_free = Count("ob_free", 16)
        ob_ready = Count("ob_ready", 1)
        ea_a, ea_b = Chain("dve_a", 18), Chain("dve_b", 3)
        act_a, act_b = Chain("act_a", 2), Chain("act_b", 1)
        a_stats = Count("a_stats", 1)
        a_sums = Count("a_sums", 4)
        a_spread = Count("a_spread", 2)
        a_var = Count("a_var", 2)
        a_rstd = Count("a_rstd", 2)
        a_shift = Count("a_shift", 1)
        a_xh = Count("a_xh", CT)
        a_hi = Count("a_hi", CT)
        a_pad = Count("a_pad", CT)
        a_key = Count("a_key", 1)
        a_keyb = Count("a_keyb", 1)
        a_max = Count("a_max", 1)
        a_exp = Count("a_exp", 1)
        a_dg = Count("a_dg", 1)
        a_xt = Count("a_xt", 4)
        a_xtc = Count("a_xtc", 4)
        a_kt = Count("a_kt", 1)
        a_ktc = Count("a_ktc", 1)
        a_fi = Count("a_fi", 1)
        a_fic = Count("a_fic", 1)
        a_f2 = Count("a_f2", 1)
        a_f2c = Count("a_f2c", 1)
        a_f3 = Count("a_f3", 1)
        a_wg = Count("a_wg", 1)
        a_wgc = Count("a_wgc", 1)
        a_w16 = Count("a_w16", 1)
        c_w = Count("c_w", 1)
        a_copy = Count("a_copy", 1)
        diag_made = Count("diag_made", NR)
        row_done = Count("row_done", NR)
        conv_out = Count("conv_out", CT)
        b_stats = Count("b_stats", 1)
        b_sums = Count("b_sums", 2)
        b_spread = Count("b_spread", 1)
        b_var = Count("b_var", 1)
        b_rstd = Count("b_rstd", 1)
        b_shift = Count("b_shift", 1)
        b_xg = Count("b_xg", CT)
        b_xc = Count("b_xc", 1)
        b_proj = Count("b_proj", 4)
        b_f = Count("b_f", 3)
        b_z = Count("b_z", 2)
        b_sz = Count("b_sz", 1)
        ch_bc = Count("ch_bc", NCH)
        ch_dt = Count("ch_dt", NCH)
        ch_hi = Count("ch_hi", NCH)
        ch_abs = Count("ch_abs", NCH)
        ch_exp = Count("ch_exp", NCH)
        ch_q = Count("ch_q", NCH)
        ch_pos = Count("ch_pos", NCH)
        ch_rest = Count("ch_rest", NCH)
        ch_err = Count("ch_err", NCH)
        ch_ln = Count("ch_ln", NCH)
        ch_mid = Count("ch_mid", NCH)
        ch_sub = Count("ch_sub", NCH)
        ch_min = Count("ch_min", NCH)
        ch_lo = Count("ch_lo", NCH)
        ch_delta = Count("ch_delta", NCH)
        ch_u = Count("ch_u", NCH)
        y_init = Count("y_init", 5)
        u_b = Count("u_b", NU)
        u_c = Count("u_c", NU)
        u_ea = Count("u_ea", NU)
        u_bx = Count("u_bx", NU)
        u_zero = Count("u_zero", 2)
        z_clip = Count("z_clip", 1)
        z_ln = Count("z_ln", 1)
        z_sig = Count("z_sig", 1)
        q_h = Count("q_h", NP)
        q_pr = Count("q_pr", NP)
        q_y = Count("q_y", NP)
        n_y = Count("n_y", 24)
        n_yc = Count("n_yc", NN)
        n_sq = Count("n_sq", NN)
        n_var = Count("n_var", NN)
        n_ln = Count("n_ln", NN)
        n_rs = Count("n_rs", NN)
        n_t = Count("n_t", NN)
        n_o = Count("n_o", STEPS[-1])
        b_g = Count("b_g", 2)
        b_out = Count("b_out", 4)

        xv = a["x"].rearrange("b (t p) h w -> b p t (h w)", p=P)
        ov = out.rearrange("b (t p) h w -> b p t (h w)", p=P)
        block = ctx.enter_context(nc.Block())

        loads = [(mats[n][:, :], a["c_" + n]) for n in CONSTS] + [
            (sel32[:, :], a["c_sel"]),
            (wk[:, :, :], a["wk"]), (w0[:, :, :], a["w0"]), (w1[:, :, :], a["w1"]), (win[:, :], a["win"]),
            (wz[:, :, :], a["wz"]), (wc1[:, :], a["wc1"]), (wc2[:, :, :], a["wc2"]), (wc3[:, :, :], a["wc3"]),
            (wo[:, :], a["wo"]), (wx8[:, :, :], a["wx8"]), (wdt[:, :, :], a["wdt"]), (wbc[:, :, :], a["wbc"]),
            (vec[:, 0:23], a["vec"]), (kb[:, :], a["kb"]), (lnw[:, :, :], a["lnw"]), (lnb[:, :, :], a["lnb"]),
            (al[:, :, :], a["al"])]
        LOADED = 16 * len(loads)
        DVE_SET, ACT_SET = 7, 5

        def bank(t, k):
            return t[:, k * HALF:(k + 1) * HALF]

        def norm_psum(k):
            t = slot_b if k == 5 else pm
            return bank(t, 0), bank(t, 1)

        def norm_sbuf(k):
            return (es[:, 1], qs[:, 0], qs[:, 1]) if k == 5 else (es[:, 0], rs[:, 0], rs[:, 1])

        def img(ap, side):
            return ap.rearrange("p (r c) -> p r c", c=side)

        @block.sync
        def _(sp):
            for dst, src in loads:
                sp.dma_start(dst, src).then_inc(consts_in, 16)
            sp.dma_start(token[0:K2, :], a["kb"]).then_inc(ob_free.sem, 16)
            sp.dma_start(xr[:, :, :], xv[0]).then_inc(x_in.sem, 16)
            sp.wait_ge(a_copy.sem, a_copy.at(1, 0))
            sp.dma_start(xr[:, :, :], xv[1]).then_inc(x_in.sem, 16)
            with sp.Fori(0, B - 2) as i:
                sp.wait_ge(a_copy.sem, a_copy.at(i + 2, 0))
                sp.dma_start(xr[:, :, :], xv[i + 2]).then_inc(x_in.sem, 16)
                sp.wait_ge(ob_ready.sem, ob_ready.at(i + 1, 0))
                sp.dma_start(ov[i], ob[:, :, :]).then_inc(ob_free.sem, 16)
            for i in range(B - 2, B):
                sp.wait_ge(ob_ready.sem, ob_ready.at(i + 1, 0))
                sp.dma_start(ov[i], ob[:, :, :]).then_inc(ob_free.sem, 16)
            sp.wait_ge(ob_free.sem, ob_free.at(B + 1, 0))

        @block.vector
        def _(dve):
            for ins in (nc.vector.memset(eps[:, :], EPS), nc.vector.memset(pad[:, :, :, :, :], 0.0),
                        nc.vector.memset(a3[:, :, :], 0.0), nc.vector.memset(b3[:, :, :], 0.0)):
                ins.then_inc(setup, 1)
            dve.wait_ge(consts_in, LOADED)
            nc.vector.tensor_copy(id16[:, :], ident[:, :]).then_inc(setup, 1)
            nc.vector.tensor_copy(sel[:, :], sel32[:, :]).then_inc(setup, 1)
            nc.vector.scalar_tensor_tensor(bes[:, 0:1], v_be[:, 0:1], 0.0, v_be[:, 1:2], ALU.add, ALU.add)
            nc.vector.tensor_scalar(bes[:, 1:3], v_be[:, 1:3], 2.0, None, ALU.mult).then_inc(setup, 1)
            dve.wait_ge(setup, DVE_SET + ACT_SET)

            def stats(b, s, x, done):
                for t in range(CT):
                    for k in range(2):
                        ins = nc.vector.bn_stats(s[:, 12 * t + 6 * k:12 * t + 6 * k + 6], bank(x[:, t, :], k))
                ins.then_inc(done.sem, 1)

            def a_s0(m):
                ea_a.start(dve, m)
                dve.wait_ge(x_in.sem, x_in.at(m + 1, 0))
                stats(m, sa, xr, a_stats)

            def gn_spread(ch, b, s, pp, sums, spread):
                st = s[:, 0:24].rearrange("p (t k c) -> p t k c", t=CT, c=3)
                gm = pp[:, 0:24].rearrange("p (t k c) -> p t k c", t=CT, c=3)
                d = s[:, 32:40].rearrange("p (t k) -> p t k", t=CT)
                w = s[:, 40:48].rearrange("p (t k) -> p t k", t=CT)
                dve.wait_ge(sums.sem, sums.at(b, 1))
                ch(nc.vector.tensor_reduce(s[:, 24:26], gm[:, :, :, 1], AX.X, ALU.add))
                ch(nc.vector.tensor_tensor(d, st[:, :, :, 1], s[:, 24:26, None].to_broadcast([P, CT, 4]), ALU.subtract))
                ch(nc.vector.tensor_tensor(w, d, d, ALU.mult))
                nc.vector.scalar_tensor_tensor(w, st[:, :, :, 2], 1.0 / 256, w, ALU.mult, ALU.add).then_inc(spread.sem, 1)

            def gn_var(b, s, pp, sums, var):
                dve.wait_ge(sums.sem, sums.at(b, 2))
                nc.vector.tensor_reduce(s[:, 50:52], pp[:, 32:40].rearrange("p (t k) -> p t k", t=CT), AX.X,
                                        ALU.add).then_inc(var.sem, 1)

            def gn_shift(b, s, rstd, shift):
                dve.wait_ge(rstd.sem, rstd.at(b, 1))
                nc.vector.scalar_tensor_tensor(s[:, 56:58], s[:, 24:26], -1.0, s[:, 54:56], ALU.mult, ALU.mult).then_inc(shift.sem, 1)

            def prep(j):
                dve.wait_ge(a_w16.sem, a_w16.at(j, 1))
                nc.vector.tensor_copy(chi[:, :, :], whi[:, :, :])
                nc.vector.tensor_copy(clo[:, :, :], wlo[:, :, :])
                nc.vector.tensor_copy(csc[:, :], wsc[:, :]).then_inc(c_w.sem, 1)
                for t in range(CT):
                    dve.wait_ge(a_hi.sem, a_hi.at(j, t + 1))
                    inner = pad[:, t, :, 3:3 + H, 3:3 + W]
                    nc.vector.tensor_tensor(inner[:, 1], img(xh[:, t, :], W), inner[:, 0], ALU.subtract).then_inc(a_pad.sem, 1)

            def a_max_(j):
                dve.wait_ge(a_keyb.sem, a_keyb.at(j, 1))
                nc.vector.tensor_reduce(sk[:, 0:1], ex[:, :], AX.X, ALU.max, negate=True).then_inc(a_max.sem, 1)

            def a_dg_(j):
                ch = ea_a
                dve.wait_ge(a_exp.sem, a_exp.at(j, 1))
                ch(nc.vector.reciprocal(sk[:, 2:3], sk[:, 1:2]))
                nc.vector.tensor_scalar(dg49[:, :], ident[0:K2, 0:K2], sk[:, 2:3], None, ALU.mult).then_inc(a_dg.sem, 1)

            def a_ktc_(j):
                dve.wait_ge(a_kt.sem, a_kt.at(j, 1))
                nc.vector.tensor_copy(kt[:, :, :], pm[:, 0:8 * K2].rearrange("p (n k) -> p n k", n=8)).then_inc(a_ktc.sem, 1)

            def a_fic_(j):
                dve.wait_ge(a_fi.sem, a_fi.at(j, 1))
                nc.vector.tensor_copy(fi[:, :, :], pm[:, HALF:HALF + 2 * K2].rearrange("p (t k) -> p t k", t=CT)).then_inc(a_fic.sem, 1)

            def a_f2c_(j):
                ch = ea_a
                dve.wait_ge(a_f2.sem, a_f2.at(j, 1))
                for t in range(CT):
                    ins = nc.vector.tensor_scalar(f2[:, t, :], pm[:, t * 64:t * 64 + K2], v_b0[:, t:t + 1], None, ALU.add)
                ch(ins)
                s = sa
                nc.vector.bn_stats(s[:, 60:66], f2[:, :, :].rearrange("p t k -> p (t k)")).then_inc(a_f2c.sem, 1)

            def a_spread_(j):
                ch, s = ea_a, sa
                st = s[:, 60:66].rearrange("p (k c) -> p k c", c=3)
                dve.wait_ge(a_sums.sem, a_sums.at(j, 3))
                ch(nc.vector.tensor_reduce(s[:, 66:67], pm[:, 128:134].rearrange("p (k c) -> p k c", c=3)[:, :, 1], AX.X, ALU.add))
                ch(nc.vector.tensor_scalar(s[:, 67:68], s[:, 66:67], 0.5, None, ALU.mult))
                ch(nc.vector.tensor_tensor(s[:, 68:70], st[:, :, 1], s[:, 67:68].to_broadcast([P, 2]), ALU.subtract))
                ch(nc.vector.scalar_tensor_tensor(s[:, 70:72], s[:, 68:70], 0.5, s[:, 68:70], ALU.mult, ALU.mult))
                nc.vector.scalar_tensor_tensor(s[:, 72:74], st[:, :, 2], 0.5 / K2, s[:, 70:72], ALU.mult, ALU.add).then_inc(a_spread.sem, 1)

            def a_var_(j):
                s = sa
                dve.wait_ge(a_sums.sem, a_sums.at(j, 4))
                nc.vector.tensor_reduce(s[:, 74:75], pm[:, 136:138], AX.X, ALU.add).then_inc(a_var.sem, 1)

            def a_f3_(j):
                ch, s = ea_a, sa
                dve.wait_ge(a_rstd.sem, a_rstd.at(j, 2))
                ch(nc.vector.tensor_scalar(f2[:, :, :], f2[:, :, :], s[:, 67:68], s[:, 76:77], ALU.subtract, ALU.mult))
                ch(nc.vector.tensor_tensor(f2[:, :, :], f2[:, :, :], lnw[:, :, :], ALU.mult))
                ch(nc.vector.tensor_tensor(f2[:, :, :], f2[:, :, :], lnb[:, :, :], ALU.add))
                nc.vector.tensor_scalar(f2[:, :, :], f2[:, :, :], 0.0, None, ALU.max).then_inc(a_f3.sem, 1)

            def a_w_(j):
                ch, s = ea_a, sa
                dve.wait_ge(a_wg.sem, a_wg.at(j, 1))
                for t in range(CT):
                    ins = nc.vector.tensor_scalar(wg[:, t, :], pm[:, 256 + t * 64:256 + t * 64 + K2], v_b1[:, t:t + 1], None, ALU.add)
                ch(ins)
                ch(nc.vector.tensor_reduce(s[:, 80:82], wg[:, :, :], AX.X, ALU.max, apply_absolute_value=True))
                ch(nc.vector.tensor_scalar(wsc[:, :], s[:, 80:82], 1e-30, None, ALU.max))
                ch(nc.vector.reciprocal(s[:, 82:84], wsc[:, :]))
                ch(nc.vector.tensor_tensor(wg[:, :, :], wg[:, :, :], s[:, 82:84, None].to_broadcast([P, CT, K2]), ALU.mult))
                ch(nc.vector.tensor_copy(whi[:, :, :], wg[:, :, :]))
                nc.vector.tensor_tensor(wlo[:, :, :], wg[:, :, :], whi[:, :, :], ALU.subtract).then_inc(a_w16.sem, 1)
                ch.end()

            def conv_add(j, t):
                dve.wait_ge(row_done.sem, row_done.at(j, KK * (t + 1)))
                if t == 0:
                    dve.wait_ge(a_copy.sem, a_copy.at(j, 1))
                nc.vector.scalar_tensor_tensor(xn[:, t, :], pconv[:, :], csc[:, t:t + 1], xn[:, t, :],
                                               ALU.mult, ALU.add).then_inc(conv_out.sem, 1)

            def b_s0(i):
                ea_b.start(dve, i)
                dve.wait_ge(conv_out.sem, conv_out.at(i, CT))
                stats(i, sg, xn, b_stats)
                nc.vector.tensor_copy(xc[:, :, :], xn[:, :, :]).then_inc(b_xc.sem, 1)

            def chunk_first(i, c):
                s, n, fc, st = CHUNKS[c]
                k = c % 2
                dve.wait_ge(ch_abs.sem, ch_abs.at(i, c + 1))
                nc.vector.tensor_scalar(delta[:, s:s + n], bank(pm, 1)[:, 0:n], v_dtb[:, st:st + 1], 0.0, ALU.add,
                                        ALU.max).then_inc(ch_pos.sem, 1)
                dve.wait_ge(ch_hi.sem, ch_hi.at(i, c + 1))
                if c >= 2:
                    dve.wait_ge(ch_lo.sem, ch_lo.at(i, c - 1))
                nc.vector.tensor_tensor(rest[:, k, 0:n], bank(pm, 0)[0:64, 0:n], bcs[0:64, s:s + n], ALU.subtract).then_inc(ch_rest.sem, 1)
                dve.wait_ge(ch_q.sem, ch_q.at(i, c + 1))
                if c >= 2:
                    dve.wait_ge(ch_delta.sem, ch_delta.at(i, c - 1))
                nc.vector.scalar_tensor_tensor(er[:, k, 0:n], qs[:, k, 0:n], 1.0, es[:, k, 0:n], ALU.subtract,
                                               ALU.subtract).then_inc(ch_err.sem, 1)

            def chunk_last(i, c):
                s, n, fc, st = CHUNKS[c]
                k = c % 2
                dve.wait_ge(ch_ln.sem, ch_ln.at(i, c + 1))
                nc.vector.tensor_tensor(er[:, k, 0:n], qs[:, k, 0:n], er[:, k, 0:n], ALU.subtract).then_inc(ch_sub.sem, 1)
                dve.wait_ge(ch_sub.sem, ch_sub.at(i, c + 1))
                nc.vector.tensor_tensor(er[:, k, 0:n], er[:, k, 0:n], es[:, k, 0:n], ALU.min).then_inc(ch_min.sem, 1)

            def silu_clip(i):
                dve.wait_ge(b_z.sem, b_z.at(i, 2))
                nc.vector.tensor_scalar(o1[:, :], o1[:, :], 1e18, None, ALU.min).then_inc(z_clip.sem, 1)

            def silu_end(i):
                dve.wait_ge(z_sig.sem, z_sig.at(i, 1))
                nc.vector.tensor_tensor(sz[:, :], sz[:, :], o1[:, :], ALU.mult).then_inc(b_sz.sem, 1)

            def inputs(i, k):
                lv, st, dd, n0, m = UNITS[k]
                ln, fc, sc, _ = LEVEL[lv]
                so = SB if dd == 1 else sc
                dve.wait_ge(u_b.sem, u_b.at(i, k + 1))
                if k in CHUNKS_OF:
                    dve.wait_ge(ch_u.sem, ch_u.at(i, CHUNKS_OF[k]))
                us = u[:, so:so + ln]
                if lv == 1:
                    o, i0, i1 = bx[:, k % 2, 0:ln], slot_b[:, :], us
                else:
                    o = b3[:, :, 0:ln] if lv == 3 else b2[:, k % 2, :, 0:ln]
                    i0 = slot_b[:, :].rearrange("p (m l) -> p m l", m=m)
                    i1 = us[:, None, :].to_broadcast([P, m, ln])
                nc.vector.tensor_tensor(o, i0, i1, ALU.mult).then_inc(u_bx.sem, 1)

            def scan(i, q):
                k, d = PRODUCTS[q]
                lv, m = UNITS[k][0], UNITS[k][4]
                ln = LEVEL[lv][0]
                n = ln if lv == 1 else m * (ln + 1)
                if lv == 1:
                    av, bv = ea[:, k % 2, 0:n], bx[:, k % 2, 0:n]
                elif lv == 2:
                    av, bv = (v[:, k % 2].rearrange("p m l -> p (m l)") for v in (a2, b2))
                else:
                    av, bv = (v[:, :, :].rearrange("p m l -> p (m l)") for v in (a3, b3))
                hv = h[:, q % HR, 0:n]
                if d:
                    av, bv, hv = av[:, ::-1], bv[:, ::-1], hv[:, ::-1]
                dve.wait_ge(u_ea.sem, u_ea.at(i, k + 1))
                dve.wait_ge(u_bx.sem, u_bx.at(i, k + 1))
                if k == 1:
                    dve.wait_ge(u_zero.sem, u_zero.at(i, 2))
                if q >= HR:
                    dve.wait_ge(q_y.sem, q_y.at(i, q - HR + 1))
                nc.vector.tensor_tensor_scan(hv, av, bv, 0.0, ALU.mult, ALU.add).then_inc(q_h.sem, 1)

            def weigh(i, q):
                k, d = PRODUCTS[q]
                lv, m = UNITS[k][0], UNITS[k][4]
                ln = LEVEL[lv][0]
                dve.wait_ge(u_c.sem, u_c.at(i, k + 1))
                dve.wait_ge(q_h.sem, q_h.at(i, q + 1))
                if lv == 1:
                    hv = h[:, q % HR, 0:ln]
                    nc.vector.tensor_tensor(hv, slot_c[:, :], hv, ALU.mult).then_inc(q_pr.sem, 1)
                    return
                hv = h[:, q % HR, 0:m * (ln + 1)].rearrange("p (m l) -> p m l", m=m)[:, :, 0:ln]
                nc.vector.tensor_tensor(hv, slot_c[:, :].rearrange("p (m l) -> p m l", m=m), hv, ALU.mult).then_inc(q_pr.sem, 1)

            def up_add(dst, src, side):
                dv = dst.rearrange("p (r s c) -> p r s c", s=2, c=2 * side)
                sv = src.rearrange("p (r c) -> p r c", c=side)
                rows = dv.shape[1]
                for s in range(2):
                    d = dv[:, :, s, :].rearrange("p r (c e) -> p r c e", e=2)
                    ins = nc.vector.tensor_tensor(d, d, sv[:, :, :, None].to_broadcast([P, rows, side, 2]), ALU.add)
                return ins

            def norm(i, k):
                d, c0, n = NORMS[k]
                cols = 2 * n if d == 2 else n
                seq = n_o

                def step(ins):
                    step.n += 1
                    ins.then_inc(seq.sem, 1)
                    dve.wait_ge(seq.sem, seq.at(i, step.n))
                step.n = STEPS[k]
                t_ = norm_sbuf(k)[1][:, 0:cols]
                dve.wait_ge(n_rs.sem, n_rs.at(i, k + 1))
                ins = nc.vector.tensor_tensor(t_, norm_psum(k)[0][:, 0:cols], norm_sbuf(k)[2][:, 0:cols], ALU.mult)
                ins.then_inc(n_t.sem, 1)
                dve.wait_ge(n_t.sem, n_t.at(i, k + 1))
                if k < 2:
                    o = (o3, o2)[k]
                    step(nc.vector.tensor_tensor(o[:, :], t_[:, 0:n], t_[:, n:2 * n], ALU.add))
                    p = 2 - k
                    step(nc.vector.tensor_scalar(o[:, :], o[:, :], v_g[:, p:p + 1], bes[:, p:p + 1], ALU.mult, ALU.add))
                    if k == 1:
                        step(up_add(o2[:, :], o3[:, :], 8))
                elif d == 0:
                    o = o1[:, c0:c0 + n]
                    step(nc.vector.tensor_scalar(o, t_, v_g[:, 0:1], bes[:, 0:1], ALU.mult, ALU.add))
                    hh = c0 // HALF
                    step(up_add(o, o2[:, hh * 128:hh * 128 + 128], 16))
                else:
                    o = o1[:, c0:c0 + n]
                    step(nc.vector.scalar_tensor_tensor(o, t_, v_g[:, 1:2], o, ALU.mult, ALU.add))
                    nc.vector.tensor_tensor(o, o, sz[:, c0:c0 + n], ALU.mult).then_inc(b_g.sem, 1)
                assert step.n == STEPS[k + 1]

            def b_end(i):
                norm(i, 3)
                norm(i, 4)
                norm(i, 5)
                dve.wait_ge(ob_free.sem, ob_free.at(i + 1, 0))
                for hh in range(2):
                    for t in range(CT):
                        k = 2 * hh + t
                        dve.wait_ge(b_out.sem, b_out.at(i, k + 1))
                        src = bank((slot_c, pm)[hh], t)
                        ins = nc.vector.scalar_tensor_tensor(ob[:, t, hh * HALF:(hh + 1) * HALF], src, v_out[:, t:t + 1],
                                                             xc[:, t, hh * HALF:(hh + 1) * HALF], ALU.add, ALU.add)
                ins.then_inc(ob_ready.sem, 1)

            def start(i, j):
                if i is not None:
                    b_s0(i)
                    gn_spread(ea_b, i, sg, slot_b, b_sums, b_spread)
                if j is not None:
                    prep(j)
                if i is not None:
                    gn_var(i, sg, slot_b, b_sums, b_var)
                    gn_shift(i, sg, b_rstd, b_shift)
                    ea_b.end()
                    for v in (a2, b2):
                        nc.vector.memset(v[:, :, :, L2], 0.0).then_inc(u_zero.sem, 1)
                    chunk_first(i, 0)
                    chunk_first(i, 1)
                    chunk_last(i, 0)
                    chunk_last(i, 1)
                    inputs(i, 0)

            pre = {3: a_s0, 5: lambda m: gn_spread(ea_a, m, sa, pm, a_sums, a_spread), 7: lambda m: gn_var(m, sa, pm, a_sums, a_var),
                   8: lambda m: gn_shift(m, sa, a_rstd, a_shift), 15: a_max_, 17: a_dg_, 19: a_ktc_, 21: a_fic_, 23: a_f2c_,
                   25: a_spread_, 27: a_var_, 28: a_f3_, 30: a_w_}

            def unit(i, j, m, k):
                if i is not None:
                    for n, q in enumerate(products_of(k)):
                        scan(i, q)
                        if n == 0 and k + 1 < NU:
                            inputs(i, k + 1)
                        weigh(i, q)
                    if k < 4:
                        chunk_first(i, k + 2)
                    if 1 <= k < 5:
                        chunk_last(i, k + 1)
                    if k == 6:
                        silu_clip(i)
                    if k == 7:
                        silu_end(i)
                    if k in NORM_DVE:
                        norm(i, NORM_DVE[k])
                if m is not None and k in pre:
                    pre[k](m)
                if j is not None and k == HALF_AT:
                    conv_add(j, 0)

            def end(i, j):
                if i is not None:
                    b_end(i)
                if j is not None:
                    conv_add(j, 1)

            stages(start, unit, end, dve)

        @block.tensor
        def _(pe):
            pe.wait_ge(consts_in, LOADED)
            for t in range(CT):
                nc.tensor.matmul(pm[:, t * P:(t + 1) * P], win[:, t * P:(t + 1) * P], wc1[:, :], start=True, stop=True)
            nc.tensor.matmul(pm[:, HALF:HALF + 1], wc1[:, :], v_inx, start=True, stop=True).then_inc(setup_pe, 1)
            for p in range(3):
                ins = nc.tensor.matmul(pconv[:, p * P:(p + 1) * P], wx8[:, p, :], wdt[:, p, :], start=True, stop=True)
            ins.then_inc(setup_pe, 1)
            pe.wait_ge(setup, DVE_SET + ACT_SET)

            def sums1(b, s, pp, sums, stats):
                pe.wait_ge(stats.sem, stats.at(b, 1))
                nc.tensor.matmul(pp[:, 0:24], grp[:, :], s[:, 0:24], start=True, stop=True).then_inc(sums.sem, 1)

            def sums2(b, s, pp, sums, spread):
                pe.wait_ge(spread.sem, spread.at(b, 1))
                nc.tensor.matmul(pp[:, 32:40], grp[:, :], s[:, 40:48], start=True, stop=True).then_inc(sums.sem, 1)

            def a_key_(j):
                for t in range(CT):
                    pe.wait_ge(a_xh.sem, a_xh.at(j, t + 1))
                    for k in range(2):
                        ins = nc.tensor.matmul(bank(pm, k)[0:K2], wk[:, t, :], bank(xh[:, t, :], k),
                                               start=(t == 0), stop=(t == CT - 1))
                ins.then_inc(a_key.sem, 1)

            def a_turn(j, g):
                if g < 2:
                    pe.wait_ge(a_keyb.sem, a_keyb.at(j, 1))
                else:
                    pe.wait_ge(a_xtc.sem, a_xtc.at(j, g - 1))
                for b in range(2):
                    for t in range(CT):
                        n = 2 * g + b
                        ins = nc.tensor.transpose(bank(pm, g % 2)[:, (2 * b + t) * P:(2 * b + t + 1) * P],
                                                  xh[:, t, n * P:(n + 1) * P], ident[:, :])
                ins.then_inc(a_xt.sem, 1)

            def a_kt_(j):
                pe.wait_ge(a_dg.sem, a_dg.at(j, 1))
                for n in range(8):
                    ins = nc.tensor.matmul(pm[:, n * K2:(n + 1) * K2], ex[:, n * P:(n + 1) * P], dg49[:, :], start=True, stop=True)
                ins.then_inc(a_kt.sem, 1)

            def a_fi_(j):
                pe.wait_ge(a_ktc.sem, a_ktc.at(j, 1))
                pe.wait_ge(a_xtc.sem, a_xtc.at(j, 4))
                for t in range(CT):
                    for n in range(8):
                        ins = nc.tensor.matmul(pm[:, HALF + t * K2:HALF + (t + 1) * K2], xt[:, n, t * P:(t + 1) * P], kt[:, n, :],
                                               start=(n == 0), stop=(n == 7))
                ins.then_inc(a_fi.sem, 1)

            def mix(w, src, o):
                for t in range(CT):
                    for k in range(CT):
                        ins = nc.tensor.matmul(pm[:, o + t * 64:o + t * 64 + K2], w[:, k, t * P:(t + 1) * P], src[:, k, :],
                                               start=(k == 0), stop=(k == CT - 1))
                return ins

            def a_f2_(j):
                pe.wait_ge(a_fic.sem, a_fic.at(j, 1))
                mix(w0, fi, 0).then_inc(a_f2.sem, 1)

            def a_sum3(j):
                pe.wait_ge(a_f2c.sem, a_f2c.at(j, 1))
                nc.tensor.matmul(pm[:, 128:134], ones[:, :], sa[:, 60:66], start=True, stop=True).then_inc(a_sums.sem, 1)

            def a_sum4(j):
                pe.wait_ge(a_spread.sem, a_spread.at(j, 2))
                nc.tensor.matmul(pm[:, 136:138], ones[:, :], sa[:, 72:74], start=True, stop=True).then_inc(a_sums.sem, 1)

            def a_wg_(j):
                pe.wait_ge(a_f3.sem, a_f3.at(j, 1))
                mix(w1, f2, 256).then_inc(a_wg.sem, 1)

            def taps(j, lo, hi):
                for n in range(lo, hi):
                    r, dx = divmod(n, KK)
                    t, dy = ROWS[r]
                    if dx == 0:
                        pe.wait_ge(diag_made.sem, diag_made.at(j, r + 1))
                        if dy == 0:
                            pe.wait_ge(a_pad.sem, a_pad.at(j, t + 1))
                        if dy == 0 and t > 0:
                            pe.wait_ge(conv_out.sem, conv_out.at(j, t))
                    first, last = dy == 0 and dx == 0, dy == KK - 1 and dx == KK - 1
                    dh, dl = diag[:, r % RING, 0, dx, :], diag[:, r % RING, 1, dx, :]
                    for m, (w, part) in enumerate(((dh, 0), (dh, 1), (dl, 0))):
                        for k in range(2):
                            rows = dy + 16 * k
                            ins = nc.tensor.matmul(bank(pconv, k), w, pad[:, t, part, rows:rows + 16, dx:dx + W],
                                                   start=first and m == 0, stop=last and m == 2)
                    if dx == KK - 1:
                        ins.then_inc(row_done.sem, 1)

            def project(i):
                for t in range(CT):
                    pe.wait_ge(b_xg.sem, b_xg.at(i, t + 1))
                    for k in range(2):
                        ins = nc.tensor.matmul(bank(slot_b, k), wf[:, t, :], bank(xg[:, t, :], k), start=(t == 0), stop=(t == CT - 1))
                ins.then_inc(b_proj.sem, 1)
                for t in range(CT):
                    for k in range(2):
                        ins = nc.tensor.matmul(bank(slot_c, k), wz[:, t, :], bank(xg[:, t, :], k), start=(t == 0), stop=(t == CT - 1))
                ins.then_inc(b_proj.sem, 1)

            def lower(i, lv):
                w, o, n, side = ((wc2, 0, L2, 16), (wc3, HALF, L3, 8))[lv]
                src = f[:, (0, L1)[lv]:(0, L1)[lv] + 4 * n].rearrange("p (r s c e) -> p r s c e", s=2, e=2, c=side)
                pe.wait_ge(b_f.sem, b_f.at(i, lv + 1))
                for m in range(4):
                    ins = nc.tensor.matmul(slot_b[:, o:o + n], w[:, m, :], src[:, :, m // 2, :, m % 2], start=(m == 0), stop=(m == 3))
                ins.then_inc(b_proj.sem, 1)

            def chunk(i, c):
                s, n, fc, st = CHUNKS[c]
                if c == 0:
                    pe.wait_ge(b_f.sem, b_f.at(i, 3))
                else:
                    pe.wait_ge(ch_rest.sem, ch_rest.at(i, c))
                    pe.wait_ge(ch_pos.sem, ch_pos.at(i, c))
                nc.tensor.matmul(bank(pm, 0)[0:96, 0:n], wbc[:, st, :], f[:, fc:fc + n], start=True, stop=True).then_inc(ch_bc.sem, 1)
                nc.tensor.matmul(bank(pm, 1)[:, 0:n], wdelta[:, st, :], f[:, fc:fc + n], start=True, stop=True).then_inc(ch_dt.sem, 1)

            def spread(i, k, slot, row0, done):
                lv, st, dd, n0, m = UNITS[k]
                ln, fc, sc, _ = LEVEL[lv]
                so = SB if dd == 1 else sc
                per = min(ln, HALF)
                for n in range(m):
                    for c in range(0, ln, per):
                        o = n * ln + c
                        ins = nc.tensor.matmul(slot[:, o:o + per], sel[:, row0 + n0 + n:row0 + n0 + n + 1].to_broadcast([96, P]), bcs[:, so + c:so + c + per],
                                               start=True, stop=True)
                ins.then_inc(done.sem, 1)

            def put_b(i, k):
                if k in CHUNKS_OF:
                    pe.wait_ge(ch_lo.sem, ch_lo.at(i, CHUNKS_OF[k]))
                if k:
                    pe.wait_ge(u_bx.sem, u_bx.at(i, k))
                spread(i, k, slot_b, 0, u_b)

            def put_c(i, k):
                if k:
                    pe.wait_ge(q_pr.sem, q_pr.at(i, products_of(k - 1)[-1] + 1))
                else:
                    pe.wait_ge(b_z.sem, b_z.at(i, 1))
                spread(i, k, slot_c, NS, u_c)

            def norm_centre(i, k):
                d, c0, n = NORMS[k]
                src = y[:, :, c0:c0 + n] if d == 2 else y[:, d, c0:c0 + n]
                cols = 2 * n if d == 2 else n
                if k == 0:
                    pe.wait_ge(y_init.sem, y_init.at(i, 5))
                elif k < 5:
                    pe.wait_ge(n_t.sem, n_t.at(i, k))
                pe.wait_ge(q_y.sem, q_y.at(i, NORM_NEEDS[k]))
                o = norm_psum(k)[0][:, 0:cols]
                if d == 2:
                    o = o.rearrange("p (d n) -> p d n", d=2)
                nc.tensor.matmul(o, cen[:, :], src, start=True, stop=True).then_inc(n_yc.sem, 1)

            def norm_spread(i, k):
                d, c0, n = NORMS[k]
                cols = 2 * n if d == 2 else n
                pe.wait_ge(n_sq.sem, n_sq.at(i, k + 1))
                nc.tensor.matmul(norm_psum(k)[1][:, 0:cols], ones[:, :], norm_sbuf(k)[0][:, 0:cols], start=True, stop=True).then_inc(n_var.sem, 1)

            def b_end(i):
                norm_centre(i, 4)
                norm_centre(i, 5)
                norm_spread(i, 4)
                norm_spread(i, 5)
                for hh in range(2):
                    pe.wait_ge(b_g.sem, b_g.at(i, hh + 1))
                    for t in range(CT):
                        nc.tensor.matmul(bank((slot_c, pm)[hh], t), wo[:, t * P:(t + 1) * P], o1[:, hh * HALF:(hh + 1) * HALF],
                                         start=True, stop=True).then_inc(b_out.sem, 1)

            def start(i, j):
                at = 0

                def some(n):
                    nonlocal at
                    if j is not None:
                        taps(j, at, n)
                    at = n
                if i is not None:
                    sums1(i, sg, slot_b, b_sums, b_stats)
                    sums2(i, sg, slot_b, b_sums, b_spread)
                some(5)
                if i is not None:
                    project(i)
                some(9)
                if i is not None:
                    lower(i, 0)
                some(11)
                if i is not None:
                    lower(i, 1)
                some(13)
                if i is not None:
                    chunk(i, 0)
                some(15)
                if i is not None:
                    chunk(i, 1)
                some(START_TAPS)
                if i is not None:
                    put_b(i, 0)
                    put_c(i, 0)

            pre = {4: lambda m: sums1(m, sa, pm, a_sums, a_stats), 5: lambda m: sums2(m, sa, pm, a_sums, a_spread),
                   13: a_key_, 14: lambda m: (a_turn(m, 0), a_turn(m, 1)), 15: lambda m: (a_turn(m, 2), a_turn(m, 3)),
                   17: a_kt_, 19: a_fi_, 21: a_f2_, 23: a_sum3, 25: a_sum4, 28: a_wg_}

            def unit(i, j, m, k):
                if i is not None:
                    if k == 0:
                        put_b(i, 1)
                    if k + 1 < NU:
                        put_c(i, k + 1)
                    if k + 2 < NU:
                        put_b(i, k + 2)
                if i is not None and k < 4:
                    chunk(i, k + 2)
                if j is not None:
                    taps(j, taps_at(k), taps_at(k + 1))
                if m is not None and k in pre:
                    if i is not None and k == 4:
                        pe.wait_ge(ch_pos.sem, ch_pos.at(i, NCH))
                        pe.wait_ge(ch_rest.sem, ch_rest.at(i, NCH))
                    if i is not None and k == 13:
                        pe.wait_ge(n_t.sem, n_t.at(i, 2))
                    pre[k](m)
                if i is not None and k in NORM_PE_YC:
                    if k == 7:
                        pe.wait_ge(ch_pos.sem, ch_pos.at(i, NCH))
                        pe.wait_ge(ch_rest.sem, ch_rest.at(i, NCH))
                        if m is not None:
                            pe.wait_ge(a_var.sem, a_var.at(m, 1))
                    if k == 31 and m is not None:
                        pe.wait_ge(a_w16.sem, a_w16.at(m, 1))
                    norm_centre(i, NORM_PE_YC[k])
                if i is not None and k in NORM_PE_VAR:
                    norm_spread(i, NORM_PE_VAR[k])

            stages(start, unit, lambda i, j: b_end(i) if i is not None else None, pe)

        @block.scalar
        def _(act):
            act.preload_act_table_set("natural_log_exp_and_others")
            act.wait_ge(consts_in, LOADED)
            nc.scalar.activation(nega[:, :, :], al[:, :, :], ACT.Exp).then_inc(setup, 1)
            act.wait_ge(setup_pe, 1)
            nc.scalar.activation(wf[:, :, :], pm[:, 0:C].rearrange("p (t m) -> p t m", t=CT), ACT.Copy).then_inc(setup, 1)
            nc.scalar.activation(bf1[:, :], pm[:, HALF:HALF + 1], ACT.Identity, bias=v_c1).then_inc(setup, 1)
            act.wait_ge(setup_pe, 2)
            nc.scalar.activation(wdelta[:, :, :], pconv[:, 0:3 * P].rearrange("p (t m) -> p t m", t=3), ACT.Copy).then_inc(setup, 1)
            act.wait_ge(setup, 5)
            act.wait_ge(setup, DVE_SET + 4)
            nc.scalar.mul(nega[:, :, :], nega[:, :, :], -1.0).then_inc(setup, 1)
            act.wait_ge(setup, DVE_SET + ACT_SET)

            def rsqrt(b, s, var, rstd, c, iv, io, n):
                act.wait_ge(var.sem, var.at(b, c))
                return (nc.scalar.activation(s[:, io - 2:io - 2 + n], s[:, iv:iv + n], ACT.Ln, bias=eps[:, 0:1]),
                        lambda: nc.scalar.activation(s[:, io:io + n], s[:, io - 2:io - 2 + n], ACT.Exp, scale=-0.5).then_inc(rstd.sem, 1))

            def a_rstd_(m):
                act_a.start(act, m)
                ins, fin = rsqrt(m, sa, a_var, a_rstd, 1, 50, 54, 2)
                act_a(ins)
                fin()

            def a_xh_(m):
                act.wait_ge(a_rstd.sem, a_rstd.at(m, 1))
                act.wait_ge(a_shift.sem, a_shift.at(m, 1))
                if not (isinstance(m, int) and m == 0):
                    act.wait_ge(a_pad.sem, a_pad.at(m, 0))
                for t in range(CT):
                    nc.scalar.activation(xh[:, t, :], xr[:, t, :], ACT.Identity, scale=sa[:, 54 + t:55 + t],
                                         bias=sa[:, 56 + t:57 + t]).then_inc(a_xh.sem, 1)

            def prep(j):
                if not (isinstance(j, int) and j == 0):
                    act.wait_ge(row_done.sem, row_done.at(j, 0))
                act.wait_ge(a_xh.sem, a_xh.at(j, CT))
                for t in range(CT):
                    nc.scalar.activation(pad[:, t, 0, 3:3 + H, 3:3 + W], img(xh[:, t, :], W), ACT.Copy).then_inc(a_hi.sem, 1)

            def copy_x(j):
                if not (isinstance(j, int) and j == 0):
                    act.wait_ge(b_xc.sem, b_xc.at(j, 0))
                    act.wait_ge(b_xg.sem, b_xg.at(j, 0))
                nc.scalar.activation(xn[:, :, :], xr[:, :, :], ACT.Copy).then_inc(a_copy.sem, 1)

            def a_keyb_(j):
                act.wait_ge(a_key.sem, a_key.at(j, 1))
                nc.scalar.activation(ex[:, :], pm[0:K2, :], ACT.Identity, bias=kb[:, 0:1]).then_inc(a_keyb.sem, 1)

            def a_xtc_(j, g):
                act.wait_ge(a_xt.sem, a_xt.at(j, g + 1))
                nc.scalar.activation(xt[:, 2 * g:2 * g + 2, :], bank(pm, g % 2).rearrange("p (n c) -> p n c", n=2),
                                     ACT.Copy).then_inc(a_xtc.sem, 1)

            def a_exp_(j):
                act.wait_ge(a_max.sem, a_max.at(j, 1))
                nc.scalar.activation(ex[:, :], ex[:, :], ACT.Exp, bias=sk[:, 0:1], accum_out=sk[:, 1:2]).then_inc(a_exp.sem, 1)

            def a_rstd2(j):
                ins, fin = rsqrt(j, sa, a_var, a_rstd, 2, 74, 78, 1)
                act_a(ins)
                nc.scalar.activation(sa[:, 76:77], sa[:, 76:77], ACT.Exp, scale=-0.5).then_inc(a_rstd.sem, 1)
                act_a.end()

            def b1(i):
                act_b.start(act, i)
                ins, fin = rsqrt(i, sg, b_var, b_rstd, 1, 50, 54, 2)
                act_b(ins)
                fin()
                act.wait_ge(b_rstd.sem, b_rstd.at(i, 1))
                act.wait_ge(b_shift.sem, b_shift.at(i, 1))
                for t in range(CT):
                    nc.scalar.activation(xg[:, t, :], xn[:, t, :], ACT.Identity, scale=sg[:, 54 + t:55 + t],
                                         bias=sg[:, 56 + t:57 + t]).then_inc(b_xg.sem, 1)
                act_b.end()

            def b2_(i):
                act.wait_ge(b_proj.sem, b_proj.at(i, 1))
                nc.scalar.activation(f[:, 0:L1], slot_b[:, :], ACT.Identity, bias=bf1[:, 0:1]).then_inc(b_f.sem, 1)
                act.wait_ge(b_proj.sem, b_proj.at(i, 3))
                nc.scalar.activation(f[:, L1:L1 + L2], slot_b[:, 0:L2], ACT.Identity, bias=v_c2).then_inc(b_f.sem, 1)
                nc.scalar.activation(sz[:, :], slot_c[:, :], ACT.Identity, bias=v_inz).then_inc(b_z.sem, 1)
                act.wait_ge(b_proj.sem, b_proj.at(i, 4))
                nc.scalar.activation(f[:, L1 + L2:LF], slot_b[:, HALF:HALF + L3], ACT.Identity, bias=v_c3).then_inc(b_f.sem, 1)

            def chunk_exp(i, c):
                s, n, fc, st = CHUNKS[c]
                k = c % 2
                act.wait_ge(ch_bc.sem, ch_bc.at(i, c + 1))
                nc.scalar.activation(bcs[:, s:s + n], bank(pm, 0)[0:96, 0:n], ACT.Copy).then_inc(ch_hi.sem, 1)
                act.wait_ge(ch_dt.sem, ch_dt.at(i, c + 1))
                if c >= 2:
                    act.wait_ge(ch_min.sem, ch_min.at(i, c - 1))
                nc.scalar.activation(es[:, k, 0:n], bank(pm, 1)[:, 0:n], ACT.Abs, bias=v_dtb[:, st:st + 1]).then_inc(ch_abs.sem, 1)
                act.wait_ge(ch_abs.sem, ch_abs.at(i, c + 1))
                nc.scalar.activation(es[:, k, 0:n], es[:, k, 0:n], ACT.Exp, scale=-1.0).then_inc(ch_exp.sem, 1)
                act.wait_ge(ch_exp.sem, ch_exp.at(i, c + 1))
                nc.scalar.activation(qs[:, k, 0:n], es[:, k, 0:n], ACT.Identity, bias=1.0).then_inc(ch_q.sem, 1)

            def chunk_log(i, c):
                s, n, _, _ = CHUNKS[c]
                k = c % 2
                act.wait_ge(ch_rest.sem, ch_rest.at(i, c + 1))
                nc.scalar.activation(bcs[0:64, s:s + n], rest[:, k, 0:n], ACT.Copy).then_inc(ch_mid.sem, 1)
                act.wait_ge(ch_err.sem, ch_err.at(i, c + 1))
                nc.scalar.activation(qs[:, k, 0:n], qs[:, k, 0:n], ACT.Ln).then_inc(ch_ln.sem, 1)

            def silu_exp(i):
                act.wait_ge(b_z.sem, b_z.at(i, 1))
                nc.scalar.activation(o1[:, :], sz[:, :], ACT.Exp, scale=-1.0).then_inc(b_z.sem, 1)

            def silu_end(i):
                act.wait_ge(z_clip.sem, z_clip.at(i, 1))
                nc.scalar.activation(o1[:, :], o1[:, :], ACT.Ln, bias=1.0).then_inc(z_ln.sem, 1)
                act.wait_ge(z_ln.sem, z_ln.at(i, 1))
                nc.scalar.activation(o1[:, :], o1[:, :], ACT.Exp, scale=-1.0).then_inc(z_sig.sem, 1)

            def y_start(i):
                for d, o, n, p in ((0, 0, L1, 0), (0, L1, L2, 1), (0, L1 + L2, L3, 2), (1, 0, L1 + L2, 1), (1, L1 + L2, L3, 2)):
                    nc.scalar.activation(y[:, d, o:o + n], f[:, o:o + n], ACT.Copy, scale=v_dv[:, p:p + 1]).then_inc(y_init.sem, 1)

            def decay(i, k):
                lv, st, dd, n0, m = UNITS[k]
                ln, fc, sc, _ = LEVEL[lv]
                so = SB if dd == 1 else sc
                if k in CHUNKS_OF:
                    act.wait_ge(ch_delta.sem, ch_delta.at(i, CHUNKS_OF[k]))
                if k >= 2:
                    act.wait_ge(q_h.sem, q_h.at(i, products_of(k - 2)[-1] + 1))
                for n in range(m):
                    o = ea[:, k % 2, 0:ln] if lv == 1 else a3[:, n, 0:ln] if lv == 3 else a2[:, k % 2, n, 0:ln]
                    ins = nc.scalar.activation(o, delta[:, so:so + ln], ACT.Exp, scale=nega[:, st, n0 + n:n0 + n + 1])
                ins.then_inc(u_ea.sem, 1)

            def norm_square(i, k):
                d, c0, n = NORMS[k]
                cols = 2 * n if d == 2 else n
                act.wait_ge(n_yc.sem, n_yc.at(i, k + 1))
                if k == 0:
                    act.wait_ge(ch_min.sem, ch_min.at(i, NCH))
                nc.scalar.activation(norm_sbuf(k)[0][:, 0:cols], norm_psum(k)[0][:, 0:cols], ACT.Square).then_inc(n_sq.sem, 1)

            def norm_root(i, k):
                d, c0, n = NORMS[k]
                cols = 2 * n if d == 2 else n
                _, ln_, rt = norm_sbuf(k)
                act.wait_ge(n_var.sem, n_var.at(i, k + 1))
                if k == 0:
                    act.wait_ge(ch_delta.sem, ch_delta.at(i, NCH))
                elif k < 5:
                    act.wait_ge(n_o.sem, n_o.at(i, STEPS[k]))
                nc.scalar.activation(ln_[:, 0:cols], norm_psum(k)[1][:, 0:cols], ACT.Ln, bias=eps[:, 0:1]).then_inc(n_ln.sem, 1)
                act.wait_ge(n_ln.sem, n_ln.at(i, k + 1))
                nc.scalar.activation(rt[:, 0:cols], ln_[:, 0:cols], ACT.Exp, scale=-0.5).then_inc(n_rs.sem, 1)

            def start(i, j):
                if j is not None:
                    prep(j)
                if i is not None:
                    b1(i)
                if j is not None:
                    copy_x(j)
                if i is not None:
                    b2_(i)
                    chunk_exp(i, 0)
                    chunk_exp(i, 1)
                    chunk_log(i, 0)
                    chunk_log(i, 1)
                    y_start(i)
                    decay(i, 0)
                    decay(i, 1)

            pre = {7: a_rstd_, 8: a_xh_, 14: a_keyb_, 15: lambda m: (a_xtc_(m, 0), a_xtc_(m, 1)), 17: a_exp_,
                   16: lambda m: (a_xtc_(m, 2), a_xtc_(m, 3)), 27: a_rstd2}

            def unit(i, j, m, k):
                if i is not None:
                    if k < 4:
                        chunk_exp(i, k + 2)
                        chunk_log(i, k + 2)
                    if k + 2 < NU:
                        decay(i, k + 2)
                    if k == 5:
                        silu_exp(i)
                    if k == 6:
                        silu_end(i)
                    if k in NORM_ACT_SQ:
                        norm_square(i, NORM_ACT_SQ[k])
                    if k in NORM_ACT_RT:
                        norm_root(i, NORM_ACT_RT[k])
                if m is not None and k in pre:
                    pre[k](m)

            def b_end(i):
                norm_square(i, 4)
                norm_square(i, 5)
                norm_root(i, 4)
                norm_root(i, 5)

            stages(start, unit, lambda i, j: b_end(i) if i is not None else None, act)

        @block.gpsimd
        def _(pool):
            pool.wait_ge(setup, DVE_SET + ACT_SET)

            def chunk_low(i, c):
                s, n, fc, _ = CHUNKS[c]
                pool.wait_ge(ch_mid.sem, ch_mid.at(i, c + 1))
                pool.tensor_tensor(bcs[0:32, s:s + n], rest[0:32, c % 2, 0:n], bcs[0:32, s:s + n], ALU.subtract).then_inc(ch_lo.sem, 1)
                pool.wait_ge(ch_min.sem, ch_min.at(i, c + 1))
                pool.tensor_tensor(delta[:, s:s + n], delta[:, s:s + n], er[:, c % 2, 0:n], ALU.add).then_inc(ch_delta.sem, 1)
                pool.wait_ge(ch_delta.sem, ch_delta.at(i, c + 1))
                pool.tensor_tensor(u[:, s:s + n], delta[:, s:s + n], f[:, fc:fc + n], ALU.mult).then_inc(ch_u.sem, 1)

            def make_row(j, r):
                t, dy = ROWS[r]
                if r >= RING:
                    pool.wait_ge(row_done.sem, row_done.at(j, r - RING + 1))
                elif not (isinstance(j, int) and j == 0):
                    pool.wait_ge(row_done.sem, row_done.at(j, 0))
                for m, w in enumerate((chi, clo)):
                    ins = pool.tensor_tensor(diag[:, r % RING, m, :, :], id16[:, None, :].to_broadcast([P, KK, P]),
                                             w[:, t, dy * KK:(dy + 1) * KK, None].to_broadcast([P, KK, P]), ALU.mult)
                ins.then_inc(diag_made.sem, 1)

            def gather(i, q):
                k, d = PRODUCTS[q]
                lv, m = UNITS[k][0], UNITS[k][4]
                ln, fc, _, _ = LEVEL[lv]
                yv = y[:, d, fc:fc + ln]
                if q == 0:
                    pool.wait_ge(y_init.sem, y_init.at(i, 5))
                pool.wait_ge(q_pr.sem, q_pr.at(i, q + 1))
                src = h[:, q % HR, 0:ln]
                if m > 1:
                    src = h[:, q % HR, 0:m * (ln + 1)].rearrange("p (m l) -> p m l", m=m)[:, :, 0:ln]
                while m > 1:
                    m //= 2
                    pool.tensor_tensor(src[:, 0:m], src[:, 0:m], src[:, m:2 * m], ALU.add).then_inc(n_y.sem, 1)
                    gather.n += 1
                    pool.wait_ge(n_y.sem, n_y.at(i, gather.n))
                if q:
                    pool.wait_ge(q_y.sem, q_y.at(i, q))
                pool.tensor_tensor(yv, yv, src[:, 0] if len(src.shape) == 3 else src, ALU.add).then_inc(q_y.sem, 1)

            def start(i, j):
                gather.n = 0
                if j is not None:
                    pool.wait_ge(c_w.sem, c_w.at(j, 1))
                    for r in range(RING):
                        make_row(j, r)
                if i is not None:
                    chunk_low(i, 0)
                    chunk_low(i, 1)

            def unit(i, j, m, k):
                if j is not None:
                    for r in range(RING, NR):
                        if row_unit(r) == k:
                            make_row(j, r)
                if i is not None:
                    for q in products_of(k):
                        gather(i, q)
                    if 1 <= k < 5:
                        chunk_low(i, k + 1)
                    if k == NU - 1:
                        assert gather.n == n_y.per

            stages(start, unit, None, pool)


TAPS = CT * K2
START_TAPS = 17


def taps_at(n):
    return START_TAPS + (TAPS - START_TAPS) * n // NU


HALF_AT = next(k for k in range(NU) if taps_at(k + 1) > K2)


def row_unit(r):
    return next(k for k in range(NU) if taps_at(k) >= KK * (r - RING + 1) + 2)


CHUNKS_OF = {0: 1, 1: 2, 5: 4, 21: 6}
NORM_PE_YC = {7: 0, 10: 1, 31: 2, 34: 3}
NORM_PE_VAR = {8: 0, 11: 1, 32: 2, 35: 3}
NORM_ACT_SQ = {8: 0, 11: 1, 32: 2, 35: 3}
NORM_ACT_RT = {9: 0, 12: 1, 33: 2, 36: 3}
NORM_DVE = {10: 0, 13: 1, 34: 2}
NORM_NEEDS = {0: 2, 1: 10, 2: 26, 3: 26, 4: 42, 5: 42}
STEPS = [0, 2, 5, 7, 9, 10, 11]


def stages(start, unit, end, eng):
    def body(i, j, m):
        start(i, j)
        for k in range(NU):
            unit(i, j, m, k)
        if end is not None:
            end(i, j)
    body(None, None, 0)
    body(None, 0, 1)
    with eng.Fori(0, B - 2) as i:
        body(i, i + 1, i + 2)
    body(B - 2, B - 1, None)
    body(B - 1, None, None)


def kernel(**inputs):
    import numpy as np
    import concourse.bacc as bacc
    from concourse.bass_utils import run_bass_kernel_spmd as run

    A = {n: np.asarray(v) for n, v in inputs.items()}
    g0 = lambda n: A["L0_conv_" + n]
    g1 = lambda n: A["L1_conv_" + n]

    def tiles(w):
        return w.reshape(CT, P, -1).transpose(1, 0, 2)

    eye = np.eye(P, dtype=np.float32)
    sel = np.concatenate([np.eye(32, dtype=np.float32)] * 3)
    arrays = {
        "x": A["x"],
        "c_ident": eye,
        "c_cen": eye - np.float32(1.0 / D),
        "c_ones": np.full((P, P), 1.0 / D, np.float32),
        "c_grp": np.kron(np.eye(P // GROUP), np.full((GROUP, GROUP), 1.0 / (4 * GROUP))).astype(np.float32),
        "c_sel": sel,
        "wk": tiles(g0("K_w").T),
        "w0": tiles(g0("conv0_w").T),
        "w1": tiles(g0("conv1_w").T),
        "win": g1("in_w")[:P],
        "wz": tiles(g1("in_w")[P:].T),
        "wc1": g1("c1_w").T,
        "wc2": g1("c2_w").reshape(P, P, 4).transpose(1, 2, 0),
        "wc3": g1("c3_w").reshape(P, P, 4).transpose(1, 2, 0),
        "wo": g1("out_w").T,
        "wx8": np.stack([g1(f"xw{s}")[:R_DT] for s in (1, 2, 3)], 1),
        "wdt": np.stack([g1(f"dtw{s}").T for s in (1, 2, 3)], 1),
        "wbc": np.stack([np.concatenate([g1(f"xw{s}")[R_DT:].T] * 3, 1) for s in (1, 2, 3)], 1),
        "vec": np.stack([g1("in_b")[:P], g1("in_b")[P:], g1("c1_b"), g1("c2_b"), g1("c3_b"),
                         *g1("out_b").reshape(CT, P), *g0("conv0_b").reshape(CT, P), *g0("conv1_b").reshape(CT, P),
                         *[g1(f"{n}{s}") for n in ("dtb", "Dv", "g", "be") for s in (1, 2, 3)]], 1),
        "kb": g0("K_b")[:, None],
        "lnw": tiles(g0("ln_w").reshape(C, K2)),
        "lnb": tiles(g0("ln_b").reshape(C, K2)),
        "al": np.stack([g1(f"Al{s}") for s in (1, 2, 3)], 1),
    }
    arrays = {n: np.ascontiguousarray(v) for n, v in arrays.items()}
    nc = bacc.Bacc("TRN2", target_bir_lowering=False, num_devices=1)
    aps = {n: nc.dram_tensor("in_" + n, v.shape, mybir.dt.from_np(v.dtype), kind="ExternalInput").ap() for n, v in arrays.items()}
    out = nc.dram_tensor("out_0", A["x"].shape, F32, kind="ExternalOutput").ap()
    build(nc, aps, out)
    r = run(nc, [{"in_" + n: v for n, v in arrays.items()}], core_ids=[0])
    return r.results[0]["out_0"]
```

```python
from contextlib import ExitStack

import concourse.bass as bass
from concourse import mybir

ALU = mybir.AluOpType
ACT = mybir.ActivationFunctionType
AX = mybir.AxisListType
F32 = mybir.dt.float32
F16 = mybir.dt.float16
BF16 = mybir.dt.bfloat16

P = 128
B, C, H, W = 16, 256, 32, 32
HW = H * W
CT = C // P
KK = 7
K2 = KK * KK
PADW = W + KK - 1
D = 128
NS = 16
R_DT = 8
L1, L2, L3 = HW, HW // 4, HW // 16
LF = L1 + L2 + L3
HALF = 512
GROUP = C // 32
SA, SB, SC, SD = 0, L1, 2 * L1, 2 * L1 + L2
LS = 2 * L1 + L2 + L3
CHUNKS = [(SD, L3, L1 + L2, 2), (SC, L2, L1, 1),
          (SA, HALF, 0, 0), (SA + HALF, HALF, HALF, 0), (SB, HALF, 0, 1), (SB + HALF, HALF, HALF, 1)]
NCH = len(CHUNKS)
UNITS = [(3, 2, 2, 0, NS)] + [(2, 1, 2, n, 4) for n in range(0, NS, 4)] + \
        [(1, 0, 0, n, 1) for n in range(NS)] + [(1, 1, 1, n, 1) for n in range(NS)]
NU = len(UNITS)
PRODUCTS = [(u, d) for u, (_, _, dd, _, _) in enumerate(UNITS) for d in ((0, 1) if dd == 2 else (dd,))]
NP = len(PRODUCTS)
LEVEL = {1: (L1, 0, SA, 1), 2: (L2, L1, SC, 4), 3: (L3, L1 + L2, SD, NS)}
BUF = NS * (L3 + 1)
MIDDLE = KK // 2
ROWS = [(t, r) for t in range(CT) for r in range(KK) if r != MIDDLE]
NR = len(ROWS)
MID_TAPS = [(dx, t) for dx in sorted(range(KK), key=lambda d: abs(d - MIDDLE)) for t in range(CT)]
HR = 3
RING = 4
EPS = 1e-5
NORMS = [(2, L1 + L2, L3), (2, L1, L2), (0, 0, HALF), (0, HALF, HALF), (1, 0, HALF), (1, HALF, HALF)]
NN = len(NORMS)

CONSTS = ["ident", "cen", "ones", "grp"]


def products_of(u):
    return [q for q, (v, _) in enumerate(PRODUCTS) if v == u]


def build(nc, a, out):
    with ExitStack() as ctx:
        def sb(name, shape, dt=F32):
            return ctx.enter_context(nc.sbuf_tensor(name, shape, dt))

        def ps(name, shape, dt=F32):
            return ctx.enter_context(nc.psum_tensor(name, shape, dt))

        def sem(name):
            return ctx.enter_context(nc.semaphore(name))

        class Count:

            def __init__(self, name, per):
                self.sem, self.per = sem(name), per

            def at(self, b, c):
                return b * self.per + c

        class Chain:

            def __init__(self, name, per):
                self.count, self.per = Count(name, per), per

            def start(self, eng, b):
                self.eng, self.b, self.n = eng, b, 0

            def __call__(self, ins):
                self.n += 1
                ins.then_inc(self.count.sem, 1)
                self.eng.wait_ge(self.count.sem, self.count.at(self.b, self.n))

            def end(self):
                assert self.n == self.per, (self.n, self.per)

        mats = {n: sb(n, [P, P]) for n in CONSTS}
        ident, cen, ones, grp = (mats[n] for n in CONSTS)
        id16 = sb("id16", [P, P], F16)
        sel = sb("sel", [96, 32], BF16)
        sel32 = sb("sel32", [96, 32])
        wk = sb("wk", [P, CT, K2])
        w0 = sb("w0", [P, CT, C])
        w1 = sb("w1", [P, CT, C])
        win = sb("win", [P, C])
        wz = sb("wz", [P, CT, P])
        wc1 = sb("wc1", [P, P])
        wf = sb("wf", [P, CT, P])
        wc2 = sb("wc2", [P, 4, P])
        wc3 = sb("wc3", [P, 4, P])
        wo = sb("wo", [P, C])
        wx8 = sb("wx8", [R_DT, 3, P])
        wdt = sb("wdt", [R_DT, 3, P])
        wdelta = sb("wdelta", [P, 3, P])
        wbc = sb("wbc", [P, 3, 96])
        vec = sb("vec", [P, 32])
        kb = sb("kb", [K2, 1])
        lnw = sb("lnw", [P, CT, K2])
        lnb = sb("lnb", [P, CT, K2])
        al = sb("al", [P, 3, NS])
        nega = sb("nega", [P, 3, NS])
        bf1 = sb("bf1", [P, 1])
        eps = sb("eps", [P, 1])
        bes = sb("bes", [P, 3])
        v_inx, v_inz, v_c1, v_c2, v_c3 = (vec[:, i:i + 1] for i in range(5))
        v_out, v_b0, v_b1 = (vec[:, i:i + 2] for i in (5, 7, 9))
        v_dtb, v_dv, v_g, v_be = (vec[:, i:i + 3] for i in (11, 14, 17, 20))

        xr = sb("xr", [P, CT, HW])
        xh = sb("xh", [P, CT, HW])
        pad = sb("pad", [P, CT, 2, PADW, PADW], F16)
        ex = sb("ex", [K2, HW])
        kt = sb("kt", [P, HW // P, K2])
        dg49 = sb("dg49", [K2, K2])
        fi = sb("fi", [P, CT, K2])
        f2 = sb("f2", [P, CT, K2])
        wg = sb("wg", [P, CT, K2])
        whi = sb("whi", [P, CT, K2], F16)
        wmid = sb("wmid", [P, CT, KK])
        wlo = sb("wlo", [P, CT, K2], F16)
        wsc = sb("wsc", [P, CT])
        chi = sb("chi", [P, CT, K2], F16)
        clo = sb("clo", [P, CT, K2], F16)
        csc = sb("csc", [P, CT])
        diag = sb("diag", [P, RING, 2, KK, P], F16)
        sa = sb("sa", [P, 128])
        sk = sb("sk", [K2, 4])

        xn = sb("xn", [P, CT, HW])
        xc = sb("xc", [P, CT, HW])
        xg = sb("xg", [P, CT, HW])
        xt = xg[:, :, :].rearrange("p t (n c) -> p (t n) c", c=C)
        f = sb("f", [P, LF])
        sz = sb("sz", [P, HW])
        bcs = sb("bcs", [96, LS], BF16)
        rest = sb("rest", [64, 2, HALF])
        delta = sb("delta", [P, LS])
        u = sb("u", [P, LS])
        xm = u[:, 0:CT * HW].rearrange("p (t n) -> p t n", t=CT)
        y = sb("y", [P, 2, LF])
        work = sb("work", [P, 4 + HR, BUF])
        ea, bx, h = work[:, 0:2, :], work[:, 2:4, :], work[:, 4:4 + HR, :]
        es, qs, rs = (sb(n, [P, 2, HALF]) for n in ("es", "qs", "rs"))
        er = rs
        a3, b3 = sb("a3", [P, NS, L3 + 1]), sb("b3", [P, NS, L3 + 1])
        a2, b2 = (v[:, :, 0:4 * (L2 + 1)].rearrange("p a (m l) -> p a m l", m=4) for v in (ea, bx))
        sq = es
        o3 = sb("o3", [P, L3])
        o2 = sb("o2", [P, L2])
        o1 = sb("o1", [P, HW])
        ob = sb("ob", [P, CT, HW])
        token = sb("token", [P, 1])
        sg = sb("sg", [P, 128])
        slot_b = ps("slot_b", [P, HW])
        slot_c = ps("slot_c", [P, HW])
        pconv = ps("pconv", [P, HW])
        pm = ps("pm", [P, HW])

        consts_in = sem("consts_in")
        setup_pe = sem("setup_pe")
        setup = sem("setup")
        x_in = Count("x_in", 16)
        ob_free = Count("ob_free", 16)
        ob_ready = Count("ob_ready", 1)
        ea_a, ea_b = Chain("dve_a", 19), Chain("dve_b", 3)
        act_a, act_b = Chain("act_a", 2), Chain("act_b", 1)
        a_stats = Count("a_stats", 1)
        a_sums = Count("a_sums", 4)
        a_spread = Count("a_spread", 2)
        a_var = Count("a_var", 2)
        a_rstd = Count("a_rstd", 2)
        a_shift = Count("a_shift", 1)
        a_xh = Count("a_xh", CT)
        a_hi = Count("a_hi", CT)
        a_pad = Count("a_pad", CT)
        a_key = Count("a_key", 1)
        a_keyb = Count("a_keyb", 1)
        a_max = Count("a_max", 1)
        a_exp = Count("a_exp", 1)
        a_dg = Count("a_dg", 1)
        a_xt = Count("a_xt", 4)
        a_xtc = Count("a_xtc", 4)
        a_kt = Count("a_kt", 1)
        a_ktc = Count("a_ktc", 1)
        a_fi = Count("a_fi", 1)
        a_fic = Count("a_fic", 1)
        a_f2 = Count("a_f2", 1)
        a_f2c = Count("a_f2c", 1)
        a_f3 = Count("a_f3", 1)
        a_wg = Count("a_wg", 1)
        a_w16 = Count("a_w16", 1)
        c_w = Count("c_w", 1)
        mid_tap = Count("mid_tap", len(MID_TAPS))
        a_copy = Count("a_copy", 1)
        diag_made = Count("diag_made", NR)
        row_done = Count("row_done", NR)
        conv_out = Count("conv_out", CT)
        b_stats = Count("b_stats", 1)
        b_sums = Count("b_sums", 2)
        b_spread = Count("b_spread", 1)
        b_var = Count("b_var", 1)
        b_rstd = Count("b_rstd", 1)
        b_shift = Count("b_shift", 1)
        b_xg = Count("b_xg", CT)
        b_xc = Count("b_xc", 1)
        b_proj = Count("b_proj", 4)
        b_f = Count("b_f", 3)
        b_z = Count("b_z", 2)
        out_half = Count("out_half", 1)
        b_sz = Count("b_sz", 1)
        ch_bc = Count("ch_bc", NCH)
        ch_dt = Count("ch_dt", NCH)
        ch_hi = Count("ch_hi", NCH)
        ch_abs = Count("ch_abs", NCH)
        ch_exp = Count("ch_exp", NCH)
        ch_q = Count("ch_q", NCH)
        ch_pos = Count("ch_pos", NCH)
        ch_rest = Count("ch_rest", NCH)
        ch_err = Count("ch_err", NCH)
        ch_ln = Count("ch_ln", NCH)
        ch_mid = Count("ch_mid", NCH)
        ch_sub = Count("ch_sub", NCH)
        ch_min = Count("ch_min", NCH)
        ch_lo = Count("ch_lo", NCH)
        ch_delta = Count("ch_delta", NCH)
        ch_u = Count("ch_u", NCH)
        y_init = Count("y_init", 5)
        u_b = Count("u_b", NU)
        u_c = Count("u_c", NU)
        u_ea = Count("u_ea", NU)
        u_bx = Count("u_bx", NU)
        u_zero = Count("u_zero", 2)
        z_clip = Count("z_clip", 1)
        z_ln = Count("z_ln", 1)
        z_sig = Count("z_sig", 1)
        q_h = Count("q_h", NP)
        q_pr = Count("q_pr", NP)
        q_y = Count("q_y", NP)
        n_y = Count("n_y", 24)
        n_yc = Count("n_yc", NN)
        n_sq = Count("n_sq", NN)
        n_var = Count("n_var", NN)
        n_ln = Count("n_ln", NN)
        n_rs = Count("n_rs", NN)
        n_t = Count("n_t", NN)
        n_o = Count("n_o", STEPS[-1])
        b_g = Count("b_g", 2)
        b_out = Count("b_out", 4)

        xv = a["x"].rearrange("b (t p) h w -> b p t (h w)", p=P)
        ov = out.rearrange("b (t p) h w -> b p t (h w)", p=P)
        block = ctx.enter_context(nc.Block())

        loads = [(mats[n][:, :], a["c_" + n]) for n in CONSTS] + [
            (sel32[:, :], a["c_sel"]),
            (wk[:, :, :], a["wk"]), (w0[:, :, :], a["w0"]), (w1[:, :, :], a["w1"]), (win[:, :], a["win"]),
            (wz[:, :, :], a["wz"]), (wc1[:, :], a["wc1"]), (wc2[:, :, :], a["wc2"]), (wc3[:, :, :], a["wc3"]),
            (wo[:, :], a["wo"]), (wx8[:, :, :], a["wx8"]), (wdt[:, :, :], a["wdt"]), (wbc[:, :, :], a["wbc"]),
            (vec[:, 0:23], a["vec"]), (kb[:, :], a["kb"]), (lnw[:, :, :], a["lnw"]), (lnb[:, :, :], a["lnb"]),
            (al[:, :, :], a["al"])]
        LOADED = 16 * len(loads)
        DVE_SET, ACT_SET = 7, 5

        def bank(t, k):
            return t[:, k * HALF:(k + 1) * HALF]

        def norm_psum(k):
            t = {4: slot_b, 5: slot_c}.get(k, pm)
            return bank(t, 0), bank(t, 1)

        def norm_sbuf(k):
            if k < 4:
                return es[:, 0], rs[:, 0], rs[:, 1]
            if k == 4:
                return bank(delta, 0), bank(delta, 1), bank(delta, 2)
            return bank(delta, 3), bank(h[:, 0], 0), bank(h[:, 0], 1)

        def img(ap, side):
            return ap.rearrange("p (r c) -> p r c", c=side)

        @block.sync
        def _(sp):
            for dst, src in loads:
                sp.dma_start(dst, src).then_inc(consts_in, 16)
            sp.dma_start(token[0:K2, :], a["kb"]).then_inc(ob_free.sem, 16)
            sp.dma_start(xr[:, :, :], xv[0]).then_inc(x_in.sem, 16)
            sp.wait_ge(a_copy.sem, a_copy.at(1, 0))
            sp.dma_start(xr[:, :, :], xv[1]).then_inc(x_in.sem, 16)
            with sp.Fori(0, B - 2) as i:
                sp.wait_ge(a_copy.sem, a_copy.at(i + 2, 0))
                sp.dma_start(xr[:, :, :], xv[i + 2]).then_inc(x_in.sem, 16)
                sp.wait_ge(ob_ready.sem, ob_ready.at(i + 1, 0))
                sp.dma_start(ov[i], ob[:, :, :]).then_inc(ob_free.sem, 16)
            for i in range(B - 2, B):
                sp.wait_ge(ob_ready.sem, ob_ready.at(i + 1, 0))
                sp.dma_start(ov[i], ob[:, :, :]).then_inc(ob_free.sem, 16)
            sp.wait_ge(ob_free.sem, ob_free.at(B + 1, 0))

        @block.vector
        def _(dve):
            for ins in (nc.vector.memset(eps[:, :], EPS), nc.vector.memset(pad[:, :, :, :, :], 0.0),
                        nc.vector.memset(a3[:, :, :], 0.0), nc.vector.memset(b3[:, :, :], 0.0)):
                ins.then_inc(setup, 1)
            dve.wait_ge(consts_in, LOADED)
            nc.vector.tensor_copy(id16[:, :], ident[:, :]).then_inc(setup, 1)
            nc.vector.tensor_copy(sel[:, :], sel32[:, :]).then_inc(setup, 1)
            nc.vector.scalar_tensor_tensor(bes[:, 0:1], v_be[:, 0:1], 0.0, v_be[:, 1:2], ALU.add, ALU.add)
            nc.vector.tensor_scalar(bes[:, 1:3], v_be[:, 1:3], 2.0, None, ALU.mult).then_inc(setup, 1)
            dve.wait_ge(setup, DVE_SET + ACT_SET)

            def stats(b, s, x, done):
                for t in range(CT):
                    for k in range(2):
                        ins = nc.vector.bn_stats(s[:, 12 * t + 6 * k:12 * t + 6 * k + 6], bank(x[:, t, :], k))
                ins.then_inc(done.sem, 1)

            def a_s0(m):
                ea_a.start(dve, m)
                dve.wait_ge(x_in.sem, x_in.at(m + 1, 0))
                stats(m, sa, xr, a_stats)

            def gn_spread(ch, b, s, pp, sums, spread):
                st = s[:, 0:24].rearrange("p (t k c) -> p t k c", t=CT, c=3)
                gm = pp[:, 0:24].rearrange("p (t k c) -> p t k c", t=CT, c=3)
                d = s[:, 32:40].rearrange("p (t k) -> p t k", t=CT)
                w = s[:, 40:48].rearrange("p (t k) -> p t k", t=CT)
                dve.wait_ge(sums.sem, sums.at(b, 1))
                ch(nc.vector.tensor_reduce(s[:, 24:26], gm[:, :, :, 1], AX.X, ALU.add))
                ch(nc.vector.tensor_tensor(d, st[:, :, :, 1], s[:, 24:26, None].to_broadcast([P, CT, 4]), ALU.subtract))
                ch(nc.vector.tensor_tensor(w, d, d, ALU.mult))
                nc.vector.scalar_tensor_tensor(w, st[:, :, :, 2], 1.0 / 256, w, ALU.mult, ALU.add).then_inc(spread.sem, 1)

            def gn_var(b, s, pp, sums, var):
                dve.wait_ge(sums.sem, sums.at(b, 2))
                nc.vector.tensor_reduce(s[:, 50:52], pp[:, 32:40].rearrange("p (t k) -> p t k", t=CT), AX.X,
                                        ALU.add).then_inc(var.sem, 1)

            def gn_shift(b, s, rstd, shift):
                dve.wait_ge(rstd.sem, rstd.at(b, 1))
                nc.vector.scalar_tensor_tensor(s[:, 56:58], s[:, 24:26], -1.0, s[:, 54:56], ALU.mult, ALU.mult).then_inc(shift.sem, 1)

            def take_weights(j):
                dve.wait_ge(a_w16.sem, a_w16.at(j, 1))
                nc.vector.tensor_copy(chi[:, :, :], whi[:, :, :])
                nc.vector.tensor_copy(clo[:, :, :], wlo[:, :, :])
                nc.vector.tensor_copy(csc[:, :], wsc[:, :]).then_inc(c_w.sem, 1)

            def low_half(j):
                for t in range(CT):
                    dve.wait_ge(a_hi.sem, a_hi.at(j, t + 1))
                    inner = pad[:, t, :, 3:3 + H, 3:3 + W]
                    nc.vector.tensor_tensor(inner[:, 1], img(xh[:, t, :], W), inner[:, 0], ALU.subtract).then_inc(a_pad.sem, 1)

            def a_max_(j):
                dve.wait_ge(a_keyb.sem, a_keyb.at(j, 1))
                nc.vector.tensor_reduce(sk[:, 0:1], ex[:, :], AX.X, ALU.max, negate=True).then_inc(a_max.sem, 1)

            def a_dg_(j):
                ch = ea_a
                dve.wait_ge(a_exp.sem, a_exp.at(j, 1))
                ch(nc.vector.reciprocal(sk[:, 2:3], sk[:, 1:2]))
                nc.vector.tensor_scalar(dg49[:, :], ident[0:K2, 0:K2], sk[:, 2:3], None, ALU.mult).then_inc(a_dg.sem, 1)

            def a_ktc_(j):
                dve.wait_ge(a_kt.sem, a_kt.at(j, 1))
                nc.vector.tensor_copy(kt[:, :, :], pm[:, 0:8 * K2].rearrange("p (n k) -> p n k", n=8)).then_inc(a_ktc.sem, 1)

            def a_fic_(j):
                dve.wait_ge(a_fi.sem, a_fi.at(j, 1))
                nc.vector.tensor_copy(fi[:, :, :], pm[:, HALF:HALF + 2 * K2].rearrange("p (t k) -> p t k", t=CT)).then_inc(a_fic.sem, 1)

            def a_f2c_(j):
                ch = ea_a
                dve.wait_ge(a_f2.sem, a_f2.at(j, 1))
                for t in range(CT):
                    ins = nc.vector.tensor_scalar(f2[:, t, :], pm[:, t * 64:t * 64 + K2], v_b0[:, t:t + 1], None, ALU.add)
                ch(ins)
                s = sa
                nc.vector.bn_stats(s[:, 60:66], f2[:, :, :].rearrange("p t k -> p (t k)")).then_inc(a_f2c.sem, 1)

            def a_spread_(j):
                ch, s = ea_a, sa
                st = s[:, 60:66].rearrange("p (k c) -> p k c", c=3)
                dve.wait_ge(a_sums.sem, a_sums.at(j, 3))
                ch(nc.vector.tensor_reduce(s[:, 66:67], pm[:, 128:134].rearrange("p (k c) -> p k c", c=3)[:, :, 1], AX.X, ALU.add))
                ch(nc.vector.tensor_scalar(s[:, 67:68], s[:, 66:67], 0.5, None, ALU.mult))
                ch(nc.vector.tensor_tensor(s[:, 68:70], st[:, :, 1], s[:, 67:68].to_broadcast([P, 2]), ALU.subtract))
                ch(nc.vector.scalar_tensor_tensor(s[:, 70:72], s[:, 68:70], 0.5, s[:, 68:70], ALU.mult, ALU.mult))
                nc.vector.scalar_tensor_tensor(s[:, 72:74], st[:, :, 2], 0.5 / K2, s[:, 70:72], ALU.mult, ALU.add).then_inc(a_spread.sem, 1)

            def a_var_(j):
                s = sa
                dve.wait_ge(a_sums.sem, a_sums.at(j, 4))
                nc.vector.tensor_reduce(s[:, 74:75], pm[:, 136:138], AX.X, ALU.add).then_inc(a_var.sem, 1)

            def a_f3_(j):
                ch, s = ea_a, sa
                dve.wait_ge(a_rstd.sem, a_rstd.at(j, 2))
                ch(nc.vector.tensor_scalar(f2[:, :, :], f2[:, :, :], s[:, 67:68], s[:, 76:77], ALU.subtract, ALU.mult))
                ch(nc.vector.tensor_tensor(f2[:, :, :], f2[:, :, :], lnw[:, :, :], ALU.mult))
                ch(nc.vector.tensor_tensor(f2[:, :, :], f2[:, :, :], lnb[:, :, :], ALU.add))
                nc.vector.tensor_scalar(f2[:, :, :], f2[:, :, :], 0.0, None, ALU.max).then_inc(a_f3.sem, 1)

            def a_w_(j):
                ch, s = ea_a, sa
                dve.wait_ge(a_wg.sem, a_wg.at(j, 1))
                for t in range(CT):
                    ins = nc.vector.tensor_scalar(wg[:, t, :], pm[:, 256 + t * 64:256 + t * 64 + K2], v_b1[:, t:t + 1], None, ALU.add)
                ch(ins)
                ch(nc.vector.tensor_copy(wmid[:, :, :], wg[:, :, MIDDLE * KK:(MIDDLE + 1) * KK]))
                ch(nc.vector.tensor_reduce(s[:, 80:82], wg[:, :, :], AX.X, ALU.max, apply_absolute_value=True))
                ch(nc.vector.tensor_scalar(wsc[:, :], s[:, 80:82], 1e-30, None, ALU.max))
                ch(nc.vector.reciprocal(s[:, 82:84], wsc[:, :]))
                ch(nc.vector.tensor_tensor(wg[:, :, :], wg[:, :, :], s[:, 82:84, None].to_broadcast([P, CT, K2]), ALU.mult))
                ch(nc.vector.tensor_copy(whi[:, :, :], wg[:, :, :]))
                nc.vector.tensor_tensor(wlo[:, :, :], wg[:, :, :], whi[:, :, :], ALU.subtract).then_inc(a_w16.sem, 1)
                ch.end()

            def middle_taps(j, lo, hi):
                for n in range(lo, hi):
                    dx, t = MID_TAPS[n]
                    shift = dx - MIDDLE
                    w = wmid[:, t, dx:dx + 1]
                    if shift == 0:
                        ins = nc.vector.scalar_tensor_tensor(xm[:, t, :], xh[:, t, :], w, xr[:, t, :], ALU.mult, ALU.add)
                    else:
                        dve.wait_ge(mid_tap.sem, mid_tap.at(j, n - CT + 1))
                        o = img(xm[:, t, :], W)[:, :, max(0, -shift):W - max(0, shift)]
                        src = img(xh[:, t, :], W)[:, :, max(0, shift):W - max(0, -shift)]
                        ins = nc.vector.scalar_tensor_tensor(o, src, w, o, ALU.mult, ALU.add)
                    ins.then_inc(mid_tap.sem, 1)

            def conv_add(j, t):
                dve.wait_ge(row_done.sem, row_done.at(j, NR // CT * (t + 1)))
                if t == 0:
                    dve.wait_ge(a_copy.sem, a_copy.at(j, 1))
                nc.vector.scalar_tensor_tensor(xn[:, t, :], pconv[:, :], csc[:, t:t + 1], xn[:, t, :],
                                               ALU.mult, ALU.add).then_inc(conv_out.sem, 1)

            def b_s0(i):
                ea_b.start(dve, i)
                dve.wait_ge(conv_out.sem, conv_out.at(i, CT))
                stats(i, sg, xn, b_stats)

            def chunk_first(i, c):
                s, n, fc, st = CHUNKS[c]
                k = c % 2
                dve.wait_ge(ch_hi.sem, ch_hi.at(i, c + 1))
                if c >= 2:
                    dve.wait_ge(ch_lo.sem, ch_lo.at(i, c - 1))
                nc.vector.tensor_tensor(rest[:, k, 0:n], bank(pm, 0)[0:64, 0:n], bcs[0:64, s:s + n], ALU.subtract).then_inc(ch_rest.sem, 1)
                dve.wait_ge(ch_q.sem, ch_q.at(i, c + 1))
                if c >= 2:
                    dve.wait_ge(ch_delta.sem, ch_delta.at(i, c - 1))
                nc.vector.scalar_tensor_tensor(er[:, k, 0:n], qs[:, k, 0:n], 1.0, es[:, k, 0:n], ALU.subtract,
                                               ALU.subtract).then_inc(ch_err.sem, 1)

            def chunk_last(i, c):
                s, n, fc, st = CHUNKS[c]
                k = c % 2
                dve.wait_ge(ch_ln.sem, ch_ln.at(i, c + 1))
                nc.vector.tensor_tensor(er[:, k, 0:n], qs[:, k, 0:n], er[:, k, 0:n], ALU.subtract).then_inc(ch_sub.sem, 1)
                dve.wait_ge(ch_sub.sem, ch_sub.at(i, c + 1))
                nc.vector.tensor_tensor(er[:, k, 0:n], er[:, k, 0:n], es[:, k, 0:n], ALU.min).then_inc(ch_min.sem, 1)

            def silu_clip(i):
                dve.wait_ge(b_z.sem, b_z.at(i, 2))
                nc.vector.tensor_scalar(o1[:, :], o1[:, :], 1e18, None, ALU.min).then_inc(z_clip.sem, 1)

            def inputs(i, k):
                lv, st, dd, n0, m = UNITS[k]
                ln, fc, sc, _ = LEVEL[lv]
                so = SB if dd == 1 else sc
                dve.wait_ge(u_b.sem, u_b.at(i, k + 1))
                if k in CHUNKS_OF:
                    dve.wait_ge(ch_u.sem, ch_u.at(i, CHUNKS_OF[k]))
                us = u[:, so:so + ln]
                if lv == 1:
                    o, i0, i1 = bx[:, k % 2, 0:ln], slot_b[:, :], us
                else:
                    o = b3[:, :, 0:ln] if lv == 3 else b2[:, k % 2, :, 0:ln]
                    i0 = slot_b[:, :].rearrange("p (m l) -> p m l", m=m)
                    i1 = us[:, None, :].to_broadcast([P, m, ln])
                nc.vector.tensor_tensor(o, i0, i1, ALU.mult).then_inc(u_bx.sem, 1)

            def scan(i, q):
                k, d = PRODUCTS[q]
                lv, m = UNITS[k][0], UNITS[k][4]
                ln = LEVEL[lv][0]
                n = ln if lv == 1 else m * (ln + 1)
                if lv == 1:
                    av, bv = ea[:, k % 2, 0:n], bx[:, k % 2, 0:n]
                elif lv == 2:
                    av, bv = (v[:, k % 2].rearrange("p m l -> p (m l)") for v in (a2, b2))
                else:
                    av, bv = (v[:, :, :].rearrange("p m l -> p (m l)") for v in (a3, b3))
                hv = h[:, q % HR, 0:n]
                if d:
                    av, bv, hv = av[:, ::-1], bv[:, ::-1], hv[:, ::-1]
                dve.wait_ge(u_ea.sem, u_ea.at(i, k + 1))
                dve.wait_ge(u_bx.sem, u_bx.at(i, k + 1))
                if k == 1:
                    dve.wait_ge(u_zero.sem, u_zero.at(i, 2))
                if q >= HR:
                    dve.wait_ge(q_y.sem, q_y.at(i, q - HR + 1))
                nc.vector.tensor_tensor_scan(hv, av, bv, 0.0, ALU.mult, ALU.add).then_inc(q_h.sem, 1)

            def weigh(i, q):
                k, d = PRODUCTS[q]
                lv, m = UNITS[k][0], UNITS[k][4]
                ln = LEVEL[lv][0]
                dve.wait_ge(u_c.sem, u_c.at(i, k + 1))
                dve.wait_ge(q_h.sem, q_h.at(i, q + 1))
                if lv == 1:
                    hv = h[:, q % HR, 0:ln]
                    nc.vector.tensor_tensor(hv, slot_c[:, :], hv, ALU.mult).then_inc(q_pr.sem, 1)
                    return
                hv = h[:, q % HR, 0:m * (ln + 1)].rearrange("p (m l) -> p m l", m=m)[:, :, 0:ln]
                nc.vector.tensor_tensor(hv, slot_c[:, :].rearrange("p (m l) -> p m l", m=m), hv, ALU.mult).then_inc(q_pr.sem, 1)

            def up_add(dst, src, side):
                dv = dst.rearrange("p (r s c) -> p r s c", s=2, c=2 * side)
                sv = src.rearrange("p (r c) -> p r c", c=side)
                rows = dv.shape[1]
                for s in range(2):
                    d = dv[:, :, s, :].rearrange("p r (c e) -> p r c e", e=2)
                    ins = nc.vector.tensor_tensor(d, d, sv[:, :, :, None].to_broadcast([P, rows, side, 2]), ALU.add)
                return ins

            def norm(i, k):
                d, c0, n = NORMS[k]
                cols = 2 * n if d == 2 else n
                seq = n_o

                def step(ins):
                    step.n += 1
                    ins.then_inc(seq.sem, 1)
                    dve.wait_ge(seq.sem, seq.at(i, step.n))
                step.n = STEPS[k]
                t_ = norm_sbuf(k)[1][:, 0:cols]
                dve.wait_ge(n_rs.sem, n_rs.at(i, k + 1))
                ins = nc.vector.tensor_tensor(t_, norm_psum(k)[0][:, 0:cols], norm_sbuf(k)[2][:, 0:cols], ALU.mult)
                ins.then_inc(n_t.sem, 1)
                dve.wait_ge(n_t.sem, n_t.at(i, k + 1))
                if k < 2:
                    o = (o3, o2)[k]
                    step(nc.vector.tensor_tensor(o[:, :], t_[:, 0:n], t_[:, n:2 * n], ALU.add))
                    p = 2 - k
                    step(nc.vector.tensor_scalar(o[:, :], o[:, :], v_g[:, p:p + 1], bes[:, p:p + 1], ALU.mult, ALU.add))
                    if k == 1:
                        step(up_add(o2[:, :], o3[:, :], 8))
                elif d == 0:
                    o = o1[:, c0:c0 + n]
                    step(nc.vector.tensor_scalar(o, t_, v_g[:, 0:1], bes[:, 0:1], ALU.mult, ALU.add))
                    hh = c0 // HALF
                    step(up_add(o, o2[:, hh * 128:hh * 128 + 128], 16))
                else:
                    o = o1[:, c0:c0 + n]
                    step(nc.vector.scalar_tensor_tensor(o, t_, v_g[:, 1:2], o, ALU.mult, ALU.add))
                    nc.vector.tensor_tensor(o, o, sz[:, c0:c0 + n], ALU.mult).then_inc(b_g.sem, 1)
                assert step.n == STEPS[k + 1]

            def output(i, hh):
                if hh == 0:
                    dve.wait_ge(ob_free.sem, ob_free.at(i + 1, 0))
                for t in range(CT):
                    dve.wait_ge(b_out.sem, b_out.at(i, 2 * hh + t + 1))
                    src = bank((slot_c, slot_b)[hh], t)
                    ins = nc.vector.scalar_tensor_tensor(ob[:, t, hh * HALF:(hh + 1) * HALF], src, v_out[:, t:t + 1],
                                                         xc[:, t, hh * HALF:(hh + 1) * HALF], ALU.add, ALU.add)
                ins.then_inc((out_half, ob_ready)[hh].sem, 1)

            def bridge(i, j, m):
                def some(lo, hi):
                    if m is not None:
                        middle_taps(m, BRIDGE_MID[lo], BRIDGE_MID[hi])
                some(0, 1)
                if j is not None:
                    for v in (a2, b2):
                        nc.vector.memset(v[:, :, :, L2], 0.0).then_inc(u_zero.sem, 1)
                    chunk_first(j, 0)
                some(1, 2)
                if i is not None:
                    norm(i, 4)
                if j is not None:
                    chunk_first(j, 1)
                if i is not None:
                    norm(i, 5)
                if j is not None:
                    chunk_last(j, 0)
                    chunk_last(j, 1)
                some(2, 3)
                if i is not None:
                    output(i, 0)
                    some(3, 4)
                    output(i, 1)
                else:
                    some(3, 4)
                some(4, 5)
                if j is not None:
                    inputs(j, 0)

            pre = {3: a_s0, 6: lambda m: gn_spread(ea_a, m, sa, pm, a_sums, a_spread), 7: lambda m: gn_var(m, sa, pm, a_sums, a_var),
                   8: lambda m: gn_shift(m, sa, a_rstd, a_shift), 17: a_max_, 19: a_dg_, 20: a_ktc_, 21: a_fic_, 22: a_f2c_,
                   23: a_spread_, 24: a_var_, 25: a_f3_, 26: a_w_}

            def unit(i, j, m, k):
                if i is None and k == PREP + 2 and j is not None:
                    gn_shift(j, sg, b_rstd, b_shift)
                    ea_b.end()
                if i is not None:
                    for n, q in enumerate(products_of(k)):
                        scan(i, q)
                        if k == PREP + 2 and j is not None:
                            gn_shift(j, sg, b_rstd, b_shift)
                            ea_b.end()
                        if n == 0 and k + 1 < NU:
                            inputs(i, k + 1)
                        weigh(i, q)
                        if n == 0 and k in CHUNK_FIRST:
                            chunk_first(i, CHUNK_FIRST[k])
                    if k in CHUNK_LAST:
                        chunk_last(i, CHUNK_LAST[k])
                    if k == 6:
                        silu_clip(i)
                    if k in NORM_DVE:
                        norm(i, NORM_DVE[k])
                if m is not None and k in pre:
                    pre[k](m)
                if j is not None and k == HALF_AT:
                    conv_add(j, 0)
                if k == PREP:
                    if j is not None:
                        conv_add(j, 1)
                        b_s0(j)
                    if m is not None:
                        take_weights(m)
                if k == PREP + 1:
                    if j is not None:
                        gn_spread(ea_b, j, sg, pconv, b_sums, b_spread)
                    if m is not None:
                        low_half(m)
                    if j is not None:
                        gn_var(j, sg, pconv, b_sums, b_var)

            stages(unit, bridge, dve)

        @block.tensor
        def _(pe):
            pe.wait_ge(consts_in, LOADED)
            for t in range(CT):
                nc.tensor.matmul(pm[:, t * P:(t + 1) * P], win[:, t * P:(t + 1) * P], wc1[:, :], start=True, stop=True)
            nc.tensor.matmul(pm[:, HALF:HALF + 1], wc1[:, :], v_inx, start=True, stop=True).then_inc(setup_pe, 1)
            for p in range(3):
                ins = nc.tensor.matmul(pconv[:, p * P:(p + 1) * P], wx8[:, p, :], wdt[:, p, :], start=True, stop=True)
            ins.then_inc(setup_pe, 1)
            pe.wait_ge(setup, DVE_SET + ACT_SET)

            def sums1(b, s, pp, sums, stats):
                pe.wait_ge(stats.sem, stats.at(b, 1))
                nc.tensor.matmul(pp[:, 0:24], grp[:, :], s[:, 0:24], start=True, stop=True).then_inc(sums.sem, 1)

            def sums2(b, s, pp, sums, spread):
                pe.wait_ge(spread.sem, spread.at(b, 1))
                nc.tensor.matmul(pp[:, 32:40], grp[:, :], s[:, 40:48], start=True, stop=True).then_inc(sums.sem, 1)

            def a_key_(j):
                for t in range(CT):
                    pe.wait_ge(a_xh.sem, a_xh.at(j, t + 1))
                    for k in range(2):
                        ins = nc.tensor.matmul(bank(pm, k)[0:K2], wk[:, t, :], bank(xh[:, t, :], k),
                                               start=(t == 0), stop=(t == CT - 1))
                ins.then_inc(a_key.sem, 1)

            def a_turn(j, g):
                if g < 2:
                    pe.wait_ge(a_keyb.sem, a_keyb.at(j, 1))
                else:
                    pe.wait_ge(a_xtc.sem, a_xtc.at(j, g - 1))
                for b in range(2):
                    for t in range(CT):
                        n = 2 * g + b
                        ins = nc.tensor.transpose(bank(pm, g % 2)[:, (2 * b + t) * P:(2 * b + t + 1) * P],
                                                  xh[:, t, n * P:(n + 1) * P], ident[:, :])
                ins.then_inc(a_xt.sem, 1)

            def a_kt_(j):
                pe.wait_ge(a_dg.sem, a_dg.at(j, 1))
                for n in range(8):
                    ins = nc.tensor.matmul(pm[:, n * K2:(n + 1) * K2], ex[:, n * P:(n + 1) * P], dg49[:, :], start=True, stop=True)
                ins.then_inc(a_kt.sem, 1)

            def a_fi_(j):
                pe.wait_ge(a_ktc.sem, a_ktc.at(j, 1))
                pe.wait_ge(a_xtc.sem, a_xtc.at(j, 4))
                for t in range(CT):
                    for n in range(8):
                        ins = nc.tensor.matmul(pm[:, HALF + t * K2:HALF + (t + 1) * K2], xt[:, n, t * P:(t + 1) * P], kt[:, n, :],
                                               start=(n == 0), stop=(n == 7))
                ins.then_inc(a_fi.sem, 1)

            def mix(w, src, o):
                for t in range(CT):
                    for k in range(CT):
                        ins = nc.tensor.matmul(pm[:, o + t * 64:o + t * 64 + K2], w[:, k, t * P:(t + 1) * P], src[:, k, :],
                                               start=(k == 0), stop=(k == CT - 1))
                return ins

            def a_f2_(j):
                pe.wait_ge(a_fic.sem, a_fic.at(j, 1))
                mix(w0, fi, 0).then_inc(a_f2.sem, 1)

            def a_sum3(j):
                pe.wait_ge(a_f2c.sem, a_f2c.at(j, 1))
                nc.tensor.matmul(pm[:, 128:134], ones[:, :], sa[:, 60:66], start=True, stop=True).then_inc(a_sums.sem, 1)

            def a_sum4(j):
                pe.wait_ge(a_spread.sem, a_spread.at(j, 2))
                nc.tensor.matmul(pm[:, 136:138], ones[:, :], sa[:, 72:74], start=True, stop=True).then_inc(a_sums.sem, 1)

            def a_wg_(j):
                pe.wait_ge(a_f3.sem, a_f3.at(j, 1))
                mix(w1, f2, 256).then_inc(a_wg.sem, 1)

            def taps(j, lo, hi):
                for n in range(lo, hi):
                    r, dx = divmod(n, KK)
                    t, dy = ROWS[r]
                    if dx == 0:
                        pe.wait_ge(diag_made.sem, diag_made.at(j, r + 1))
                        if n == 0 and not (isinstance(j, int) and j == 0):
                            pe.wait_ge(b_var.sem, b_var.at(j, 0))
                        if dy == 0:
                            pe.wait_ge(a_pad.sem, a_pad.at(j, t + 1))
                        if dy == 0 and t > 0:
                            pe.wait_ge(conv_out.sem, conv_out.at(j, t))
                    first, last = dy == 0 and dx == 0, dy == KK - 1 and dx == KK - 1
                    dh, dl = diag[:, r % RING, 0, dx, :], diag[:, r % RING, 1, dx, :]
                    for m, (w, part) in enumerate(((dh, 0), (dh, 1), (dl, 0))):
                        for k in range(2):
                            rows = dy + 16 * k
                            ins = nc.tensor.matmul(bank(pconv, k), w, pad[:, t, part, rows:rows + 16, dx:dx + W],
                                                   start=first and m == 0, stop=last and m == 2)
                    if dx == KK - 1:
                        ins.then_inc(row_done.sem, 1)

            def project_f(i, t):
                pe.wait_ge(b_xg.sem, b_xg.at(i, t + 1))
                for k in range(2):
                    ins = nc.tensor.matmul(bank(slot_b, k), wf[:, t, :], bank(xg[:, t, :], k), start=(t == 0), stop=(t == CT - 1))
                if t == CT - 1:
                    ins.then_inc(b_proj.sem, 1)

            def project_z(i):
                pe.wait_ge(ch_pos.sem, ch_pos.at(i, 2))
                pe.wait_ge(ch_rest.sem, ch_rest.at(i, 2))
                for t in range(CT):
                    for k in range(2):
                        ins = nc.tensor.matmul(bank(pm, k), wz[:, t, :], bank(xg[:, t, :], k), start=(t == 0), stop=(t == CT - 1))
                ins.then_inc(b_proj.sem, 1)

            def lower(i, lv):
                w, o, n, side = ((wc2, 0, L2, 16), (wc3, HALF, L3, 8))[lv]
                src = f[:, (0, L1)[lv]:(0, L1)[lv] + 4 * n].rearrange("p (r s c e) -> p r s c e", s=2, e=2, c=side)
                pe.wait_ge(b_f.sem, b_f.at(i, lv + 1))
                for m in range(4):
                    ins = nc.tensor.matmul(slot_b[:, o:o + n], w[:, m, :], src[:, :, m // 2, :, m % 2], start=(m == 0), stop=(m == 3))
                ins.then_inc(b_proj.sem, 1)

            def chunk(i, c):
                s, n, fc, st = CHUNKS[c]
                if c == 2:
                    pe.wait_ge(b_z.sem, b_z.at(i, 1))
                if c == 4:
                    pe.wait_ge(n_t.sem, n_t.at(i, 2))
                if c == 0:
                    pe.wait_ge(b_f.sem, b_f.at(i, 3))
                else:
                    pe.wait_ge(ch_rest.sem, ch_rest.at(i, c))
                    pe.wait_ge(ch_pos.sem, ch_pos.at(i, c))
                nc.tensor.matmul(bank(pm, 0)[0:96, 0:n], wbc[:, st, :], f[:, fc:fc + n], start=True, stop=True).then_inc(ch_bc.sem, 1)
                nc.tensor.matmul(bank(pm, 1)[:, 0:n], wdelta[:, st, :], f[:, fc:fc + n], start=True, stop=True).then_inc(ch_dt.sem, 1)

            def spread(i, k, slot, row0, done):
                lv, st, dd, n0, m = UNITS[k]
                ln, fc, sc, _ = LEVEL[lv]
                so = SB if dd == 1 else sc
                per = min(ln, HALF)
                for n in range(m):
                    for c in range(0, ln, per):
                        o = n * ln + c
                        ins = nc.tensor.matmul(slot[:, o:o + per], sel[:, row0 + n0 + n:row0 + n0 + n + 1].to_broadcast([96, P]), bcs[:, so + c:so + c + per],
                                               start=True, stop=True)
                ins.then_inc(done.sem, 1)

            def put_b(i, k):
                if k in CHUNKS_OF:
                    pe.wait_ge(ch_lo.sem, ch_lo.at(i, CHUNKS_OF[k]))
                if k:
                    pe.wait_ge(u_bx.sem, u_bx.at(i, k))
                spread(i, k, slot_b, 0, u_b)

            def put_c(i, k):
                if k:
                    pe.wait_ge(q_pr.sem, q_pr.at(i, products_of(k - 1)[-1] + 1))
                spread(i, k, slot_c, NS, u_c)

            def norm_centre(i, k):
                d, c0, n = NORMS[k]
                src = y[:, :, c0:c0 + n] if d == 2 else y[:, d, c0:c0 + n]
                cols = 2 * n if d == 2 else n
                if k == 0:
                    pe.wait_ge(y_init.sem, y_init.at(i, 5))
                elif k < 4:
                    pe.wait_ge(n_t.sem, n_t.at(i, k))
                pe.wait_ge(q_y.sem, q_y.at(i, NORM_NEEDS[k]))
                o = norm_psum(k)[0][:, 0:cols]
                if d == 2:
                    o = o.rearrange("p (d n) -> p d n", d=2)
                nc.tensor.matmul(o, cen[:, :], src, start=True, stop=True).then_inc(n_yc.sem, 1)

            def norm_spread(i, k):
                d, c0, n = NORMS[k]
                cols = 2 * n if d == 2 else n
                pe.wait_ge(n_sq.sem, n_sq.at(i, k + 1))
                nc.tensor.matmul(norm_psum(k)[1][:, 0:cols], ones[:, :], norm_sbuf(k)[0][:, 0:cols], start=True, stop=True).then_inc(n_var.sem, 1)

            def output(i, hh):
                pe.wait_ge(b_g.sem, b_g.at(i, hh + 1))
                if hh == 0:
                    pe.wait_ge(n_t.sem, n_t.at(i, NN))
                for t in range(CT):
                    nc.tensor.matmul(bank((slot_c, slot_b)[hh], t), wo[:, t * P:(t + 1) * P], o1[:, hh * HALF:(hh + 1) * HALF],
                                     start=True, stop=True).then_inc(b_out.sem, 1)

            def bridge(i, j, m):
                def some(lo, hi):
                    if m is not None:
                        taps(m, BRIDGE_TAPS[lo], BRIDGE_TAPS[hi])
                some(2, 3)
                if j is not None:
                    lower(j, 0)
                some(3, 4)
                if j is not None:
                    lower(j, 1)
                some(4, 5)
                if j is not None:
                    chunk(j, 0)
                if i is not None:
                    if j is not None:
                        pe.wait_ge(b_f.sem, b_f.at(j, 3))
                    norm_centre(i, 4)
                    norm_centre(i, 5)
                if j is not None:
                    chunk(j, 1)
                if i is not None:
                    norm_spread(i, 4)
                    norm_spread(i, 5)
                some(5, 6)
                if j is not None:
                    project_z(j)
                if i is not None:
                    output(i, 0)
                    output(i, 1)
                some(6, 7)
                if j is not None:
                    if i is not None:
                        pe.wait_ge(ob_ready.sem, ob_ready.at(j, 0))
                    put_b(j, 0)
                    put_c(j, 0)

            pre = {5: lambda m: sums1(m, sa, pm, a_sums, a_stats), 6: lambda m: sums2(m, sa, pm, a_sums, a_spread),
                   15: a_key_, 16: lambda m: (a_turn(m, 0), a_turn(m, 1)), 17: lambda m: (a_turn(m, 2), a_turn(m, 3)),
                   19: a_kt_, 20: a_fi_, 21: a_f2_, 22: a_sum3, 23: a_sum4, 25: a_wg_}

            def unit(i, j, m, k):
                lo, hi = taps_at(k), taps_at(k + 1)
                if i is not None:
                    if k == 0:
                        put_b(i, 1)
                    if k + 2 < NU:
                        put_b(i, k + 2)
                mid = min(hi, lo + (FIRST_TAPS if 2 <= k < 5 else 1))
                if j is not None:
                    taps(j, lo, mid)
                if m is not None and k == PREP + 2:
                    taps(m, 0, BRIDGE_TAPS[1])
                if i is not None:
                    if k in CHUNK_PE:
                        chunk(i, CHUNK_PE[k])
                    if k + 1 < NU:
                        put_c(i, k + 1)
                if j is not None:
                    taps(j, mid, hi)
                    if k == PREP + 1:
                        sums1(j, sg, pconv, b_sums, b_stats)
                        sums2(j, sg, pconv, b_sums, b_spread)
                if k == PREP + 3:
                    if j is not None:
                        project_f(j, 0)
                        project_f(j, 1)
                    if m is not None:
                        taps(m, BRIDGE_TAPS[1], BRIDGE_TAPS[2])
                if m is not None and k in pre:
                    if i is not None and k in (5, 15):
                        pe.wait_ge(ch_pos.sem, ch_pos.at(i, {5: 4, 15: NCH}[k]))
                        pe.wait_ge(ch_rest.sem, ch_rest.at(i, {5: 4, 15: NCH}[k]))
                    pre[k](m)
                if i is not None and k in NORM_PE_YC:
                    n = NORM_PE_YC[k]
                    if n in (0, 2):
                        pe.wait_ge(ch_pos.sem, ch_pos.at(i, {0: 4, 2: NCH}[n]))
                        pe.wait_ge(ch_rest.sem, ch_rest.at(i, {0: 4, 2: NCH}[n]))
                        if m is not None:
                            pe.wait_ge(*((a_var.sem, a_var.at(m, 1)) if n == 0 else (a_w16.sem, a_w16.at(m, 1))))
                    norm_centre(i, NORM_PE_YC[k])
                if i is not None and k in NORM_PE_VAR:
                    norm_spread(i, NORM_PE_VAR[k])

            stages(unit, bridge, pe)

        @block.scalar
        def _(act):
            act.preload_act_table_set("natural_log_exp_and_others")
            act.wait_ge(consts_in, LOADED)
            nc.scalar.activation(nega[:, :, :], al[:, :, :], ACT.Exp).then_inc(setup, 1)
            act.wait_ge(setup_pe, 1)
            nc.scalar.activation(wf[:, :, :], pm[:, 0:C].rearrange("p (t m) -> p t m", t=CT), ACT.Copy).then_inc(setup, 1)
            nc.scalar.activation(bf1[:, :], pm[:, HALF:HALF + 1], ACT.Identity, bias=v_c1).then_inc(setup, 1)
            act.wait_ge(setup_pe, 2)
            nc.scalar.activation(wdelta[:, :, :], pconv[:, 0:3 * P].rearrange("p (t m) -> p t m", t=3), ACT.Copy).then_inc(setup, 1)
            act.wait_ge(setup, 5)
            act.wait_ge(setup, DVE_SET + 4)
            nc.scalar.mul(nega[:, :, :], nega[:, :, :], -1.0).then_inc(setup, 1)
            act.wait_ge(setup, DVE_SET + ACT_SET)

            def rsqrt(b, s, var, rstd, c, iv, io, n):
                act.wait_ge(var.sem, var.at(b, c))
                return (nc.scalar.activation(s[:, io - 2:io - 2 + n], s[:, iv:iv + n], ACT.Ln, bias=eps[:, 0:1]),
                        lambda: nc.scalar.activation(s[:, io:io + n], s[:, io - 2:io - 2 + n], ACT.Exp, scale=-0.5).then_inc(rstd.sem, 1))

            def a_rstd_(m):
                act_a.start(act, m)
                ins, fin = rsqrt(m, sa, a_var, a_rstd, 1, 50, 54, 2)
                act_a(ins)
                fin()

            def a_xh_(m):
                act.wait_ge(a_rstd.sem, a_rstd.at(m, 1))
                act.wait_ge(a_shift.sem, a_shift.at(m, 1))
                if not (isinstance(m, int) and m == 0):
                    act.wait_ge(a_pad.sem, a_pad.at(m, 0))
                for t in range(CT):
                    nc.scalar.activation(xh[:, t, :], xr[:, t, :], ACT.Identity, scale=sa[:, 54 + t:55 + t],
                                         bias=sa[:, 56 + t:57 + t]).then_inc(a_xh.sem, 1)

            def prep(j):
                if not (isinstance(j, int) and j == 0):
                    act.wait_ge(row_done.sem, row_done.at(j, 0))
                act.wait_ge(a_xh.sem, a_xh.at(j, CT))
                for t in range(CT):
                    nc.scalar.activation(pad[:, t, 0, 3:3 + H, 3:3 + W], img(xh[:, t, :], W), ACT.Copy).then_inc(a_hi.sem, 1)

            def keep_x(i):
                if not (isinstance(i, int) and i == 0):
                    act.wait_ge(ob_ready.sem, ob_ready.at(i, 0))
                nc.scalar.activation(xc[:, :, :], xn[:, :, :], ACT.Copy).then_inc(b_xc.sem, 1)

            def copy_x(j):
                if not (isinstance(j, int) and j == 0):
                    act.wait_ge(b_xc.sem, b_xc.at(j, 0))
                    act.wait_ge(b_xg.sem, b_xg.at(j, 0))
                act.wait_ge(mid_tap.sem, mid_tap.at(j + 1, 0))
                nc.scalar.activation(xn[:, :, :], xm[:, :, :], ACT.Copy).then_inc(a_copy.sem, 1)

            def a_keyb_(j):
                act.wait_ge(a_key.sem, a_key.at(j, 1))
                nc.scalar.activation(ex[:, :], pm[0:K2, :], ACT.Identity, bias=kb[:, 0:1]).then_inc(a_keyb.sem, 1)

            def a_xtc_(j, g):
                act.wait_ge(a_xt.sem, a_xt.at(j, g + 1))
                nc.scalar.activation(xt[:, 2 * g:2 * g + 2, :], bank(pm, g % 2).rearrange("p (n c) -> p n c", n=2),
                                     ACT.Copy).then_inc(a_xtc.sem, 1)

            def a_exp_(j):
                act.wait_ge(a_max.sem, a_max.at(j, 1))
                nc.scalar.activation(ex[:, :], ex[:, :], ACT.Exp, bias=sk[:, 0:1], accum_out=sk[:, 1:2]).then_inc(a_exp.sem, 1)

            def a_rstd2(j):
                ins, fin = rsqrt(j, sa, a_var, a_rstd, 2, 74, 78, 1)
                act_a(ins)
                nc.scalar.activation(sa[:, 76:77], sa[:, 76:77], ACT.Exp, scale=-0.5).then_inc(a_rstd.sem, 1)
                act_a.end()

            def b1(i):
                act_b.start(act, i)
                ins, fin = rsqrt(i, sg, b_var, b_rstd, 1, 50, 54, 2)
                act_b(ins)
                fin()
                act.wait_ge(b_rstd.sem, b_rstd.at(i, 1))
                act.wait_ge(b_shift.sem, b_shift.at(i, 1))
                for t in range(CT):
                    nc.scalar.activation(xg[:, t, :], xn[:, t, :], ACT.Identity, scale=sg[:, 54 + t:55 + t],
                                         bias=sg[:, 56 + t:57 + t]).then_inc(b_xg.sem, 1)
                act_b.end()

            def copy_f(i, lv):
                o, n, src, bias = ((0, L1, slot_b[:, :], bf1[:, 0:1]), (L1, L2, slot_b[:, 0:L2], v_c2),
                                   (L1 + L2, L3, slot_b[:, HALF:HALF + L3], v_c3))[lv]
                act.wait_ge(b_proj.sem, b_proj.at(i, lv + 1))
                nc.scalar.activation(f[:, o:o + n], src, ACT.Identity, bias=bias).then_inc(b_f.sem, 1)

            def copy_z(i):
                act.wait_ge(b_proj.sem, b_proj.at(i, 4))
                nc.scalar.activation(sz[:, :], pm[:, :], ACT.Identity, bias=v_inz).then_inc(b_z.sem, 1)

            def chunk_exp(i, c):
                s, n, fc, st = CHUNKS[c]
                k = c % 2
                act.wait_ge(ch_bc.sem, ch_bc.at(i, c + 1))
                nc.scalar.activation(bcs[:, s:s + n], bank(pm, 0)[0:96, 0:n], ACT.Copy).then_inc(ch_hi.sem, 1)
                act.wait_ge(ch_dt.sem, ch_dt.at(i, c + 1))
                if c >= 2:
                    act.wait_ge(ch_min.sem, ch_min.at(i, c - 1))
                nc.scalar.activation(es[:, k, 0:n], bank(pm, 1)[:, 0:n], ACT.Abs, bias=v_dtb[:, st:st + 1]).then_inc(ch_abs.sem, 1)
                nc.scalar.activation(delta[:, s:s + n], bank(pm, 1)[:, 0:n], ACT.Relu, bias=v_dtb[:, st:st + 1]).then_inc(ch_pos.sem, 1)
                act.wait_ge(ch_abs.sem, ch_abs.at(i, c + 1))
                nc.scalar.activation(es[:, k, 0:n], es[:, k, 0:n], ACT.Exp, scale=-1.0).then_inc(ch_exp.sem, 1)
                act.wait_ge(ch_exp.sem, ch_exp.at(i, c + 1))
                nc.scalar.activation(qs[:, k, 0:n], es[:, k, 0:n], ACT.Identity, bias=1.0).then_inc(ch_q.sem, 1)

            def chunk_log(i, c):
                s, n, _, _ = CHUNKS[c]
                k = c % 2
                act.wait_ge(ch_rest.sem, ch_rest.at(i, c + 1))
                nc.scalar.activation(bcs[0:64, s:s + n], rest[:, k, 0:n], ACT.Copy).then_inc(ch_mid.sem, 1)
                act.wait_ge(ch_err.sem, ch_err.at(i, c + 1))
                nc.scalar.activation(qs[:, k, 0:n], qs[:, k, 0:n], ACT.Ln).then_inc(ch_ln.sem, 1)

            def silu_exp(i):
                act.wait_ge(b_z.sem, b_z.at(i, 1))
                nc.scalar.activation(o1[:, :], sz[:, :], ACT.Exp, scale=-1.0).then_inc(b_z.sem, 1)

            def silu_end(i):
                act.wait_ge(z_clip.sem, z_clip.at(i, 1))
                nc.scalar.activation(o1[:, :], o1[:, :], ACT.Ln, bias=1.0).then_inc(z_ln.sem, 1)
                act.wait_ge(z_ln.sem, z_ln.at(i, 1))
                nc.scalar.activation(o1[:, :], o1[:, :], ACT.Exp, scale=-1.0).then_inc(z_sig.sem, 1)

            def y_start(i):
                for d, o, n, p in ((0, 0, L1, 0), (0, L1, L2, 1), (0, L1 + L2, L3, 2), (1, 0, L1 + L2, 1), (1, L1 + L2, L3, 2)):
                    nc.scalar.activation(y[:, d, o:o + n], f[:, o:o + n], ACT.Copy, scale=v_dv[:, p:p + 1]).then_inc(y_init.sem, 1)

            def decay(i, k):
                lv, st, dd, n0, m = UNITS[k]
                ln, fc, sc, _ = LEVEL[lv]
                so = SB if dd == 1 else sc
                if k in CHUNKS_OF:
                    act.wait_ge(ch_delta.sem, ch_delta.at(i, CHUNKS_OF[k]))
                if k >= 2:
                    act.wait_ge(q_h.sem, q_h.at(i, products_of(k - 2)[-1] + 1))
                for n in range(m):
                    o = ea[:, k % 2, 0:ln] if lv == 1 else a3[:, n, 0:ln] if lv == 3 else a2[:, k % 2, n, 0:ln]
                    ins = nc.scalar.activation(o, delta[:, so:so + ln], ACT.Exp, scale=nega[:, st, n0 + n:n0 + n + 1])
                ins.then_inc(u_ea.sem, 1)

            def norm_square(i, k):
                d, c0, n = NORMS[k]
                cols = 2 * n if d == 2 else n
                act.wait_ge(n_yc.sem, n_yc.at(i, k + 1))
                if k in (0, 2):
                    act.wait_ge(ch_min.sem, ch_min.at(i, {0: 4, 2: NCH}[k]))
                nc.scalar.activation(norm_sbuf(k)[0][:, 0:cols], norm_psum(k)[0][:, 0:cols], ACT.Square).then_inc(n_sq.sem, 1)

            def norm_root(i, k):
                d, c0, n = NORMS[k]
                cols = 2 * n if d == 2 else n
                _, ln_, rt = norm_sbuf(k)
                act.wait_ge(n_var.sem, n_var.at(i, k + 1))
                if k in (0, 2):
                    act.wait_ge(ch_delta.sem, ch_delta.at(i, {0: 4, 2: NCH}[k]))
                if 0 < k < 4:
                    act.wait_ge(n_o.sem, n_o.at(i, STEPS[k]))
                nc.scalar.activation(ln_[:, 0:cols], norm_psum(k)[1][:, 0:cols], ACT.Ln, bias=eps[:, 0:1]).then_inc(n_ln.sem, 1)
                act.wait_ge(n_ln.sem, n_ln.at(i, k + 1))
                nc.scalar.activation(rt[:, 0:cols], ln_[:, 0:cols], ACT.Exp, scale=-0.5).then_inc(n_rs.sem, 1)

            def bridge(i, j, m):
                if j is not None:
                    copy_f(j, 1)
                    copy_f(j, 2)
                    chunk_exp(j, 0)
                if i is not None:
                    norm_square(i, 4)
                    norm_square(i, 5)
                if j is not None:
                    chunk_exp(j, 1)
                if i is not None:
                    norm_root(i, 4)
                    norm_root(i, 5)
                if j is not None:
                    chunk_log(j, 0)
                    chunk_log(j, 1)
                    if i is not None:
                        act.wait_ge(b_g.sem, b_g.at(j, 0))
                    copy_z(j)
                    decay(j, 0)
                    decay(j, 1)
                    y_start(j)
                    keep_x(j)
                if m is not None:
                    copy_x(m)

            pre = {7: a_rstd_, 8: a_xh_, 16: a_keyb_, 17: lambda m: (a_xtc_(m, 0), a_xtc_(m, 1)),
                   18: lambda m: (a_xtc_(m, 2), a_xtc_(m, 3), a_exp_(m)), 24: a_rstd2}

            def unit(i, j, m, k):
                if j is not None and k == PREP + 2:
                    b1(j)
                if i is not None:
                    if k in CHUNK_LAST:
                        chunk_log(i, CHUNK_LAST[k])
                    if k + 2 < NU:
                        decay(i, k + 2)
                    if k in CHUNK_PE:
                        chunk_exp(i, CHUNK_PE[k])
                    if k == 5:
                        silu_exp(i)
                    if k == 6:
                        silu_end(i)
                    if k in NORM_ACT_SQ:
                        norm_square(i, NORM_ACT_SQ[k])
                    if k in NORM_ACT_RT:
                        norm_root(i, NORM_ACT_RT[k])
                if m is not None:
                    if k in pre:
                        pre[k](m)
                    if k == PREP:
                        prep(m)
                if j is not None and k == PREP + 3:
                    copy_f(j, 0)

            stages(unit, bridge, act)

        @block.gpsimd
        def _(pool):
            pool.wait_ge(setup, DVE_SET + ACT_SET)

            def chunk_low(i, j, c):
                s, n, fc, _ = CHUNKS[c]
                pool.wait_ge(ch_mid.sem, ch_mid.at(i, c + 1))
                pool.tensor_tensor(bcs[0:32, s:s + n], rest[0:32, c % 2, 0:n], bcs[0:32, s:s + n], ALU.subtract).then_inc(ch_lo.sem, 1)
                pool.wait_ge(ch_pos.sem, ch_pos.at(i, c + 1))
                pool.wait_ge(ch_min.sem, ch_min.at(i, c + 1))
                pool.tensor_tensor(delta[:, s:s + n], delta[:, s:s + n], er[:, c % 2, 0:n], ALU.add).then_inc(ch_delta.sem, 1)
                pool.wait_ge(ch_delta.sem, ch_delta.at(i, c + 1))
                if c == 2 and j is not None:
                    pool.wait_ge(a_copy.sem, a_copy.at(j, 1))
                pool.tensor_tensor(u[:, s:s + n], delta[:, s:s + n], f[:, fc:fc + n], ALU.mult).then_inc(ch_u.sem, 1)

            def silu_end(i):
                pool.wait_ge(z_sig.sem, z_sig.at(i, 1))
                pool.tensor_tensor(sz[:, :], sz[:, :], o1[:, :], ALU.mult).then_inc(b_sz.sem, 1)

            def make_row(j, r):
                t, dy = ROWS[r]
                if r >= RING:
                    pool.wait_ge(row_done.sem, row_done.at(j, r - RING + 1))
                elif not (isinstance(j, int) and j == 0):
                    pool.wait_ge(row_done.sem, row_done.at(j, 0))
                for m, w in enumerate((chi, clo)):
                    ins = pool.tensor_tensor(diag[:, r % RING, m, :, :], id16[:, None, :].to_broadcast([P, KK, P]),
                                             w[:, t, dy * KK:(dy + 1) * KK, None].to_broadcast([P, KK, P]), ALU.mult)
                ins.then_inc(diag_made.sem, 1)

            def gather(i, q):
                k, d = PRODUCTS[q]
                lv, m = UNITS[k][0], UNITS[k][4]
                ln, fc, _, _ = LEVEL[lv]
                yv = y[:, d, fc:fc + ln]
                if q == 0:
                    pool.wait_ge(y_init.sem, y_init.at(i, 5))
                pool.wait_ge(q_pr.sem, q_pr.at(i, q + 1))
                src = h[:, q % HR, 0:ln]
                if m > 1:
                    src = h[:, q % HR, 0:m * (ln + 1)].rearrange("p (m l) -> p m l", m=m)[:, :, 0:ln]
                while m > 1:
                    m //= 2
                    pool.tensor_tensor(src[:, 0:m], src[:, 0:m], src[:, m:2 * m], ALU.add).then_inc(n_y.sem, 1)
                    gather.n += 1
                    pool.wait_ge(n_y.sem, n_y.at(i, gather.n))
                if q:
                    pool.wait_ge(q_y.sem, q_y.at(i, q))
                pool.tensor_tensor(yv, yv, src[:, 0] if len(src.shape) == 3 else src, ALU.add).then_inc(q_y.sem, 1)

            def bridge(i, j, m):
                if j is not None:
                    chunk_low(j, m, 0)
                    chunk_low(j, m, 1)
                if m is not None:
                    for r in range(RING, NR):
                        if row_unit(r) == 0:
                            make_row(m, r)

            def unit(i, j, m, k):
                if k == 0:
                    gather.n = 0
                if i is not None:
                    for q in products_of(k):
                        gather(i, q)
                    if k in CHUNK_LAST:
                        chunk_low(i, j, CHUNK_LAST[k])
                    if k == 7:
                        silu_end(i)
                    if k == NU - 1:
                        assert gather.n == n_y.per
                if j is not None:
                    for r in range(RING, NR):
                        if row_unit(r) == k > 0:
                            make_row(j, r)
                if m is not None:
                    if k == PREP:
                        pool.wait_ge(c_w.sem, c_w.at(m, 1))
                    for r in FIRST_ROWS.get(k, ()):
                        make_row(m, r)

            stages(unit, bridge, pool)


TAPS = NR * KK
PREP = NU - 4
BRIDGE_TAPS = (0, 2, 3, 3, 3, 3, 6, 9)
BRIDGE_MID = (0, 7, 10, 11, 11, 14)
FIRST_TAPS = 2
FIRST_ROWS = {PREP: (0,), PREP + 1: (1, 2), PREP + 2: (3,)}


CHUNK_PE = {0: 2, 1: 3, 13: 4, 14: 5}
CHUNK_FIRST = {1: 2, 2: 3, 14: 4, 15: 5}
CHUNK_LAST = {1: 2, 2: 3, 15: 4, 16: 5}
ROOM = [49 if k < 5 else 27 for k in range(NU)]
for k, v in {0: -16, 1: 8, 2: 4, 3: 14, 4: 4, 6: 6, 10: 0, 11: -8, 13: -10, 14: -8, 15: -28, 16: -10, 17: -12, 19: -4, 20: -10, 22: 3, 23: 7,
             25: 8, 26: 10, 27: -8, 28: -8, 30: 8, 31: -8, 33: 16}.items():
    ROOM[k] += v


def taps_at(n):
    n = min(n, PREP)
    return BRIDGE_TAPS[-1] + -(-(TAPS - BRIDGE_TAPS[-1]) * sum(ROOM[:n]) // sum(ROOM[:PREP]))


HALF_AT = next(k for k in range(NU) if taps_at(k + 1) > TAPS // CT)


def row_unit(r):
    if r == RING:
        return next(k for k in range(NU) if taps_at(k) >= KK + 2)
    return next(k for k in range(r, NU) if taps_at(k) >= KK * (r - 2) + 2)


CHUNKS_OF = {0: 1, 1: 2, 5: 4, 21: 6}
NORM_PE_YC = {7: 0, 10: 1, 27: 2, 30: 3}
NORM_PE_VAR = {8: 0, 11: 1, 28: 2, 31: 3}
NORM_ACT_SQ = {8: 0, 11: 1, 28: 2, 31: 3}
NORM_ACT_RT = {9: 0, 12: 1, 29: 2, 32: 3}
NORM_DVE = {10: 0, 13: 1, 30: 2, 33: 3}
NORM_NEEDS = {0: 2, 1: 10, 2: 26, 3: 26, 4: 42, 5: 42}
STEPS = [0, 2, 5, 7, 9, 10, 11]


def stages(unit, bridge, eng):
    def body(i, j, m):
        for k in range(NU):
            unit(i, j, m, k)
        bridge(i, j, m)
    body(None, None, 0)
    body(None, 0, 1)
    with eng.Fori(0, B - 2) as i:
        body(i, i + 1, i + 2)
    body(B - 2, B - 1, None)
    body(B - 1, None, None)


def kernel(**inputs):
    import numpy as np
    import concourse.bacc as bacc
    from concourse.bass_utils import run_bass_kernel_spmd as run

    A = {n: np.asarray(v) for n, v in inputs.items()}
    g0 = lambda n: A["L0_conv_" + n]
    g1 = lambda n: A["L1_conv_" + n]

    def tiles(w):
        return w.reshape(CT, P, -1).transpose(1, 0, 2)

    eye = np.eye(P, dtype=np.float32)
    sel = np.concatenate([np.eye(32, dtype=np.float32)] * 3)
    arrays = {
        "x": A["x"],
        "c_ident": eye,
        "c_cen": eye - np.float32(1.0 / D),
        "c_ones": np.full((P, P), 1.0 / D, np.float32),
        "c_grp": np.kron(np.eye(P // GROUP), np.full((GROUP, GROUP), 1.0 / (4 * GROUP))).astype(np.float32),
        "c_sel": sel,
        "wk": tiles(g0("K_w").T),
        "w0": tiles(g0("conv0_w").T),
        "w1": tiles(g0("conv1_w").T),
        "win": g1("in_w")[:P],
        "wz": tiles(g1("in_w")[P:].T),
        "wc1": g1("c1_w").T,
        "wc2": g1("c2_w").reshape(P, P, 4).transpose(1, 2, 0),
        "wc3": g1("c3_w").reshape(P, P, 4).transpose(1, 2, 0),
        "wo": g1("out_w").T,
        "wx8": np.stack([g1(f"xw{s}")[:R_DT] for s in (1, 2, 3)], 1),
        "wdt": np.stack([g1(f"dtw{s}").T for s in (1, 2, 3)], 1),
        "wbc": np.stack([np.concatenate([g1(f"xw{s}")[R_DT:].T] * 3, 1) for s in (1, 2, 3)], 1),
        "vec": np.stack([g1("in_b")[:P], g1("in_b")[P:], g1("c1_b"), g1("c2_b"), g1("c3_b"),
                         *g1("out_b").reshape(CT, P), *g0("conv0_b").reshape(CT, P), *g0("conv1_b").reshape(CT, P),
                         *[g1(f"{n}{s}") for n in ("dtb", "Dv", "g", "be") for s in (1, 2, 3)]], 1),
        "kb": g0("K_b")[:, None],
        "lnw": tiles(g0("ln_w").reshape(C, K2)),
        "lnb": tiles(g0("ln_b").reshape(C, K2)),
        "al": np.stack([g1(f"Al{s}") for s in (1, 2, 3)], 1),
    }
    arrays = {n: np.ascontiguousarray(v) for n, v in arrays.items()}
    nc = bacc.Bacc("TRN2", target_bir_lowering=False, num_devices=1)
    aps = {n: nc.dram_tensor("in_" + n, v.shape, mybir.dt.from_np(v.dtype), kind="ExternalInput").ap() for n, v in arrays.items()}
    out = nc.dram_tensor("out_0", A["x"].shape, F32, kind="ExternalOutput").ap()
    build(nc, aps, out)
    r = run(nc, [{"in_" + n: v for n, v in arrays.items()}], core_ids=[0])
    return r.results[0]["out_0"]
```
